# Optimizing a Trainium2 kernel written in Bass

```python
import numpy as np
import jax
import jax.numpy as jnp

def _softmax(x, axis=-1):
    return jax.nn.softmax(x, axis=axis)

def _gelu(x):
    return jax.nn.gelu(x, approximate=True)

def _silu(x):
    return jax.nn.silu(x)

def _sigmoid(x):
    return jax.nn.sigmoid(x)

def _layernorm(x, axis=-1, eps=1e-05):
    m = jnp.mean(x, axis=axis, keepdims=True)
    v = jnp.var(x, axis=axis, keepdims=True)
    return (x - m) / jnp.sqrt(v + eps)

def _scatter_add(tgt, idx, src, axis=0):
    return tgt.at[idx].add(src)

def _segment_sum(src, seg, n):
    return jax.ops.segment_sum(src, seg, n)
kernel_name = 'mk_hybrid_d2_jaxref_r8_c28098'

def setup_inputs(seed: int=0):
    np.random.seed(seed)
    _w = jnp.asarray

    def _L0_attn_a_setup():
        import jax, jax.numpy as jnp
        import numpy as np
        HEAD_NUM = 16
        NEG_BIG = 1000000.0
        key = jax.random.key(seed)
        ks = jax.random.split(key, 5)
        E = 128
        B, S = (1, 512)
        x = jax.random.normal(ks[0], (B, S, E), dtype=jnp.float32)
        W1 = jax.random.normal(ks[1], (E, 3 * E), dtype=jnp.float32) * (1.0 / np.sqrt(E))
        b1 = jax.random.normal(ks[2], (3 * E,), dtype=jnp.float32) * 0.02
        Wp = jax.random.normal(ks[3], (E, E), dtype=jnp.float32) * (1.0 / np.sqrt(E))
        bp = jax.random.normal(ks[4], (E,), dtype=jnp.float32) * 0.02
        return {'x': x, 'W1': W1, 'b1': b1, 'Wp': Wp, 'bp': bp}
    _L0_attn_a_in = _L0_attn_a_setup()

    def _L0_attn_b_setup():
        import jax, jax.numpy as jnp
        import numpy as np
        D_MODEL, N_HEADS = (128, 16)
        D_H = D_MODEL // N_HEADS
        D_HR = D_H // 2
        D_LATENT = 32
        THETA = 10000.0

        def rope(x, theta=THETA):
            S, d = (x.shape[-2], x.shape[-1])
            inv = theta ** (-jnp.arange(0, d, 2, dtype=jnp.float32) / d)
            ang = jnp.arange(S, dtype=jnp.float32)[:, None] * inv
            cos, sin = (jnp.cos(ang), jnp.sin(ang))
            x1, x2 = (x[..., 0::2], x[..., 1::2])
            r1 = x1 * cos - x2 * sin
            r2 = x1 * sin + x2 * cos
            return jnp.stack([r1, r2], axis=-1).reshape(x.shape)
        key = jax.random.key(seed)
        ks = jax.random.split(key, 9)
        s = lambda fan_in: 1.0 / np.sqrt(fan_in)
        return {'x': jax.random.normal(ks[0], (4, 256, D_MODEL), jnp.float32), 'W_DQ': jax.random.normal(ks[1], (D_MODEL, D_LATENT), jnp.float32) * s(D_MODEL), 'W_UQ': jax.random.normal(ks[2], (D_LATENT, N_HEADS * D_H), jnp.float32) * s(D_LATENT), 'W_QR': jax.random.normal(ks[3], (D_LATENT, N_HEADS * D_HR), jnp.float32) * s(D_LATENT), 'W_DKV': jax.random.normal(ks[4], (D_MODEL, D_LATENT), jnp.float32) * s(D_MODEL), 'W_UK': jax.random.normal(ks[5], (D_LATENT, N_HEADS * D_H), jnp.float32) * s(D_LATENT), 'W_UV': jax.random.normal(ks[6], (D_LATENT, N_HEADS * D_H), jnp.float32) * s(D_LATENT), 'W_KR': jax.random.normal(ks[7], (D_MODEL, D_HR), jnp.float32) * s(D_MODEL), 'W_O': jax.random.normal(ks[8], (N_HEADS * D_H, D_MODEL), jnp.float32) * s(N_HEADS * D_H)}
    _L0_attn_b_in = _L0_attn_b_setup()

    def _L0_ffn_setup():
        import jax, jax.numpy as jnp
        import numpy as np
        B, L, D = (2, 256, 128)
        E = 15
        H = D * 1
        K = 3
        T = 1.0
        key = jax.random.key(seed)
        ks = jax.random.split(key, 12)
        s = 0.02
        return {'x': jax.random.normal(ks[0], (B, L, D), dtype=jnp.float32), 'router_W': jax.random.normal(ks[1], (D, E), dtype=jnp.float32) * s, 'router_b': jnp.zeros((E,), dtype=jnp.float32), 'sW1': jax.random.normal(ks[2], (D, H), dtype=jnp.float32) * s, 'sb1': jnp.zeros((H,), dtype=jnp.float32), 'sW2': jax.random.normal(ks[3], (H, D), dtype=jnp.float32) * s, 'sb2': jnp.zeros((D,), dtype=jnp.float32), 'eW1': jax.random.normal(ks[4], (E, D, H), dtype=jnp.float32) * s, 'eb1': jnp.zeros((E, H), dtype=jnp.float32), 'eW2': jax.random.normal(ks[5], (E, H, D), dtype=jnp.float32) * s, 'eb2': jnp.zeros((E, D), dtype=jnp.float32)}
    _L0_ffn_in = _L0_ffn_setup()

    def _L1_attn_a_setup():
        import jax, jax.numpy as jnp
        import numpy as np
        B, T, DIM, H = (2, 256, 128, 16)
        HD = DIM // H

        def _custom_softmax(a):
            a = jnp.clip(a, -100.0, 100.0)
            m = jnp.max(a, axis=-1, keepdims=True)
            e = jnp.exp(a - m)
            p = e / (jnp.sum(e, axis=-1, keepdims=True) + 1e-06)
            p = p + 1e-08
            return p / jnp.sum(p, axis=-1, keepdims=True)
        key = jax.random.key(seed)
        k1, k2, k3 = jax.random.split(key, 3)
        x = jax.random.normal(k1, (B, T, DIM), dtype=jnp.float32)
        w_qkv = jax.random.normal(k2, (3 * DIM, DIM), dtype=jnp.float32) / np.sqrt(DIM)
        w_proj = jax.random.normal(k3, (DIM, DIM), dtype=jnp.float32) / np.sqrt(DIM)
        return {'x': x, 'w_qkv': w_qkv, 'w_proj': w_proj}
    _L1_attn_a_in = _L1_attn_a_setup()

    def _L1_attn_b_setup():
        import jax, jax.numpy as jnp
        import numpy as np
        import math
        B, T, D = (2, 256, 128)
        N_HEADS = 16
        D_HEAD = D // N_HEADS

        def _rope_tables(t, d_head, dtype=jnp.float32):
            theta = 1.0 / 10000.0 ** (jnp.arange(0, d_head, 2, dtype=jnp.float32) / d_head)
            angles = jnp.outer(jnp.arange(t, dtype=jnp.float32), theta)
            angles = jnp.concatenate([angles, angles], axis=-1)
            return (jnp.cos(angles).astype(dtype), jnp.sin(angles).astype(dtype))

        def _rotate_half(x):
            half = x.shape[-1] // 2
            return jnp.concatenate([-x[..., half:], x[..., :half]], axis=-1)

        def _apply_rope(x, cos, sin):
            return x * cos[None, None] + _rotate_half(x) * sin[None, None]
        key = jax.random.key(seed)
        k1, k2, k3, k4 = jax.random.split(key, 4)
        s_in = 1.0 / math.sqrt(D)
        return {'x': jax.random.normal(k1, (B, T, D), dtype=jnp.float32), 'w_qkv': jax.random.normal(k2, (D, 3 * D), dtype=jnp.float32) * s_in, 'w_out': jax.random.normal(k3, (D, D), dtype=jnp.float32) * s_in, 'b_out': jax.random.normal(k4, (D,), dtype=jnp.float32) * 0.01}
    _L1_attn_b_in = _L1_attn_b_setup()

    def _L1_ffn_setup():
        import jax, jax.numpy as jnp
        import numpy as np
        B, SEQ, D, E, F = (4, 128, 128, 8, 512)
        CAPACITY = 2
        key = jax.random.key(seed)
        ks = jax.random.split(key, 8)
        x = jax.random.normal(ks[0], (B, SEQ, D), jnp.float32)
        gate_weight = jax.random.normal(ks[1], (E, D), jnp.float32) * 0.006
        W1 = jax.random.normal(ks[2], (E, D, F), jnp.float32) * (1.0 / np.sqrt(D))
        b1 = jnp.zeros((E, F), jnp.float32)
        W2 = jax.random.normal(ks[3], (E, F, D), jnp.float32) * (1.0 / np.sqrt(F))
        b2 = jnp.zeros((E, D), jnp.float32)
        Ws1 = jax.random.normal(ks[4], (D, F), jnp.float32) * (1.0 / np.sqrt(D))
        bs1 = jnp.zeros((F,), jnp.float32)
        Ws2 = jax.random.normal(ks[5], (F, D), jnp.float32) * (1.0 / np.sqrt(F))
        bs2 = jnp.zeros((D,), jnp.float32)
        return {'x': x, 'gate_weight': gate_weight, 'W1': W1, 'b1': b1, 'W2': W2, 'b2': b2, 'Ws1': Ws1, 'bs1': bs1, 'Ws2': Ws2, 'bs2': bs2}
    _L1_ffn_in = _L1_ffn_setup()
    _d = {'L0_attn_a_x': _L0_attn_a_in['x'], 'L0_attn_a_W1': _L0_attn_a_in['W1'], 'L0_attn_a_b1': _L0_attn_a_in['b1'], 'L0_attn_a_Wp': _L0_attn_a_in['Wp'], 'L0_attn_a_bp': _L0_attn_a_in['bp'], 'L0_attn_b_W_DQ': _L0_attn_b_in['W_DQ'], 'L0_attn_b_W_UQ': _L0_attn_b_in['W_UQ'], 'L0_attn_b_W_QR': _L0_attn_b_in['W_QR'], 'L0_attn_b_W_DKV': _L0_attn_b_in['W_DKV'], 'L0_attn_b_W_UK': _L0_attn_b_in['W_UK'], 'L0_attn_b_W_UV': _L0_attn_b_in['W_UV'], 'L0_attn_b_W_KR': _L0_attn_b_in['W_KR'], 'L0_attn_b_W_O': _L0_attn_b_in['W_O'], 'L0_ffn_router_W': _L0_ffn_in['router_W'], 'L0_ffn_router_b': _L0_ffn_in['router_b'], 'L0_ffn_sW1': _L0_ffn_in['sW1'], 'L0_ffn_sb1': _L0_ffn_in['sb1'], 'L0_ffn_sW2': _L0_ffn_in['sW2'], 'L0_ffn_sb2': _L0_ffn_in['sb2'], 'L0_ffn_eW1': _L0_ffn_in['eW1'], 'L0_ffn_eb1': _L0_ffn_in['eb1'], 'L0_ffn_eW2': _L0_ffn_in['eW2'], 'L0_ffn_eb2': _L0_ffn_in['eb2'], 'L1_attn_a_w_qkv': _L1_attn_a_in['w_qkv'], 'L1_attn_a_w_proj': _L1_attn_a_in['w_proj'], 'L1_attn_b_w_qkv': _L1_attn_b_in['w_qkv'], 'L1_attn_b_w_out': _L1_attn_b_in['w_out'], 'L1_attn_b_b_out': _L1_attn_b_in['b_out'], 'L1_ffn_gate_weight': _L1_ffn_in['gate_weight'], 'L1_ffn_W1': _L1_ffn_in['W1'], 'L1_ffn_b1': _L1_ffn_in['b1'], 'L1_ffn_W2': _L1_ffn_in['W2'], 'L1_ffn_b2': _L1_ffn_in['b2'], 'L1_ffn_Ws1': _L1_ffn_in['Ws1'], 'L1_ffn_bs1': _L1_ffn_in['bs1'], 'L1_ffn_Ws2': _L1_ffn_in['Ws2'], 'L1_ffn_bs2': _L1_ffn_in['bs2']}
    _x0 = _d['L0_attn_a_x']
    _d['L0_attn_a_x'] = jax.random.normal(jax.random.fold_in(jax.random.key(seed), 1), (4, 1024, 128), dtype=_x0.dtype)
    del _x0
    return _d

def reference(L0_attn_a_x, L0_attn_a_W1, L0_attn_a_b1, L0_attn_a_Wp, L0_attn_a_bp, L0_attn_b_W_DQ, L0_attn_b_W_UQ, L0_attn_b_W_QR, L0_attn_b_W_DKV, L0_attn_b_W_UK, L0_attn_b_W_UV, L0_attn_b_W_KR, L0_attn_b_W_O, L0_ffn_router_W, L0_ffn_router_b, L0_ffn_sW1, L0_ffn_sb1, L0_ffn_sW2, L0_ffn_sb2, L0_ffn_eW1, L0_ffn_eb1, L0_ffn_eW2, L0_ffn_eb2, L1_attn_a_w_qkv, L1_attn_a_w_proj, L1_attn_b_w_qkv, L1_attn_b_w_out, L1_attn_b_b_out, L1_ffn_gate_weight, L1_ffn_W1, L1_ffn_b1, L1_ffn_W2, L1_ffn_b2, L1_ffn_Ws1, L1_ffn_bs1, L1_ffn_Ws2, L1_ffn_bs2):

    def _L0_attn_a_ref(x, W1, b1, Wp, bp):
        import jax, jax.numpy as jnp
        import numpy as np
        HEAD_NUM = 16
        NEG_BIG = 1000000.0
        B, S, E = x.shape
        H = HEAD_NUM
        d = E // H
        dk = jnp.asarray(d, x.dtype) ** 0.5
        h = x @ W1 + b1
        h = jnp.swapaxes(h.reshape(B, S, H, 3 * d), 1, 2)
        q, k, v = (h[..., :d], h[..., d:2 * d], h[..., 2 * d:])
        w = jnp.einsum('bhqd,bhkd->bhqk', q, k) / dk
        mask = jnp.tril(jnp.ones((S, S), dtype=x.dtype))
        w = jax.nn.softmax(w * mask - (1.0 - mask) * NEG_BIG, axis=-1)
        a = jnp.einsum('bhqk,bhkd->bhqd', w, v)
        a = jnp.swapaxes(a, 1, 2).reshape(B, S, E)
        return a @ Wp + bp

    def _L0_attn_b_ref(x, W_DQ, W_UQ, W_QR, W_DKV, W_UK, W_UV, W_KR, W_O):
        import jax, jax.numpy as jnp
        import numpy as np
        D_MODEL, N_HEADS = (128, 16)
        D_H = D_MODEL // N_HEADS
        D_HR = D_H // 2
        D_LATENT = 32
        THETA = 10000.0

        def rope(x, theta=THETA):
            S, d = (x.shape[-2], x.shape[-1])
            inv = theta ** (-jnp.arange(0, d, 2, dtype=jnp.float32) / d)
            ang = jnp.arange(S, dtype=jnp.float32)[:, None] * inv
            cos, sin = (jnp.cos(ang), jnp.sin(ang))
            x1, x2 = (x[..., 0::2], x[..., 1::2])
            r1 = x1 * cos - x2 * sin
            r2 = x1 * sin + x2 * cos
            return jnp.stack([r1, r2], axis=-1).reshape(x.shape)
        B, S, _ = x.shape
        d_qk = D_H + D_HR
        c_q = x @ W_DQ
        Qc = (c_q @ W_UQ).reshape(B, S, N_HEADS, D_H).transpose(0, 2, 1, 3)
        Qr = (c_q @ W_QR).reshape(B, S, N_HEADS, D_HR).transpose(0, 2, 1, 3)
        Qr = rope(Qr)
        c_kv = x @ W_DKV
        Kc = (c_kv @ W_UK).reshape(B, S, N_HEADS, D_H).transpose(0, 2, 1, 3)
        Kr = rope((x @ W_KR)[:, None, :, :])
        Kr = jnp.broadcast_to(Kr, (B, N_HEADS, S, D_HR))
        V = (c_kv @ W_UV).reshape(B, S, N_HEADS, D_H).transpose(0, 2, 1, 3)
        Q = jnp.concatenate([Qc, Qr], axis=-1)
        K = jnp.concatenate([Kc, Kr], axis=-1)
        scores = jnp.einsum('bhqd,bhkd->bhqk', Q, K)
        scores = jnp.clip(scores, -80.0, 80.0)
        causal = jnp.tril(jnp.ones((S, S), dtype=bool))
        scores = jnp.where(causal, scores, -jnp.inf)
        weights = jax.nn.softmax(scores / jnp.sqrt(jnp.float32(d_qk)), axis=-1)
        attn = jnp.einsum('bhqk,bhkd->bhqd', weights, V)
        attn = attn.transpose(0, 2, 1, 3).reshape(B, S, N_HEADS * D_H)
        return attn @ W_O

    def _L0_ffn_ref(x, router_W, router_b, sW1, sb1, sW2, sb2, eW1, eb1, eW2, eb2):
        import jax, jax.numpy as jnp
        import numpy as np
        B, L, D = (2, 256, 128)
        E = 15
        H = D * 1
        K = 3
        T = 1.0
        b, l, d = x.shape
        n = b * l
        xt = x.reshape(n, d)
        shared = jax.nn.relu(xt @ sW1 + sb1) @ sW2 + sb2
        logits = xt @ router_W + router_b
        probs = jax.nn.softmax(logits / T, axis=-1)
        top_p, top_i = jax.lax.top_k(probs, K)
        cw = jnp.zeros((n, E), dtype=probs.dtype)
        cw = cw.at[jnp.arange(n)[:, None], top_i].set(top_p)
        h = jax.nn.relu(jnp.einsum('nd,edh->neh', xt, eW1) + eb1)
        ye = jnp.einsum('neh,ehd->ned', h, eW2) + eb2
        routed = jnp.einsum('ned,ne->nd', ye, cw)
        return (shared + routed).reshape(b, l, d)

    def _L1_attn_a_ref(x, w_qkv, w_proj):
        import jax, jax.numpy as jnp
        import numpy as np
        B, T, DIM, H = (2, 256, 128, 16)
        HD = DIM // H

        def _custom_softmax(a):
            a = jnp.clip(a, -100.0, 100.0)
            m = jnp.max(a, axis=-1, keepdims=True)
            e = jnp.exp(a - m)
            p = e / (jnp.sum(e, axis=-1, keepdims=True) + 1e-06)
            p = p + 1e-08
            return p / jnp.sum(p, axis=-1, keepdims=True)
        b, t, c = x.shape
        scale = HD ** (-0.5)
        qkv = jnp.einsum('btc,oc->bto', x, w_qkv)
        qkv = qkv.reshape(b, t, 3, H, HD)
        q = jnp.transpose(qkv[:, :, 0], (0, 2, 1, 3))
        k = jnp.transpose(qkv[:, :, 1], (0, 2, 1, 3))
        v = jnp.transpose(qkv[:, :, 2], (0, 2, 1, 3))
        attn = jnp.einsum('bhqd,bhkd->bhqk', q, k) * scale
        causal = jnp.tril(jnp.ones((t, t), dtype=bool))
        attn = jnp.where(causal, attn, -jnp.inf)
        attn = _custom_softmax(attn)
        out = jnp.einsum('bhqk,bhkd->bhqd', attn, v)
        out = jnp.transpose(out, (0, 2, 1, 3)).reshape(b, t, c)
        return jnp.einsum('btc,oc->bto', out, w_proj)

    def _L1_attn_b_ref(x, w_qkv, w_out, b_out):
        import jax, jax.numpy as jnp
        import numpy as np
        import math
        B, T, D = (2, 256, 128)
        N_HEADS = 16
        D_HEAD = D // N_HEADS

        def _rope_tables(t, d_head, dtype=jnp.float32):
            theta = 1.0 / 10000.0 ** (jnp.arange(0, d_head, 2, dtype=jnp.float32) / d_head)
            angles = jnp.outer(jnp.arange(t, dtype=jnp.float32), theta)
            angles = jnp.concatenate([angles, angles], axis=-1)
            return (jnp.cos(angles).astype(dtype), jnp.sin(angles).astype(dtype))

        def _rotate_half(x):
            half = x.shape[-1] // 2
            return jnp.concatenate([-x[..., half:], x[..., :half]], axis=-1)

        def _apply_rope(x, cos, sin):
            return x * cos[None, None] + _rotate_half(x) * sin[None, None]
        b, t, d = x.shape
        qkv = x @ w_qkv
        qkv = qkv.reshape(b, t, 3, N_HEADS, D_HEAD)
        q = jnp.transpose(qkv[:, :, 0], (0, 2, 1, 3))
        k = jnp.transpose(qkv[:, :, 1], (0, 2, 1, 3))
        v = jnp.transpose(qkv[:, :, 2], (0, 2, 1, 3))
        cos, sin = _rope_tables(t, D_HEAD, x.dtype)
        q = _apply_rope(q, cos, sin)
        k = _apply_rope(k, cos, sin)
        scores = jnp.einsum('bhqd,bhkd->bhqk', q, k) / math.sqrt(D_HEAD)
        probs = jax.nn.softmax(scores, axis=-1)
        out = jnp.einsum('bhqk,bhkd->bhqd', probs, v)
        out = jnp.transpose(out, (0, 2, 1, 3)).reshape(b, t, d)
        return out @ w_out + b_out

    def _L1_ffn_ref(x, gate_weight, W1, b1, W2, b2, Ws1, bs1, Ws2, bs2):
        import jax, jax.numpy as jnp
        import numpy as np
        B, SEQ, D, E, F = (4, 128, 128, 8, 512)
        CAPACITY = 2
        Bb, s, Dd = x.shape
        Ee = gate_weight.shape[0]
        xf = x.reshape(-1, Dd)
        S = xf.shape[0]
        logits = xf @ gate_weight.T
        scores = jax.nn.softmax(logits, axis=-1).T
        k = S * CAPACITY
        vals, idx = jax.lax.top_k(scores.reshape(-1), k)
        eidx = idx // S
        tidx = idx % S
        gate = jnp.zeros((Ee, S), x.dtype).at[eidx, tidx].add(vals)
        h = jax.nn.gelu(jnp.einsum('sd,edf->esf', xf, W1) + b1[:, None, :], approximate=True)
        y = jnp.einsum('esf,efd->esd', h, W2) + b2[:, None, :]
        out = jnp.einsum('es,esd->sd', gate, y)
        shared = jax.nn.gelu(xf @ Ws1 + bs1, approximate=True) @ Ws2 + bs2
        out = out + shared
        return out.reshape(Bb, s, Dd)
    x = L0_attn_a_x
    x = x + _L0_attn_a_ref(_layernorm(x, axis=-1), L0_attn_a_W1, L0_attn_a_b1, L0_attn_a_Wp, L0_attn_a_bp)
    x = x + _L0_ffn_ref(_layernorm(x, axis=-1), L0_ffn_router_W, L0_ffn_router_b, L0_ffn_sW1, L0_ffn_sb1, L0_ffn_sW2, L0_ffn_sb2, L0_ffn_eW1, L0_ffn_eb1, L0_ffn_eW2, L0_ffn_eb2)
    x = x + _L0_attn_b_ref(_layernorm(x, axis=-1), L0_attn_b_W_DQ, L0_attn_b_W_UQ, L0_attn_b_W_QR, L0_attn_b_W_DKV, L0_attn_b_W_UK, L0_attn_b_W_UV, L0_attn_b_W_KR, L0_attn_b_W_O)
    x = x + _L0_ffn_ref(_layernorm(x, axis=-1), L0_ffn_router_W, L0_ffn_router_b, L0_ffn_sW1, L0_ffn_sb1, L0_ffn_sW2, L0_ffn_sb2, L0_ffn_eW1, L0_ffn_eb1, L0_ffn_eW2, L0_ffn_eb2)
    x = x + _L1_attn_a_ref(_layernorm(x, axis=-1), L1_attn_a_w_qkv, L1_attn_a_w_proj)
    x = x + _L1_ffn_ref(_layernorm(x, axis=-1), L1_ffn_gate_weight, L1_ffn_W1, L1_ffn_b1, L1_ffn_W2, L1_ffn_b2, L1_ffn_Ws1, L1_ffn_bs1, L1_ffn_Ws2, L1_ffn_bs2)
    x = x + _L1_attn_b_ref(_layernorm(x, axis=-1), L1_attn_b_w_qkv, L1_attn_b_w_out, L1_attn_b_b_out)
    x = x + _L1_ffn_ref(_layernorm(x, axis=-1), L1_ffn_gate_weight, L1_ffn_W1, L1_ffn_b1, L1_ffn_W2, L1_ffn_b2, L1_ffn_Ws1, L1_ffn_bs1, L1_ffn_Ws2, L1_ffn_bs2)
    return x

_drawn_inputs = setup_inputs


def setup_inputs(seed=0):
    import zlib

    import numpy as np

    out = dict(_drawn_inputs(seed))
    spreads = {'L0_ffn_router_b': (0.0, 0.365),
     'L0_ffn_sb1': (0.0, 0.1),
     'L0_ffn_sb2': (0.0, 0.1),
     'L0_ffn_eb1': (0.0, 0.8),
     'L0_ffn_eb2': (0.0, 0.1),
     'L1_ffn_b1': (0.0, 0.483),
     'L1_ffn_b2': (0.0, 0.349),
     'L1_ffn_bs1': (0.0, 0.1),
     'L1_ffn_bs2': (0.0, 0.1)}
    factors = {'L0_ffn_eW1': 4.622, 'L0_ffn_eW2': 3.723, 'L1_attn_b_b_out': 7.317}
    for name, (base, spread) in spreads.items():
        noise = np.random.default_rng([zlib.crc32(name.encode()), seed]).standard_normal(out[name].shape)
        drawn = base * np.exp(spread * noise) if base else spread * noise
        out[name] = jnp.asarray(drawn.astype(out[name].dtype))
    for name, factor in factors.items():
        out[name] = (out[name] * factor).astype(out[name].dtype)
    return out
```

```python
from contextlib import ExitStack

import numpy as np

import concourse.bass as bass
from concourse import mybir

F32 = mybir.dt.float32
BF16 = mybir.dt.bfloat16
I32 = mybir.dt.int32
ALU = mybir.AluOpType
ACT = mybir.ActivationFunctionType
AX_X = mybir.AxisListType.X
ds = bass.ds

P = 128
B, S, E = 4, 1024, 128
NT = B * S // P
NB = 8
TB = 4
BW = TB * P
H, D = 16, 8
G, HG = 4, 4
UNITS = B * G
KT = S // P
VW = 32
LN_EPS = 1e-5
NEG = -1e30

Q_TERMS = (0, 0, 0, 1, 1, 2)
K_TERMS = (0, 1, 2, 0, 1, 0)
NTERM = len(Q_TERMS)
R_ROW = 64
M_ROW = 96
RING_P = 4
RING_Q = 4


class Chain:

    def __init__(self, eng, sem, base=0):
        self.eng, self.sem, self.base, self.n = eng, sem, base, 0

    def step(self, ins):
        ins.then_inc(self.sem, 1)
        self.n += 1

    def wait(self):
        self.eng.wait_ge(self.sem, self.base + self.n)

    def link(self, ins):
        self.step(ins)
        self.wait()


def semaphores(nc, ctx, prefix):
    held = []

    def sem(name):
        held.append(nc.alloc_semaphore(prefix + name))
        return held[-1]

    def give_back():
        nc.clear_and_free_semaphores(held)
        nc.all_engine_barrier()
    ctx.callback(give_back)
    return sem


def steps_of(causal):
    out = []
    for qb in range(S // BW):
        for kt in range(TB * (qb + 1) if causal else KT):
            diagonal = causal and kt >= TB * qb
            out.append((qb, kt, P * (kt - TB * qb) if diagonal else 0, diagonal))
    return out


def row_blocks_of(causal):
    out = []
    for j in range(HG):
        for qt in range(KT):
            keys = P * (qt + 1) if causal else S
            for half in range((keys + BW - 1) // BW):
                width = min(BW, keys - BW * half)
                out.append((j, qt, half, width, causal and BW * half + width == keys))
    return out


def attention_prepare(nc, L, C, X, A, w, scratch):
    rope, has_bias, latent, suffix = L["rope"], L["bias"], L["latent"], L["suffix"]
    nm = L["name"]
    with ExitStack() as ctx:
        sb = lambda name, shape, dt=F32: ctx.enter_context(nc.sbuf_tensor(nm + name, shape, dt))
        sem = semaphores(nc, ctx, nm + "prepare_")
        psum = lambda name, dt=F32: ctx.enter_context(nc.psum_tensor(nm + name, [P, BW], dt))

        stats = sb("stats", [P, 2, TB, 6])
        mv = sb("mv", [P, 2, TB, 2])
        sd = sb("sd", [P, 2, TB])
        rstd = sb("rstd", [P, 2, TB])
        xn = sb("xn", [P, 2, TB, P])
        xnT = sb("xnT", [P, 2, BW])
        psT = [psum("psT0"), psum("psT1")]
        psV = psum("psV")
        parts = [("q", P), ("k", P)] + ([("qr", 64), ("kr", 4)] if latent else [])
        roped = {"q", "k"} if rope == "half" else {"qr", "kr"} if rope == "pairs" else set()
        ps = {}
        if latent:
            ps_c = psum("psC")
            banks = [psum(f"psP{i}") for i in range(4)]
            ps = {"q": banks[0], "k": banks[1], "qr": banks[2], "kr": banks[3],
                  "qr_rot": banks[0], "kr_rot": banks[1]}
            cT = sb("cT", [64, 2, BW])
        else:
            for name, _ in parts:
                ps[name] = psum("ps" + name)
                if name in roped:
                    ps[name + "_rot"] = psum("ps" + name + "r")
        full = {n: sb("full" + n, [r, BW]) for n, r in parts}
        rest = {n: sb("rest" + n, [r, BW]) for n, r in parts}
        turned = {n: sb("turned" + n, [r, BW]) for n, r in parts if n in roped}
        pieces = {n: sb("pieces" + n, [r, 2, 3, BW], BF16) for n, r in parts}
        if suffix:
            square = {n: sb("square" + n, [P, BW]) for n in "qk"}
            norms = {n: psum("norms" + n) for n in "qk"}
            squared, norms_full, norms_read = sem("squared"), sem("norms_full"), sem("norms_read")

        mv_ready, sd_ready, xn_ready = sem("mv_ready"), sem("sd_ready"), sem("xn_ready")
        xT_in_psum, xT_ready, c_in_psum, c_ready = sem("xT_in_psum"), sem("xT_ready"), sem("c_in_psum"), sem("c_ready")
        proj_ready = {n: sem("proj_" + n) for n, _ in parts}
        rot_ready = {n: sem("rot_" + n) for n in roped}
        v_in_psum, v_ready = sem("v_in_psum"), sem("v_ready")
        full_ready = {n: sem("full_" + n) for n, _ in parts}
        first_ready = {n: sem("first_" + n) for n, _ in parts}
        rest_ready = {n: sem("rest_" + n) for n, _ in parts}
        second_ready = {n: sem("second_" + n) for n, _ in parts}
        third_ready = {n: sem("third_" + n) for n, _ in parts}
        stored = [sem("stored0"), sem("stored1")]
        dve_chain, pads_ready = sem("dve_chain"), sem("pads_ready")
        turned_ready = {n: sem("turned_" + n) for n in roped}
        w_ready = sem("w_ready")
        stores = G * len(parts)
        store_done = 16 * stores

        block = ctx.enter_context(nc.Block())

        @block.sync
        def _(sp):
            for dst, src in w["loads"]:
                sp.dma_start(dst, src).then_inc(w_ready, 16)
            for p in range(2):
                sp.sem_inc(stored[p], store_done)
            with sp.Fori(0, NB // 2) as i:
                for p in range(2):
                    for name, rows in parts:
                        sp.wait_ge(third_ready[name], 2 * i + p + 1)
                        per = rows // G if name != "kr" else rows
                        for g in range(G):
                            first = per * g if name != "kr" else 0
                            sp.dma_start(
                                scratch[name][ds(i * G + g, 1), :, :, p * BW:(p + 1) * BW].rearrange("u r c n -> (u r) c n"),
                                pieces[name][first:first + per, p]).then_inc(stored[p], 16)
            for p in range(2):
                sp.wait_ge(stored[p], store_done * (NB // 2 + 1))

        @block.tensor
        def _(pe):
            pe.wait_ge(w_ready, 16 * len(w["loads"]))
            with pe.Fori(0, NB // 2) as i:
                for p in range(2):
                    n = 2 * i + p
                    pe.wait_ge(xn_ready, n + 1)
                    for t in range(TB):
                        mm = pe.transpose(psT[p][:, t * P:(t + 1) * P], xn[:, p, t, :], C["ident"][:, :])
                    mm.then_inc(xT_in_psum, 1)
                    pe.wait_ge(xT_ready, n + 1)
                    x_block = xnT[:, p, :]
                    if latent:
                        pe.wait_ge(c_ready, n + 1)
                        pe.matmul(ps_c[0:64, :], w["down"][:, :], x_block, start=True, stop=True).then_inc(c_in_psum, 1)
                        pe.wait_ge(full_ready["kr"], n + 1)
                        pe.matmul(ps["kr"][0:4, :], w["kr"][:, :], x_block, start=True, stop=True).then_inc(proj_ready["kr"], 1)
                        pe.wait_ge(c_ready, n + 2)
                        pe.wait_ge(full_ready["qr"], n + 1)
                        pe.matmul(ps["qr"][0:64, :], w["qr"][0:32, :], cT[0:32, p, :], start=True, stop=True).then_inc(proj_ready["qr"], 1)
                        pe.matmul(ps["q"][:, :], w["q"][0:32, :], cT[0:32, p, :], start=True, stop=True).then_inc(proj_ready["q"], 1)
                        pe.matmul(ps["k"][:, :], w["k"][32:64, :], cT[32:64, p, :], start=True, stop=True).then_inc(proj_ready["k"], 1)
                        pe.wait_ge(first_ready["q"], n + 1)
                        pe.wait_ge(full_ready["q"], n + 2)
                        pe.matmul(ps["qr_rot"][0:64, :], w["qr_rot"][0:32, :], cT[0:32, p, :], start=True, stop=True).then_inc(rot_ready["qr"], 1)
                        pe.wait_ge(first_ready["k"], n + 1)
                        pe.wait_ge(full_ready["k"], n + 2)
                        pe.matmul(ps["kr_rot"][0:4, :], w["kr_rot"][:, :], x_block, start=True, stop=True).then_inc(rot_ready["kr"], 1)
                    else:
                        for name, _ in parts:
                            pe.wait_ge(full_ready[name], n + 1)
                            if name not in roped:
                                pe.wait_ge(first_ready[name], n + 1)
                            pe.matmul(ps[name][:, :], w[name][:, :], x_block, start=True, stop=True).then_inc(proj_ready[name], 1)
                            if name in roped:
                                pe.matmul(ps[name + "_rot"][:, :], w[name + "_rot"][:, :], x_block,
                                          start=True, stop=True).then_inc(rot_ready[name], 1)
                    pe.wait_ge(v_ready, n + 1)
                    for t in range(TB):
                        if latent:
                            mm = pe.matmul(psV[:, t * P:(t + 1) * P], cT[32:64, p, t * P:(t + 1) * P], w["v"][32:64, :],
                                           start=True, stop=True)
                        else:
                            mm = pe.matmul(psV[:, t * P:(t + 1) * P], xnT[:, p, t * P:(t + 1) * P], w["v"][:, :],
                                           start=True, stop=True)
                    mm.then_inc(v_in_psum, 1)
                    if suffix:
                        for k, name in enumerate("qk"):
                            pe.wait_ge(squared, 2 * n + k + 3)
                            pe.wait_ge(norms_read, 2 * n + k + 1)
                            pe.matmul(norms[name][0:H, :], w["heads"][:, :], square[name][:, :], start=True, stop=True).then_inc(norms_full, 1)

        @block.scalar
        def _(act):
            act.wait_ge(w_ready, 16 * len(w["loads"]))
            if latent:
                act.sem_inc(c_ready, 1)
            for name, _ in parts:
                if name not in roped:
                    act.sem_inc(full_ready[name], 1)
                    if not latent:
                        act.sem_inc(first_ready[name], 1)
            if not has_bias:
                act.sem_inc(v_ready, 1)
            with act.Fori(0, NB // 2) as i:
                for p in range(2):
                    n = 2 * i + p
                    act.wait_ge(mv_ready, n + 1)
                    nc.scalar.activation(sd[:, p, :], mv[:, p, :, 1], ACT.Sqrt, bias=C["eps"][:, 0:1]).then_inc(sd_ready, 1)
                    act.wait_ge(xT_in_psum, n + 1)
                    nc.scalar.activation(xnT[:, p, :], psT[p][:, :], ACT.Copy).then_inc(xT_ready, 1)
                    if latent:
                        act.wait_ge(c_in_psum, n + 1)
                        nc.scalar.activation(cT[:, p, :], ps_c[0:64, :], ACT.Copy).then_inc(c_ready, 1)
                    order = [x[0] for x in parts if x[0] not in roped] + [x[0] for x in parts if x[0] in roped]
                    for name in order:
                        if name in roped:
                            act.wait_ge(full_ready[name], n + 2)
                            src = full[name][:, :]
                        else:
                            act.wait_ge(proj_ready[name], n + 1)
                            rows = dict(parts)[name]
                            src = ps[name][0:rows, :]
                            act.wait_ge(rest_ready[name], n + 1)
                            if suffix:
                                act.wait_ge(squared, 2 * n + 1 + (name == "k"))
                            if has_bias:
                                nc.scalar.activation(full[name][:, :], src, ACT.Identity, bias=w["b" + name][:, 0:1]).then_inc(full_ready[name], 1)
                            else:
                                nc.scalar.activation(full[name][:, :], src, ACT.Copy).then_inc(full_ready[name], 1)
                        if name == order[0]:
                            act.wait_ge(stored[p], store_done * (i + 1))
                        if has_bias:
                            nc.scalar.activation(pieces[name][:, p, 0, :], src, ACT.Identity, bias=w["b" + name][:, 0:1]).then_inc(first_ready[name], 1)
                        else:
                            nc.scalar.activation(pieces[name][:, p, 0, :], src, ACT.Copy).then_inc(first_ready[name], 1)
                    if not has_bias:
                        act.wait_ge(v_in_psum, n + 1)
                        nc.scalar.activation(A["VR"][:, ds(i * G, G), p * TB:(p + 1) * TB, :],
                                             psV[:, :].rearrange("p (t g r) -> p g t r", g=G, r=32), ACT.Copy).then_inc(v_ready, 1)
                    for name in order:
                        act.wait_ge(rest_ready[name], n + 2)
                        nc.scalar.activation(pieces[name][:, p, 1, :], rest[name][:, :], ACT.Copy).then_inc(second_ready[name], 1)

        @block.vector
        def _(dve):
            dve.wait_ge(w_ready, 16 * len(w["loads"]))
            for name in roped:
                dve.sem_inc(turned_ready[name], 1)
            for name, _ in parts:
                dve.sem_inc(rest_ready[name], 1)
            if has_bias:
                dve.sem_inc(v_ready, 1)
            if suffix:
                dve.sem_inc(norms_read, 2)
            per = TB + 1
            with dve.Fori(0, NB // 2) as i:
                for p in range(2):
                    n = 2 * i + p
                    chain = Chain(dve, dve_chain, per * n)
                    for t in range(TB):
                        chain.step(nc.vector.bn_stats(stats[:, p, t, :], X[:, ds(n * TB + t, 1), :].rearrange("p a e -> p (a e)")))
                    chain.wait()
                    dve.nop(nofuse=True)
                    for t in range(TB):
                        ins = nc.vector.bn_aggr(mv[:, p, t, :], stats[:, p, t, :])
                    ins.then_inc(mv_ready, 1)
                    dve.wait_ge(sd_ready, n + 1)
                    chain.link(nc.vector.reciprocal(rstd[:, p, :], sd[:, p, :]))
                    for t in range(TB):
                        ins = nc.vector.tensor_scalar(xn[:, p, t, :], X[:, ds(n * TB + t, 1), :].rearrange("p a e -> p (a e)"),
                                                      mv[:, p, t, 0:1], rstd[:, p, t:t + 1], ALU.subtract, ALU.mult)
                    ins.then_inc(xn_ready, 1)
                    for name, rows in parts:
                        if name in roped:
                            table = C[L["tables"]]
                            dve.wait_ge(proj_ready[name], n + 1)
                            dve.wait_ge(turned_ready[name], n + 1)
                            nc.vector.tensor_tensor(rest[name][:, :], ps[name][0:rows, :], table[0:rows, 0, p * BW:(p + 1) * BW], ALU.mult)
                            dve.wait_ge(rot_ready[name], n + 1)
                            nc.vector.tensor_tensor(turned[name][:, :], ps[name + "_rot"][0:rows, :],
                                                    table[0:rows, 1, p * BW:(p + 1) * BW], ALU.mult).then_inc(turned_ready[name], 1)
                    for name, _ in parts:
                        dve.wait_ge(first_ready[name], n + 1 + (0 if latent or name in roped else 1))
                        dve.wait_ge(full_ready[name], n + 2)
                        nc.vector.tensor_tensor(rest[name][:, :], full[name][:, :], pieces[name][:, p, 0, :], ALU.subtract).then_inc(rest_ready[name], 1)
                    for name, _ in parts:
                        dve.wait_ge(second_ready[name], n + 1)
                        nc.vector.tensor_tensor(pieces[name][:, p, 2, :], rest[name][:, :], pieces[name][:, p, 1, :], ALU.subtract).then_inc(third_ready[name], 1)
                    if suffix:
                        for k, name in enumerate("qk"):
                            dve.wait_ge(norms_full, 2 * n + k + 1)
                            nc.vector.tensor_reduce(A["peak"][:, k, ds(n, 1)], norms[name][0:H, :], AX_X, ALU.max).then_inc(norms_read, 1)
                    if has_bias:
                        dve.wait_ge(v_in_psum, n + 1)
                        for t in range(TB):
                            ins = nc.vector.tensor_tensor(
                                A["VR"][:, ds(i * G, G), p * TB + t, :],
                                psV[:, t * P:(t + 1) * P].rearrange("p (g r) -> p g r", r=32),
                                w["bv"][:, :].rearrange("p (g r) -> p g r", r=32), ALU.add)
                        ins.then_inc(v_ready, 1)

        @block.gpsimd
        def _(pool):
            for name in roped:
                pool.sem_inc(full_ready[name], 1)
            nc.gpsimd.memset(A["VR"][:, UNITS, :, :], 0.0)
            for b in range(RING_Q):
                nc.gpsimd.memset(A["Q"][b][:, :, :].bitcast(I32), 0)
                nc.gpsimd.memset(A["K"][b][:, :, :].bitcast(I32), 0)
            for b in range(2):
                last = nc.gpsimd.memset(A["V"][b][:, :, :, :], 0.0)
            last.then_inc(pads_ready, 1)
            pool.wait_ge(pads_ready, 1)
            for b in range(RING_Q):
                last = nc.gpsimd.memset(A["K"][b][M_ROW:M_ROW + 3, :, :], 1.0)
            last.then_inc(pads_ready, 1)
            pool.wait_ge(pads_ready, 2)
            for b in range(2):
                last = nc.gpsimd.memset(A["V"][b][:, :, :, D:D + 1], 1.0)
            last.then_inc(pads_ready, 1)
            pool.wait_ge(pads_ready, 3)
            if suffix:
                pool.sem_inc(squared, 2)
                with pool.Fori(0, NB) as n:
                    for k, name in enumerate("qk"):
                        pool.wait_ge(full_ready[name], n + 2)
                        pool.wait_ge(norms_read, 2 * n + k + 1)
                        nc.gpsimd.tensor_tensor(square[name][:, :], full[name][:, :], full[name][:, :], ALU.mult).then_inc(squared, 1)
            if roped:
                with pool.Fori(0, NB // 2) as i:
                    for p in range(2):
                        n = 2 * i + p
                        for name, _ in parts:
                            if name in roped:
                                pool.wait_ge(turned_ready[name], n + 2)
                                nc.gpsimd.tensor_tensor(full[name][:, :], rest[name][:, :], turned[name][:, :], ALU.add).then_inc(full_ready[name], 1)


def masked_sums(nc, L, C, A, d):
    nm = L["name"]
    with ExitStack() as ctx:
        sb = lambda name, shape, dt=F32: ctx.enter_context(nc.sbuf_tensor(nm + name, shape, dt))
        sem = semaphores(nc, ctx, nm + "sums_")
        bank = lambda name: ctx.enter_context(nc.psum_tensor(nm + name, [P, BW], F32))
        later, ones = sb("later", [P, P]), sb("onesq", [P, P])
        after = sb("after", [P, 2, UNITS, 32])
        peaks, bound, most = sb("peaks", [H, 2]), sb("bound", [H, 1]), sb("most", [1, 1])
        psS, psB = [bank("psF0"), bank("psF1")], bank("psB")
        ready, later_ready, added, done, copied, bounded, turned = [sem("ms_" + x) for x in ("ready", "later", "added", "done", "copied", "bounded", "turned")]
        chain_sem = sem("ms_chain")
        block = ctx.enter_context(nc.Block())
        V = A["VR"]

        @block.sync
        def _(sp):
            sp.dma_start(A["masked"][:, :], d["masked"]).then_inc(ready, 16)
            sp.wait_ge(ready, 16)

        @block.gpsimd
        def _(pool):
            nc.gpsimd.memset(A["SUF"][:, 0, :, :], 0.0)
            nc.gpsimd.memset(A["SUM"][:, 0, :], 0.0)
            nc.gpsimd.memset(after[:, (KT - 1) % 2], 0.0).then_inc(added, 1)
            for t in reversed(range(-1, KT - 1)):
                pool.wait_ge(added, KT - 1 - t)
                if t < KT - 2:
                    pool.wait_ge(done, KT - 2 - t)
                nc.gpsimd.tensor_tensor(after[:, t % 2], after[:, (t + 1) % 2], V[:, 0:UNITS, t + 1, :], ALU.add).then_inc(added, 1)

        @block.tensor
        def _(pe):
            pe.wait_ge(later_ready, 2)
            for n, t in enumerate(reversed(range(-1, KT))):
                pe.wait_ge(added, n + 1)
                if n >= 2:
                    pe.wait_ge(copied, n - 1)
                out = psS[n % 2][:, :].rearrange("p (u r) -> p u r", r=32)
                if t >= 0:
                    pe.matmul(out, later[:, :], V[:, 0:UNITS, t, :], start=True, stop=False)
                pe.matmul(out, ones[:, :], after[:, t % 2], start=t < 0, stop=True).then_inc(done, 1)
            pe.wait_ge(bounded, 1)
            pe.matmul(psB[0:1, 0:H], bound[:, :], C["ident"][0:H, 0:H], start=True, stop=True).then_inc(turned, 1)

        @block.scalar
        def _(act):
            for n, t in enumerate(reversed(range(-1, KT))):
                act.wait_ge(done, n + 1)
                src = psS[n % 2][:, :].rearrange("p (u r) -> p u r", r=32)
                dst = A["SUF"][:, 1:UNITS + 1, t, :] if t >= 0 else A["SUM"][:, 1:UNITS + 1, :]
                nc.scalar.activation(dst, src, ACT.Copy).then_inc(copied, 1)

        @block.vector
        def _(dve):
            chain = Chain(dve, chain_sem)
            nc.vector.memset(ones[:, :], 1.0).then_inc(later_ready, 1)
            nc.vector.memset(A["clip_bias"][:, :], -L["clip"])
            chain.link(nc.vector.tensor_scalar(later[:, :], C["mask"][:, :], -1.0, None, ALU.is_ge))
            nc.vector.tensor_tensor(later[:, :], later[:, :], C["ident"][:, :], ALU.subtract).then_inc(later_ready, 1)
            chain.link(nc.vector.tensor_reduce(peaks[:, :], A["peak"][:, :, :], AX_X, ALU.max))
            nc.vector.tensor_tensor(bound[:, :], peaks[:, 0:1], peaks[:, 1:2], ALU.mult).then_inc(bounded, 1)
            dve.wait_ge(turned, 1)
            chain.link(nc.vector.tensor_reduce(most[:, :], psB[0:1, 0:H], AX_X, ALU.max))
            chain.link(nc.vector.tensor_scalar(A["may_clip"][0:1, :], most[:, :], 0.99 * (L["clip"] / L["scale"]) ** 2, None, ALU.is_ge))


def attention_core(nc, L, C, A, scratch):
    nm = L["name"]
    causal, needs_max, scale, latent = L["causal"], L["max"], L["scale"], L["latent"]
    floor = L["floor"]
    steps = steps_of(causal)
    NS = len(steps)
    rows = row_blocks_of(causal) if needs_max else []
    NR = len(rows)
    LAG = 1
    first_half = max(s for s in range(NS) if steps[s][0] == 0)
    NDIAG = sum(s[3] for s in steps)

    beside = [[] for _ in range(NS)]
    if needs_max:
        span = NS - 2
        for s in range(span):
            beside[s] += [("rows", b) for b in rows[NR * s // span:NR * (s + 1) // span]]
        beside[NS - 1].append(("maxima", None))
    beside[1].append(("output", -1))
    beside[first_half + LAG + 2].append(("output", 0))
    before = [("rows", b) for b in rows] + [("maxima", None)] if needs_max else []
    PRO = len(before)
    USES = sum(len(x) for x in beside)

    with ExitStack() as ctx:
        sb = lambda name, shape, dt=F32: ctx.enter_context(nc.sbuf_tensor(nm + name, shape, dt))
        sem = semaphores(nc, ctx, nm + "core_")
        st = [ctx.enter_context(nc.psum_tensor(nm + f"st{i}", [P, 2, BW], F32)) for i in range(2)]
        row = [ctx.enter_context(nc.psum_tensor(nm + f"row{i}", [P, BW], F32)) for i in range(2)]
        acc = [ctx.enter_context(nc.psum_tensor(nm + f"acc{i}", [P, BW], F32)) for i in range(2)]
        prob = sb("prob", [P, RING_P, HG, BW])
        halfmax = sb("halfmax", [P, HG, KT, 2])
        rowmax = sb("rowmax", [P, 2, HG, KT])
        left = sb("left", [P, 2, HG, KT])
        mpieces = sb("mpieces", [P, 3, HG, KT], BF16)
        mT = sb("mT", [3 * HG * KT, 2, P], BF16)
        accS = sb("accS", [P, 2, BW])
        rsum = sb("rsum", [P, TB, HG])
        if floor:
            lowest = sb("lowest", [P, 2, HG, KT])
            num = sb("num", [P, TB, HG, D])
            tail = sb("tail", [P, TB, HG, D])
            mass = sb("mass", [P, TB, HG])
            share = sb("share", [P, TB, HG])
            whole = sb("whole", [P, TB, HG])
            floors = sb("floors", [P, HG, S])
            low_ready, low_stored, floors_loaded = sem("low_ready"), sem("low_stored"), sem("floors_loaded")

        loaded = [sem(f"loaded{b}") for b in range(RING_Q)]
        v_loaded = sem("v_loaded")
        m_loaded = [sem("m_loaded0"), sem("m_loaded1")]
        st_full, exp_done = sem("st_full"), sem("exp_done")
        tri_done, clip_done = sem("tri_done"), sem("clip_done")
        pv_done = sem("pv_done")
        row_full, row_read = sem("row_full"), sem("row_read")
        m_split = sem("m_split")
        acc_copied, acc_turned = sem("acc_copied"), sem("acc_turned")
        dve_chain = sem("dve_chain")
        stand_in = sem("stand_in")
        NLOAD = 2 * NTERM * (2 if latent else 1)

        def over_units(eng, body):
            def rounds(general):
                with eng.Fori(0, UNITS // RING_Q) as i:
                    for q in range(RING_Q):
                        body(RING_Q * i + q, q, i, general)

            if not floor:
                rounds(L["clip"] is not None)
                return
            may_clip = eng.value_load(A["may_clip"][0:1, 0:1], min_val=0, max_val=1)
            with eng.If(may_clip):
                rounds(True)
            with eng.Else():
                rounds(False)


        block = ctx.enter_context(nc.Block())

        @block.sync
        def _(sp):
            stands = ["q", "k"] + (["qr", "kr"] if latent else [])
            for name in stands:
                for e in range(2):
                    sp.dma_start(scratch[name][UNITS + e], scratch[name][0]).then_inc(stand_in, 16)
            for par in range(2):
                sp.sem_inc(m_loaded[par], 48)

            def load(u, q):
                at = ds(u, 1)
                for t in range(NTERM):
                    for name, dst, piece in (("q", A["Q"], Q_TERMS[t]), ("k", A["K"], K_TERMS[t])):
                        sp.dma_start(dst[q][D * t:D * (t + 1), :, :],
                                     scratch[name][at, :, piece, :].rearrange("u (j d) n -> (u d) j n", d=D)).then_inc(loaded[q], 16)
                    if latent:
                        r0 = R_ROW + 4 * t
                        sp.dma_start(A["Q"][q][r0:r0 + 4, :, :],
                                     scratch["qr"][at, :, Q_TERMS[t], :].rearrange("u (j d) n -> (u d) j n", d=4)).then_inc(loaded[q], 16)
                        one = scratch["kr"][at, :, K_TERMS[t], :].rearrange("u d n -> (u d) n")
                        sp.dma_start(A["K"][q][r0:r0 + 4, :, :], one.unsqueeze(1).broadcast_to([4, HG, S])).then_inc(loaded[q], 16)

            def move_maxima(q, index):
                sp.wait_ge(row_read, index + 3)
                for c in range(3):
                    sp.dma_start(A["Q"][q][M_ROW + c:M_ROW + c + 1, :, :],
                                 mT[HG * KT * c:HG * KT * (c + 1), q % 2, :]).then_inc(m_loaded[q % 2], 16)

            load(0, 0)
            load(1, 1)
            sp.wait_ge(stand_in, 32 * len(stands))
            if needs_max:
                move_maxima(0, PRO - 1)

            def body(u, q, i, general):
                if q == 0:
                    sp.wait_ge(pv_done, NS * u + 1)
                else:
                    sp.wait_ge(pv_done, RING_P + NS * (RING_Q * i + q - 1))
                load(u + 2, (q + 2) % RING_Q)
                if floor and general:
                    sp.wait_ge(low_ready, u + 2)
                    sp.dma_start(scratch["low"][q % 2].rearrange("j t p -> p j t"), lowest[:, q % 2],
                                 allow_slow_non_contiguous=True).then_inc(low_stored, 16)
                    sp.wait_ge(low_stored, 16 * u + 16)
                    sp.wait_ge(clip_done, NS * u + 1)
                    sp.dma_start(floors[:, :, :].rearrange("p j n -> p (j n)"),
                                 scratch["low"][q % 2].rearrange("j t p -> (j t p)").partition_broadcast(P)).then_inc(floors_loaded, 16)
                if needs_max:
                    move_maxima((q + 1) % RING_Q, PRO + USES * (u + 1) - 1)
            over_units(sp, body)
            for q in range(RING_Q):
                sp.wait_ge(loaded[q], 16 * NLOAD * (UNITS // RING_Q + (q < 2)))
            if needs_max:
                for par in range(2):
                    sp.wait_ge(m_loaded[par], 48 * (1 + UNITS // 2 + (par == 0)))

        @block.gpsimd
        def _(pool):
            def load_v(u, par):
                nc.gpsimd.tensor_copy(A["V"][par][:, :, :, 0:D],
                                      A["VR"][:, ds(u, 1), :, :].rearrange("p u t (j d) -> p (u t) j d", d=D)).then_inc(v_loaded, 1)

            def body(u, q, i, general):
                nd = 0
                for s, (qb, kt, q0, diagonal) in enumerate(steps):
                    if s == LAG + 1:
                        pool.wait_ge(pv_done, RING_P + NS * u + 1)
                        load_v(u + 1, (q + 1) % 2)
                    if diagonal:
                        if general:
                            pool.wait_ge(clip_done, NS * u + s + 2)
                        else:
                            pool.wait_ge(exp_done, 2 * (NS * u + s) + 4)
                        pool.nop(nofuse=True)
                        on = prob[:, s % RING_P, :, q0:q0 + P]
                        nc.gpsimd.affine_select(out=on, in_=on, compare_op=ALU.is_ge, fill=0.0, base=0,
                                                pattern=[[0, HG], [1, P]], channel_multiplier=-1).then_inc(tri_done, 1)
            load_v(0, 0)
            over_units(pool, body)

        @block.tensor
        def _(pe):
            pe.sem_inc(pv_done, RING_P)
            pe.sem_inc(acc_turned, 1)

            def rows_of(slot, ring, b):
                j, qt, half, width, diagonal = b
                mm = pe.matmul(slot[:, 0:width], A["Q"][ring][0:M_ROW, j, qt * P:(qt + 1) * P],
                               A["K"][ring][0:M_ROW, j, half * BW:half * BW + width], start=True, stop=not diagonal)
                if diagonal:
                    mm = pe.matmul(slot[:, width - P:width], C["ident16"][:, :], C["mask16"][:, :], start=False, stop=True)
                return mm

            def maxima_of(slot, v):
                pe.wait_ge(m_split, v + 1)
                return pe.transpose(slot[0:3 * HG * KT, 0:P // 2].bitcast(BF16),
                                    mpieces[:, :, :, :].rearrange("p c j t -> p (c j t)"), C["ident16"][:, :])

            def output_of(slot, u, qb):
                pe.wait_ge(acc_copied, 2 * u + qb + 3)
                for t in range(TB):
                    mm = pe.transpose(slot[:, t * P:(t + 1) * P], accS[:, qb % 2, t * P:(t + 1) * P], C["ident"][:, :])
                return mm

            def through_v(u, q, s, general):
                qb, kt, q0, diagonal = steps[s]
                if s == 0:
                    pe.wait_ge(v_loaded, u + 1)
                if kt == 0:
                    pe.wait_ge(acc_copied, 2 * u + qb + 1)
                if diagonal:
                    pe.wait_ge(tri_done, NDIAG * u + sum(x[3] for x in steps[:s]) + 1)
                elif general:
                    pe.wait_ge(clip_done, NS * u + s + 2)
                else:
                    pe.wait_ge(exp_done, 2 * (NS * u + s) + 4)
                last = s + 1 == NS or steps[s + 1][0] != qb
                for j in range(HG):
                    mm = pe.matmul(acc[qb][VW * j:VW * (j + 1), q0:BW], A["V"][q % 2][:, kt, j, :],
                                   prob[:, s % RING_P, j, q0:BW], start=kt == 0, stop=last)
                mm.then_inc(pv_done, 1)

            if needs_max:
                pe.wait_ge(loaded[0], 16 * NLOAD)
                for k, (kind, b) in enumerate(before):
                    pe.wait_ge(row_read, k + 1)
                    mm = rows_of(row[k % 2], 0, b) if kind == "rows" else maxima_of(row[k % 2], 0)
                    mm.then_inc(row_full, 1)

            def body(u, q, i, general):
                if needs_max:
                    pe.wait_ge(m_loaded[q % 2], 48 * (2 * i + q // 2 + 2))
                else:
                    pe.wait_ge(loaded[q], 16 * NLOAD * (i + 1))
                k = 0
                for s, (qb, kt, q0, diagonal) in enumerate(steps):
                    for pair in range(2):
                        pe.wait_ge(exp_done, 2 * (NS * u + s) + pair + 1)
                        for jj in range(2):
                            j = 2 * pair + jj
                            mm = pe.matmul(st[pair][:, jj, q0:BW], A["K"][q][:, j, kt * P:(kt + 1) * P],
                                           A["Q"][q][:, j, qb * BW + q0:(qb + 1) * BW], start=True, stop=True)
                        mm.then_inc(st_full, 1)
                    for kind, b in beside[s]:
                        if kind == "rows" and k == 0:
                            pe.wait_ge(loaded[(q + 1) % RING_Q], 16 * NLOAD * (i + 1 + (q + 1) // RING_Q))
                        pe.wait_ge(row_read, PRO + USES * u + k + 1)
                        slot = row[(PRO + USES * q + k) % 2]
                        if kind == "rows":
                            rows_of(slot, (q + 1) % RING_Q, b).then_inc(row_full, 1)
                        elif kind == "maxima":
                            maxima_of(slot, u + 1).then_inc(row_full, 1)
                        else:
                            output_of(slot, u, b).then_inc(row_full, 1)
                        k += 1
                    if s >= LAG:
                        through_v(u, q, s - LAG, general)
                for s in range(NS - LAG, NS):
                    through_v(u, q, s, general)

            over_units(pe, body)
            pe.wait_ge(row_read, PRO + USES * UNITS + 1)
            output_of(row[PRO % 2], UNITS, -1).then_inc(row_full, 1)

        @block.scalar
        def _(act):
            act.sem_inc(exp_done, 2)

            def body(u, q, i, general):
                if floor:
                    act.wait_ge(m_split, u + 1)
                    nc.scalar.activation(lowest[:, q % 2], rowmax[:, q % 2], ACT.Exp, bias=A["clip_bias"][:, 0:1], scale=-scale).then_inc(low_ready, 1)
                for s, (qb, kt, q0, diagonal) in enumerate(steps):
                    act.wait_ge(pv_done, NS * u + s + 1)
                    for pair in range(2):
                        act.wait_ge(st_full, 2 * (NS * u + s) + pair + 1)
                        nc.scalar.activation(prob[:, s % RING_P, 2 * pair:2 * pair + 2, q0:BW], st[pair][:, :, q0:BW],
                                             ACT.Exp, scale=scale).then_inc(exp_done, 1)
                    if s == first_half + LAG + 1 or s == NS - 1:
                        done = first_half if s != NS - 1 else NS - 1
                        block_done = steps[done][0]
                        act.wait_ge(pv_done, RING_P + NS * u + done + 1)
                        act.wait_ge(acc_turned, 2 * u + block_done + 1)
                        nc.scalar.activation(accS[:, block_done, :], acc[block_done][:, :], ACT.Copy).then_inc(acc_copied, 1)
            with act.Fori(0, UNITS // RING_Q) as i:
                for q in range(RING_Q):
                    body(RING_Q * i + q, q, i, False)

        @block.vector
        def _(dve):
            dve.sem_inc(row_read, 2)
            dve.sem_inc(clip_done, 1)
            if floor:
                nc.vector.memset(lowest[:, :, :, :], 0.0).then_inc(low_ready, 1)
            nc.vector.memset(accS[:, 1, :], 1.0).then_inc(acc_copied, 2)

            def read_rows(slot, b):
                j, qt, half, width, diagonal = b
                return nc.vector.tensor_reduce(halfmax[:, j, qt, half:half + 1], slot[:, 0:width], AX_X, ALU.max)

            def split_maxima(index, ring, chain):
                m = rowmax[:, ring % 2]
                dve.wait_ge(row_read, index + 2)
                if causal:
                    nc.vector.tensor_copy(m[:, :, 0:TB], halfmax[:, :, 0:TB, 0])
                    chain.link(nc.vector.tensor_tensor(m[:, :, TB:KT], halfmax[:, :, TB:KT, 0], halfmax[:, :, TB:KT, 1], ALU.max))
                else:
                    chain.link(nc.vector.tensor_tensor(m[:, :, :], halfmax[:, :, :, 0], halfmax[:, :, :, 1], ALU.max))
                if floor:
                    limit = L["clip"] / scale
                    chain.link(nc.vector.tensor_scalar(m[:, :, :], m[:, :, :], limit, -limit, ALU.min, ALU.max))
                chain.link(nc.vector.tensor_scalar(left[:, 0], m[:, :, :], -1.0, None, ALU.mult))
                chain.link(nc.vector.tensor_copy(mpieces[:, 0], left[:, 0]))
                chain.link(nc.vector.tensor_tensor(left[:, 1], left[:, 0], mpieces[:, 0], ALU.subtract))
                chain.link(nc.vector.tensor_copy(mpieces[:, 1], left[:, 1]))
                nc.vector.tensor_tensor(mpieces[:, 2], left[:, 1], mpieces[:, 1], ALU.subtract).then_inc(m_split, 1)

            def take_maxima(slot, ring, v):
                dve.wait_ge(m_loaded[ring % 2], v)
                return nc.vector.tensor_copy(mT[:, ring % 2, :], slot[0:3 * HG * KT, 0:P // 2].bitcast(BF16))

            def take_output(slot, u, q, qb, chain):
                view = slot[:, :].rearrange("p (t j r) -> p t j r", t=TB, r=VW)
                at = ds(u + 1 + (-1 if qb < 0 else 0), 1)
                tiles = slice((qb % 2) * TB, (qb % 2 + 1) * TB)
                out = A["AO"][:, at, tiles, :].rearrange("p u t (j d) -> p (u t) j d", d=D)
                if floor:
                    wide = lambda x: x.unsqueeze(3).broadcast_to([P, TB, HG, D])
                    dve.wait_ge(low_ready, u + (1 if qb < 0 else 2))
                    low = lowest[:, (q + (qb < 0)) % 2, :, tiles].rearrange("p j t -> p t j")
                    masked = A["masked"][:, tiles].unsqueeze(2).broadcast_to([P, TB, HG])
                    suffix = A["SUF"][:, at, tiles, :].rearrange("p u t (j d) -> p (u t) j d", d=D)
                    every = A["SUM"][:, at, :].rearrange("p u (j d) -> p u j d", d=D).broadcast_to([P, TB, HG, D])
                    chain.link(nc.vector.tensor_tensor(mass[:, :, :], low, masked, ALU.mult))
                    chain.link(nc.vector.tensor_tensor(mass[:, :, :], mass[:, :, :], view[:, :, :, D], ALU.add))
                    chain.link(nc.vector.tensor_scalar(share[:, :, :], mass[:, :, :], 1e-6, 1e-8, ALU.add, ALU.mult))
                    chain.link(nc.vector.scalar_tensor_tensor(whole[:, :, :], share[:, :, :], float(S), mass[:, :, :], ALU.mult, ALU.add))
                    chain.step(nc.vector.reciprocal(rsum[:, :, :], whole[:, :, :]))
                    chain.link(nc.vector.tensor_tensor(tail[:, :, :, :], wide(low), suffix, ALU.mult))
                    chain.link(nc.vector.tensor_tensor(num[:, :, :, :], tail[:, :, :, :], view[:, :, :, 0:D], ALU.add))
                    chain.link(nc.vector.tensor_tensor(tail[:, :, :, :], wide(share[:, :, :]), every, ALU.mult))
                    chain.link(nc.vector.tensor_tensor(num[:, :, :, :], num[:, :, :, :], tail[:, :, :, :], ALU.add))
                    return nc.vector.tensor_tensor(out, num[:, :, :, :], wide(rsum[:, :, :]), ALU.mult)
                chain.link(nc.vector.reciprocal(rsum[:, :, :], view[:, :, :, D]))
                return nc.vector.tensor_tensor(out, view[:, :, :, 0:D], rsum[:, :, :].unsqueeze(3).broadcast_to([P, TB, HG, D]), ALU.mult)

            pre = Chain(dve, dve_chain, 0)
            for k, (kind, b) in enumerate(before):
                if kind == "maxima":
                    split_maxima(k, 0, pre)
                dve.wait_ge(row_full, k + 1)
                ins = read_rows(row[k % 2], b) if kind == "rows" else take_maxima(row[k % 2], 0, 48)
                ins.then_inc(row_read, 1)
            LINKS = 2 * (9 if floor else 1) + ((6 if floor else 5) if needs_max else 0)

            def body(u, q, i, general):
                chain = Chain(dve, dve_chain, pre.n + LINKS * u)
                k = 0
                for s, (qb, kt, q0, diagonal) in enumerate(steps):
                    for kind, b in beside[s]:
                        slot = row[(PRO + USES * q + k) % 2]
                        index = PRO + USES * u + k
                        if kind == "maxima":
                            split_maxima(index, q + 1, chain)
                        dve.wait_ge(row_full, index + 1)
                        if kind == "rows":
                            read_rows(slot, b).then_inc(row_read, 1)
                        elif kind == "maxima":
                            take_maxima(slot, q + 1, 48 * (2 * i + (q + 1) // 2 + 1)).then_inc(row_read, 1)
                        else:
                            dve.sem_inc(acc_turned, 1)
                            take_output(slot, u, q, b, chain).then_inc(row_read, 1)
                        k += 1
                    if general:
                        dve.wait_ge(exp_done, 2 * (NS * u + s) + 4)
                        on = prob[:, s % RING_P, :, q0:BW]
                        if floor:
                            dve.wait_ge(floors_loaded, 16 * u + 16)
                            ins = nc.vector.scalar_tensor_tensor(on, on, 1.0, floors[:, :, qb * BW + q0:(qb + 1) * BW], ALU.min, ALU.max)
                        else:
                            ins = nc.vector.tensor_scalar(on, on, L["most"], L["least"], ALU.min, ALU.max)
                        ins.then_inc(clip_done, 1)
                assert chain.n == LINKS, (chain.n, LINKS)
            over_units(dve, body)
            dve.wait_ge(row_full, PRO + USES * UNITS + 1)
            take_output(row[PRO % 2], UNITS, 0, -1, Chain(dve, dve_chain, pre.n + LINKS * UNITS)).then_inc(row_read, 1)


def attention_finish(nc, L, C, X, A, w):
    nm = L["name"]
    with ExitStack() as ctx:
        sb = lambda name, shape, dt=F32: ctx.enter_context(nc.sbuf_tensor(nm + name, shape, dt))
        sem = semaphores(nc, ctx, nm + "finish_")
        psT = [ctx.enter_context(nc.psum_tensor(nm + f"psA{i}", [P, BW], F32)) for i in range(2)]
        psY = [ctx.enter_context(nc.psum_tensor(nm + f"psY{i}", [P, BW], F32)) for i in range(2)]
        ao = sb("ao", [P, 2, TB, P])
        aoT = sb("aoT", [P, 2, BW])
        y = sb("y", [P, 2, BW])
        gathered, turned, aoT_ready = sem("gathered"), sem("turned"), sem("aoT_ready")
        y_in_psum, y_read, y_biased = sem("y_in_psum"), sem("y_read"), sem("y_biased")
        block = ctx.enter_context(nc.Block())

        @block.gpsimd
        def _(pool):
            pool_first = 2
            with pool.Fori(0, NB // 2) as i:
                for p in range(2):
                    n = 2 * i + p
                    pool.wait_ge(turned, n + 1)
                    nc.gpsimd.tensor_copy(ao[:, p].rearrange("p t (g r) -> p g t r", r=32),
                                          A["AO"][:, ds(i * G + 1, G), p * TB:(p + 1) * TB, :]).then_inc(gathered, 1)

        @block.tensor
        def _(pe):
            pe.sem_inc(turned, 2)
            with pe.Fori(0, NB // 2) as i:
                for p in range(2):
                    n = 2 * i + p
                    pe.wait_ge(gathered, n + 1)
                    pe.wait_ge(aoT_ready, n + 1)
                    for t in range(TB):
                        mm = pe.transpose(psT[p][:, t * P:(t + 1) * P], ao[:, p, t, :], C["ident"][:, :])
                    mm.then_inc(turned, 1)
                    pe.wait_ge(aoT_ready, n + 3)
                    pe.wait_ge(y_read, n + 1)
                    for t in range(TB):
                        mm = pe.matmul(psY[p][:, t * P:(t + 1) * P], aoT[:, p, t * P:(t + 1) * P], w["o"][:, :], start=True, stop=True)
                    mm.then_inc(y_in_psum, 1)

        @block.scalar
        def _(act):
            act.sem_inc(aoT_ready, 2)
            with act.Fori(0, NB // 2) as i:
                for p in range(2):
                    n = 2 * i + p
                    act.wait_ge(turned, n + 3)
                    act.wait_ge(y_read, n + 1)
                    nc.scalar.activation(aoT[:, p, :], psT[p][:, :], ACT.Copy).then_inc(aoT_ready, 1)

        @block.vector
        def _(dve):
            dve.sem_inc(y_read, 2)
            with dve.Fori(0, NB // 2) as i:
                for p in range(2):
                    n = 2 * i + p
                    dve.wait_ge(y_in_psum, n + 1)
                    x = X[:, ds(n * TB, TB), :]
                    ps = psY[p][:, :].rearrange("p (t e) -> p t e", t=TB)
                    if w["bo"] is None:
                        nc.vector.tensor_tensor(x, ps, x, ALU.add).then_inc(y_read, 1)
                    else:
                        nc.vector.tensor_tensor(y[:, p].rearrange("p (t e) -> p t e", t=TB), ps,
                                                w["bo"][:, :].unsqueeze(1).broadcast_to([P, TB, P]), ALU.add).then_inc(y_read, 1)
                        dve.wait_ge(y_read, n + 3)
                        nc.vector.tensor_tensor(x, y[:, p].rearrange("p (t e) -> p t e", t=TB), x, ALU.add).then_inc(y_biased, 1)


def attention(nc, L, C, X, weights, scratch, d):
    nm = L["name"]
    with ExitStack() as ctx:
        sb = lambda name, shape, dt=F32: ctx.enter_context(nc.sbuf_tensor(nm + name, shape, dt))
        A = {
            "Q": [sb(f"Q{b}", [P, HG, S], BF16) for b in range(RING_Q)],
            "K": [sb(f"K{b}", [P, HG, S], BF16) for b in range(RING_Q)],
            "V": [sb(f"V{b}", [P, KT, HG, VW]) for b in range(2)],
            "VR": sb("VR", [P, UNITS + 1, KT, HG * D]),
            "AO": sb("AO", [P, UNITS + 1, KT, HG * D]),
        }
        w = {"loads": [], "bo": None}
        for name, (src, first, shape) in weights.items():
            t = sb("w" + name, [first + shape[0], shape[1]])
            w[name] = t
            w["loads"].append((t[first:first + shape[0], :], src))
        if L["tables"]:
            rows = d[L["tables"]].shape[0]
            C = dict(C)
            C[L["tables"]] = sb("table", [rows, 2, S])
            w["loads"].append((C[L["tables"]][:, :, :], d[L["tables"]]))
        if L["floor"]:
            A.update({"SUF": sb("SUF", [P, UNITS + 1, KT, 32]), "SUM": sb("SUM", [P, UNITS + 1, 32]), "masked": sb("masked", [P, KT]),
                      "peak": sb("peak", [H, 2, NB]), "clip_bias": sb("clip_bias", [P, 1]), "may_clip": sb("may_clip", [1, 1], I32)})
        attention_prepare(nc, L, C, X, A, w, scratch)
        if L["floor"]:
            masked_sums(nc, L, C, A, d)
        attention_core(nc, L, C, A, scratch)
        attention_finish(nc, L, C, X, A, w)



FFN = {
    "f0": dict(gated=15, experts=16, chunks=1, act=ACT.Relu, top=3),
    "f1": dict(gated=8, experts=9, chunks=4, act=ACT.Gelu_apprx_tanh, chosen=2 * B * S),
}
GW = 16


def layernorm_all(nc, X, C, dve, act_sem, sd_sem, chain, T):
    stats, mean, sd, rstd, t1, t2 = T
    for t in range(NT):
        ins = nc.vector.bn_stats(stats[:, t, :], X[:, t, :])
    chain.link(ins)
    chain.link(nc.vector.tensor_tensor(t1[:, :], stats[:, :, 1], stats[:, :, 4], ALU.add))
    chain.step(nc.vector.tensor_scalar(mean[:, :], t1[:, :], 0.5, None, ALU.mult))
    chain.link(nc.vector.tensor_tensor(t2[:, :], stats[:, :, 1], stats[:, :, 4], ALU.subtract))
    chain.link(nc.vector.tensor_tensor(t2[:, :], t2[:, :], t2[:, :], ALU.mult))
    chain.link(nc.vector.tensor_tensor(t1[:, :], stats[:, :, 2], stats[:, :, 5], ALU.add))
    chain.link(nc.vector.tensor_scalar(t1[:, :], t1[:, :], 1.0 / E, None, ALU.mult))
    nc.vector.scalar_tensor_tensor(t1[:, :], t2[:, :], 0.25, t1[:, :], ALU.mult, ALU.add).then_inc(act_sem, 1)
    dve.wait_ge(sd_sem, 1)
    chain.link(nc.vector.reciprocal(rstd[:, :], sd[:, :]))


def route(nc, nm, F, C, X, R, w):
    ne, top = F["gated"], F.get("top")
    LW = 24 if top else ne
    NCOL = ne * NT
    with ExitStack() as ctx:
        sb = lambda name, shape, dt=F32: ctx.enter_context(nc.sbuf_tensor(nm + name, shape, dt))
        sem = semaphores(nc, ctx, nm + "route_")
        bank = lambda name: ctx.enter_context(nc.psum_tensor(nm + name, [P, BW], F32))
        T = [sb("stats", [P, NT, 6])] + [sb(n, [P, NT]) for n in ("mean", "sd", "rstd", "t1", "t2")]
        stats, mean, sd, rstd, t1, t2 = T
        xn, xs = sb("xn", [P, 2, TB, P]), sb("xs", [P, 2, BW])
        logits, ex = sb("logits", [P, NT, LW]), sb("ex", [P, NT, ne])
        gate, pieces = sb("gate", [P, NT, GW]), sb("pieces", [P, NT, P], BF16)
        most, total, inv = sb("most", [P, NT]), sb("total", [P, NT]), sb("inv", [P, NT])
        if top:
            best, wanted, marked = sb("best", [P, NT, 8]), sb("wanted", [P, NT, 8]), sb("marked", [P, NT, LW])
        else:
            score = sb("score", [P, ne, NT])
            over, same, pick = sb("over", [P, NCOL]), sb("same", [P, NCOL]), sb("picked", [P, NCOL])
            run = [sb("run0", [P, NCOL]), sb("run1", [P, NCOL])]
            ones, above = sb("ones", [P, P]), sb("above", [P, P])
            limit, trial, grow, stepi = [sb(n, [P, 1], I32) for n in ("limit", "trial", "grow", "stepi")]
            stepf, count, room = [sb(n, [P, 1]) for n in ("stepf", "count", "room")]
        psT, psR, psG = [bank("psT0"), bank("psT1")], [bank("psR0"), bank("psR1")], [bank("psG0"), bank("psG1")]
        psN = bank("psN")
        rest = sb("rest", [P, 2, NT, GW])
        w_ready, var_ready, sd_ready = sem("w_ready"), sem("var_ready"), sem("sd_ready")
        xn_ready, xT_in_psum, xs_ready, XT_ready = sem("xn_ready"), sem("xT_in_psum"), sem("xs_ready"), sem("XT_ready")
        lg_in_psum, lg_ready = sem("lg_in_psum"), sem("lg_ready")
        b2_ready = sem("b2_ready")
        dif_ready, ex_ready, preset = sem("dif_ready"), sem("ex_ready"), sem("preset")
        counted, summed = sem("counted"), sem("summed")
        pieces_ready, gt_in_psum, gt_ready = sem("pieces_ready"), sem("gt_in_psum"), sem("gt_ready")
        same_ready, ranked = sem("same_ready"), sem("ranked")
        chain_sem, loop_sem = sem("chain"), sem("loop")
        BITS = 30
        block = ctx.enter_context(nc.Block())

        @block.sync
        def _(sp):
            for dst, src in w["loads"]:
                sp.dma_start(dst, src).then_inc(w_ready, 16)
            sp.wait_ge(w_ready, 16 * len(w["loads"]))

        @block.gpsimd
        def _(pool):
            nc.gpsimd.memset(pieces[:, :, :].bitcast(I32), 0)
            nc.gpsimd.memset(w["b2r"][:, :], 0.0)
            nc.gpsimd.memset(gate[:, :, :], 0.0).then_inc(preset, 1)
            pool.wait_ge(preset, 1)
            ins = nc.gpsimd.memset(gate[:, :, ne:ne + 1], 1.0)
            if top:
                for c in range(ne, LW):
                    nc.gpsimd.memset(logits[:, :, c:c + 1], NEG * c)
                for c in range(top, 8):
                    ins = nc.gpsimd.memset(wanted[:, :, c:c + 1], NEG * (ne + c - top))
            ins.then_inc(preset, 1)
            pool.wait_ge(preset, 2)
            for c in range(3):
                pool.dma_start(w["b2r"][GW * c:GW * c + F["experts"], :], w["b2"]).then_inc(b2_ready, 16)

        @block.tensor
        def _(pe):
            pe.wait_ge(w_ready, 16 * len(w["loads"]))
            with pe.Fori(0, NB // 2) as i:
                for p in range(2):
                    n = 2 * i + p
                    pe.wait_ge(xn_ready, n + 1)
                    pe.wait_ge(xs_ready, n + 1)
                    for t in range(TB):
                        mm = pe.transpose(psT[p][:, t * P:(t + 1) * P], xn[:, p, t, :], C["ident"][:, :])
                    mm.then_inc(xT_in_psum, 1)
                    pe.wait_ge(xs_ready, n + 3)
                    pe.wait_ge(lg_ready, n + 1)
                    for t in range(TB):
                        mm = pe.matmul(psR[p][:, t * GW:t * GW + ne], xs[:, p, t * P:(t + 1) * P], w["router"][:, :], start=True, stop=True)
                    mm.then_inc(lg_in_psum, 1)
            if not top:
                with pe.Fori(0, BITS) as i:
                    pe.wait_ge(counted, i + 1)
                    pe.matmul(psN[:, 0:1], ones[:, :], count[:, :], start=True, stop=True).then_inc(summed, 1)
                pe.wait_ge(counted, BITS + 1)
                pe.matmul(psN[:, 0:1], ones[:, :], count[:, :], start=True, stop=True).then_inc(summed, 1)
                pe.wait_ge(same_ready, 1)
                pe.matmul(psR[0][:, 0:NCOL], above[:, :], same[:, :], start=True, stop=True).then_inc(ranked, 1)
                pe.matmul(psR[1][:, 0:NCOL], ones[:, :], same[:, :], start=True, stop=True).then_inc(ranked, 1)
            pe.wait_ge(pieces_ready, 1)
            for n in range(NB):
                if n >= 2:
                    pe.wait_ge(gt_ready, n - 1)
                for t in range(TB):
                    mm = pe.transpose(psG[n % 2][:, t * P // 2:(t + 1) * P // 2].bitcast(BF16), pieces[:, n * TB + t, :], C["ident16"][:, :])
                mm.then_inc(gt_in_psum, 1)

        @block.scalar
        def _(act):
            act.sem_inc(XT_ready, 2)
            act.wait_ge(var_ready, 1)
            nc.scalar.activation(sd[:, :], t1[:, :], ACT.Sqrt, bias=C["eps"][:, 0:1]).then_inc(sd_ready, 1)
            with act.Fori(0, NB // 2) as i:
                for p in range(2):
                    n = 2 * i + p
                    act.wait_ge(xs_ready, n + 3)
                    nc.scalar.activation(R["XT"][:, ds(n * BW, BW)], xs[:, p, :], ACT.Copy).then_inc(XT_ready, 1)
            act.wait_ge(dif_ready, 1)
            nc.scalar.activation(ex[:, :, :], ex[:, :, :], ACT.Exp).then_inc(ex_ready, 1)
            for n in range(NB):
                act.wait_ge(gt_in_psum, n + 1)
                nc.scalar.activation(R["GT"][:, n * BW:(n + 1) * BW], psG[n % 2][:, 0:BW // 2].bitcast(BF16), ACT.Copy).then_inc(gt_ready, 1)

        @block.vector
        def _(dve):
            chain = Chain(dve, chain_sem)
            dve.sem_inc(xs_ready, 2)
            dve.sem_inc(lg_ready, 2)
            layernorm_all(nc, X, C, dve, var_ready, sd_ready, chain, T)
            dve.wait_ge(w_ready, 16 * len(w["loads"]))
            dve.wait_ge(preset, 2)
            dve.wait_ge(b2_ready, 48)
            with dve.Fori(0, NB // 2) as i:
                for p in range(2):
                    n = 2 * i + p
                    dve.wait_ge(xs_ready, n + 1)
                    for t in range(TB):
                        ins = nc.vector.tensor_scalar(xn[:, p, t, :], X[:, ds(n * TB + t, 1), :].rearrange("p a e -> p (a e)"),
                                                      mean[:, ds(n * TB + t, 1)], rstd[:, ds(n * TB + t, 1)], ALU.subtract, ALU.mult)
                    ins.then_inc(xn_ready, 1)
                    dve.wait_ge(xT_in_psum, n + 1)
                    dve.wait_ge(XT_ready, n + 1)
                    nc.vector.tensor_copy(xs[:, p, :], psT[p][:, :]).then_inc(xs_ready, 1)
                    dve.wait_ge(lg_in_psum, n + 1)
                    lg = psR[p][:, 0:TB * GW].rearrange("p (t e) -> p t e", t=TB)[:, :, 0:ne]
                    dst = logits[:, ds(n * TB, TB), 0:ne]
                    if top:
                        nc.vector.tensor_tensor(dst, lg, w["br"][:, :].unsqueeze(1).broadcast_to([P, TB, ne]), ALU.add).then_inc(lg_ready, 1)
                    else:
                        nc.vector.tensor_scalar(dst, lg, 1.0, None, ALU.mult).then_inc(lg_ready, 1)
            dve.wait_ge(lg_ready, NB + 2)
            wide = lambda x, k: x.unsqueeze(2).broadcast_to([P, NT, k])
            chain.link(nc.vector.tensor_reduce(most[:, :], logits[:, :, 0:ne], AX_X, ALU.max))
            nc.vector.tensor_tensor(ex[:, :, :], logits[:, :, 0:ne], wide(most[:, :], ne), ALU.subtract).then_inc(dif_ready, 1)
            if top:
                for t in range(NT):
                    ins = nc.vector.max(best[:, t, :], logits[:, t, :])
                chain.link(ins)
                chain.link(nc.vector.tensor_copy(wanted[:, :, 0:top], best[:, :, 0:top]))
                for t in range(NT):
                    ins = nc.vector.match_replace(marked[:, t, :], wanted[:, t, :], logits[:, t, :], -NEG)
                chain.link(ins)
            dve.wait_ge(ex_ready, 1)
            chain.link(nc.vector.tensor_reduce(total[:, :], ex[:, :, :], AX_X, ALU.add))
            chain.link(nc.vector.reciprocal(inv[:, :], total[:, :]))
            if top:
                chain.link(nc.vector.tensor_tensor(ex[:, :, :], ex[:, :, :], wide(inv[:, :], ne), ALU.mult))
                chain.link(nc.vector.scalar_tensor_tensor(gate[:, :, 0:ne], marked[:, :, 0:ne], -NEG, ex[:, :, :], ALU.is_ge, ALU.mult))
            else:
                chain.link(nc.vector.tensor_tensor(score[:, :, :].rearrange("p e t -> p t e"), ex[:, :, :], wide(inv[:, :], ne), ALU.mult))
                flat = score[:, :, :].rearrange("p e t -> p (e t)")
                chain.step(nc.vector.memset(ones[:, :], 1.0))
                chain.step(nc.vector.tensor_scalar(above[:, :], C["mask"][:, :], -1.0, None, ALU.is_lt))
                chain.step(nc.vector.memset(stepf[:, :], float(2 ** (BITS - 1))))
                chain.link(nc.vector.memset(limit[:, :], 0))
                LINKS = 5
                with dve.Fori(0, BITS) as i:
                    inner = Chain(dve, loop_sem, LINKS * i)
                    inner.link(nc.vector.tensor_copy(stepi[:, :], stepf[:, :]))
                    inner.link(nc.vector.tensor_tensor(trial[:, :], limit[:, :], stepi[:, :], ALU.bitwise_or))
                    nc.vector.tensor_scalar(over[:, :], flat, trial[:, :].bitcast(F32), 0.0, ALU.is_ge, ALU.add,
                                            accum_out=count[:, :]).then_inc(counted, 1)
                    dve.wait_ge(summed, i + 1)
                    inner.link(nc.vector.tensor_scalar(grow[:, :], psN[:, 0:1], float(F["chosen"]), stepf[:, :], ALU.is_ge, ALU.mult))
                    inner.link(nc.vector.tensor_tensor(limit[:, :], limit[:, :], grow[:, :], ALU.bitwise_or))
                    inner.link(nc.vector.tensor_scalar(stepf[:, :], stepf[:, :], 0.5, None, ALU.mult))
                    assert inner.n == LINKS
                at = limit[:, :].bitcast(F32)
                nc.vector.tensor_scalar(over[:, :], flat, at, 0.0, ALU.is_gt, ALU.add, accum_out=count[:, :]).then_inc(counted, 1)
                nc.vector.tensor_scalar(same[:, :], flat, at, None, ALU.is_equal).then_inc(same_ready, 1)
                dve.wait_ge(summed, BITS + 1)
                chain.link(nc.vector.tensor_scalar(room[:, :], psN[:, 0:1], -1.0, float(F["chosen"]), ALU.mult, ALU.add))
                dve.wait_ge(ranked, 2)
                chain.link(nc.vector.tensor_copy(run[0][:, :], psR[1][:, 0:NCOL]))
                width, a = 1, 0
                while width < NCOL:
                    chain.step(nc.vector.tensor_copy(run[1 - a][:, 0:width], run[a][:, 0:width]))
                    chain.link(nc.vector.tensor_tensor(run[1 - a][:, width:], run[a][:, width:], run[a][:, 0:NCOL - width], ALU.add))
                    width, a = 2 * width, 1 - a
                chain.link(nc.vector.tensor_tensor(pick[:, :], run[a][:, :], psR[1][:, 0:NCOL], ALU.subtract))
                chain.link(nc.vector.tensor_tensor(pick[:, :], pick[:, :], psR[0][:, 0:NCOL], ALU.add))
                chain.link(nc.vector.scalar_tensor_tensor(pick[:, :], pick[:, :], room[:, 0:1], same[:, :], ALU.is_lt, ALU.mult))
                chain.link(nc.vector.tensor_tensor(pick[:, :], pick[:, :], over[:, :], ALU.add))
                chain.link(nc.vector.tensor_tensor(gate[:, :, 0:ne], pick[:, :].rearrange("p (e t) -> p t e", e=ne),
                                                   score[:, :, :].rearrange("p e t -> p t e"), ALU.mult))
            cut = lambda c: pieces[:, :, GW * c:GW * (c + 1)]
            chain.link(nc.vector.tensor_copy(cut(0), gate[:, :, :]))
            chain.link(nc.vector.tensor_tensor(rest[:, 0], gate[:, :, :], cut(0), ALU.subtract))
            chain.link(nc.vector.tensor_copy(cut(1), rest[:, 0]))
            nc.vector.tensor_tensor(cut(2), rest[:, 0], cut(1), ALU.subtract).then_inc(pieces_ready, 1)
            b2p, b2f = R["b2p"], w["b2r"]
            chain.link(nc.vector.tensor_copy(b2p[:, 0, :], b2f[:, :]))
            chain.link(nc.vector.tensor_tensor(b2f[:, :], b2f[:, :], b2p[:, 0, :], ALU.subtract))
            chain.link(nc.vector.tensor_copy(b2p[:, 1, :], b2f[:, :]))
            chain.step(nc.vector.tensor_tensor(b2p[:, 2, :], b2f[:, :], b2p[:, 1, :], ALU.subtract))
            chain.step(nc.vector.tensor_copy(R["spread"][:, :, :], w["pick"][:, :].unsqueeze(2).broadcast_to([P, GW, P])))


def experts(nc, nm, F, C, X, R, w):
    ne, chunks, fn = F["gated"], F["chunks"], F["act"]
    pairs = [(e, c) for e in range(F["experts"]) for c in range(chunks)]
    NP, RH, LAG = len(pairs), 4, 2
    NG = ne
    with ExitStack() as ctx:
        sb = lambda name, shape, dt=F32: ctx.enter_context(nc.sbuf_tensor(nm + name, shape, dt))
        sem = semaphores(nc, ctx, nm + "experts_")
        bank = lambda name: ctx.enter_context(nc.psum_tensor(nm + name, [P, BW], F32))
        psH, psG, psY, psT = [bank("psH0"), bank("psH1")], [bank("psS0"), bank("psS1")], [bank("psY0"), bank("psY1")], bank("psX")
        h, hs, yS = sb("h", [P, RH, BW]), sb("hs", [P, RH, BW]), sb("yS", [P, 2, BW])
        h_full, h_ready, g_full, g_used, hs_ready, y_done = [sem(x) for x in ("h_full", "h_ready", "g_full", "g_used", "hs_ready", "y_done")]
        y_full, y_copied, y_turned, x_added = [sem(x) for x in ("y_full", "y_copied", "y_turned", "x_added")]
        block = ctx.enter_context(nc.Block())

        @block.tensor
        def _(pe):
            pe.sem_inc(y_done, RH)
            with pe.Fori(0, NB // 2) as i:
                for p in range(2):
                    n = 2 * i + p
                    x = R["XT"][:, ds(n * BW, BW)]
                    g = R["GT"][:, ds(n * BW, BW)]

                    def out(k):
                        e, c = pairs[k]
                        if k == 0:
                            pe.wait_ge(y_copied, n + 1)
                            for b in range(3):
                                pe.matmul(psY[p][:, :], R["b2p"][:, b, :], g, start=b == 0, stop=False)
                        pe.wait_ge(hs_ready, NP * n + k + 1 + RH)
                        mm = pe.matmul(psY[p][:, :], w["W2"][:, e, c, :], hs[:, k % RH, :], start=False, stop=k == NP - 1)
                        mm.then_inc(y_done, 1)

                    for k, (e, c) in enumerate(pairs):
                        pe.wait_ge(h_ready, NP * n + k + 1)
                        pe.matmul(psH[k % 2][:, :], w["W1"][:, e, c * P:(c + 1) * P], x, start=True, stop=True).then_inc(h_full, 1)
                        if c == 0 and e < ne:
                            pe.wait_ge(g_used, NG * n + e + 1)
                            pe.matmul(psG[(NG * p + e) % 2][:, :], R["spread"][:, e, :], g, start=True, stop=True).then_inc(g_full, 1)
                        if k >= LAG:
                            out(k - LAG)
                    for k in range(NP - LAG, NP):
                        out(k)
                    pe.wait_ge(y_copied, n + 3)
                    pe.wait_ge(x_added, n + 1)
                    for t in range(TB):
                        mm = pe.transpose(psT[:, t * P:(t + 1) * P], yS[:, p, t * P:(t + 1) * P], C["ident"][:, :])
                    mm.then_inc(y_turned, 1)

        @block.scalar
        def _(act):
            act.sem_inc(h_ready, 2)
            act.sem_inc(y_copied, 2)
            with act.Fori(0, NB // 2) as i:
                for p in range(2):
                    n = 2 * i + p
                    for k, (e, c) in enumerate(pairs):
                        act.wait_ge(h_full, NP * n + k + 1)
                        act.wait_ge(hs_ready, NP * n + k + 1)
                        nc.scalar.activation(h[:, k % RH, :], psH[k % 2][:, :], fn, bias=w["b1"][:, k:k + 1]).then_inc(h_ready, 1)
                    act.wait_ge(y_done, NP * (n + 1) + RH)
                    act.wait_ge(x_added, n + 1)
                    nc.scalar.activation(yS[:, p, :], psY[p][:, :], ACT.Copy).then_inc(y_copied, 1)

        @block.vector
        def _(dve):
            dve.sem_inc(hs_ready, RH)
            dve.sem_inc(g_used, 2)
            dve.sem_inc(x_added, 1)
            with dve.Fori(0, NB // 2) as i:
                for p in range(2):
                    n = 2 * i + p
                    for k, (e, c) in enumerate(pairs):
                        dve.wait_ge(h_ready, NP * n + k + 3)
                        dve.wait_ge(y_done, NP * n + k + 1)
                        if e < ne:
                            dve.wait_ge(g_full, NG * n + e + 1)
                            nc.vector.tensor_tensor(hs[:, k % RH, :], h[:, k % RH, :], psG[(NG * p + e) % 2][:, :], ALU.mult).then_inc(hs_ready, 1)
                            if c == chunks - 1:
                                dve.wait_ge(hs_ready, NP * n + k + 1 + RH)
                                dve.sem_inc(g_used, 1)
                        else:
                            nc.vector.tensor_copy(hs[:, k % RH, :], h[:, k % RH, :]).then_inc(hs_ready, 1)
                    dve.wait_ge(y_turned, n + 1)
                    xt = X[:, ds(n * TB, TB), :]
                    nc.vector.tensor_tensor(xt, psT[:, :].rearrange("p (t e) -> p t e", t=TB), xt, ALU.add).then_inc(x_added, 1)


def feed_forward(nc, kind, nm, C, X, d):
    F = FFN[kind]
    with ExitStack() as ctx:
        sb = lambda name, shape, dt=F32: ctx.enter_context(nc.sbuf_tensor(nm + name, shape, dt))
        ne, ch = F["gated"], F["chunks"]
        R = {"XT": sb("XT", [P, B * S]), "GT": sb("GT", [P, B * S], BF16), "b2p": sb("b2p", [P, 3, P], BF16),
             "spread": sb("spread", [P, GW, P], BF16)}
        w = {"W1": sb("W1", [P, F["experts"], ch * P]), "W2": sb("W2", [P, F["experts"], ch, P]),
             "b1": sb("b1", [P, F["experts"] * ch]), "b2r": sb("b2r", [P, P]), "pick": sb("pick", [P, GW]),
             "router": sb("router", [P, ne]), "b2": d[kind + "_b2"]}
        w["loads"] = [(w["router"][:, :], d[kind + "_router"]), (w["pick"][:, :], d["pick"]), (w["b1"][:, :], d[kind + "_b1"]),
                      (w["W1"][:, :, :], d[kind + "_W1"]), (w["W2"][:, :, :, :], d[kind + "_W2"])]
        if "top" in F:
            w["br"] = sb("br", [P, ne])
            w["loads"].append((w["br"][:, :], d[kind + "_br"].broadcast_to([P, ne])))
        route(nc, nm, F, C, X, R, w)
        experts(nc, nm, F, C, X, R, w)


LAYERS = {
    "a0": dict(name="a0_", causal=True, max=True, scale=float(D) ** -0.5, clip=None, floor=False,
               rope=None, bias=True, latent=False, suffix=False, tables=None),
    "b0": dict(name="b0_", causal=True, max=False, scale=float(D + D // 2) ** -0.5, clip=80.0, floor=False,
               rope="pairs", bias=False, latent=True, suffix=False, tables="pairs",
               most=float(np.exp(80.0 / np.sqrt(12.0))), least=float(np.exp(-80.0 / np.sqrt(12.0)))),
    "a1": dict(name="a1_", causal=True, max=True, scale=float(D) ** -0.5, clip=100.0, floor=True,
               rope=None, bias=False, latent=False, suffix=True, tables=None),
    "b1": dict(name="b1_", causal=False, max=True, scale=float(D) ** -0.5, clip=None, floor=False,
               rope="half", bias=False, latent=False, suffix=False, tables="half"),
}


def weights_of(kind, d):
    sq = (P, P)
    if kind == "a0":
        return {"q": (d["a0_wq"], 0, sq), "k": (d["a0_wk"], 0, sq), "v": (d["a0_wv"], 0, sq), "o": (d["a0_wo"], 0, sq),
                "bq": (d["a0_bq"], 0, (P, 1)), "bk": (d["a0_bk"], 0, (P, 1)),
                "bv": (d["a0_bv"].broadcast_to([P, P]), 0, sq), "bo": (d["a0_bo"].broadcast_to([P, P]), 0, sq)}
    if kind == "b0":
        return {"down": (d["b0_down"], 0, (P, 64)), "kr": (d["b0_kr"], 0, (P, 4)), "kr_rot": (d["b0_krr"], 0, (P, 4)),
                "q": (d["b0_wq"], 0, (32, P)), "k": (d["b0_wk"], 32, (32, P)), "v": (d["b0_wv"], 32, (32, P)),
                "qr": (d["b0_qr"], 0, (32, 64)), "qr_rot": (d["b0_qrr"], 0, (32, 64)), "o": (d["b0_wo"], 0, sq)}
    if kind == "a1":
        return {**{n: (d["a1_w" + n], 0, sq) for n in "qkvo"}, "heads": (d["heads"], 0, (P, H))}
    return {"q": (d["b1_wq"], 0, sq), "q_rot": (d["b1_wqr"], 0, sq), "k": (d["b1_wk"], 0, sq), "k_rot": (d["b1_wkr"], 0, sq),
            "v": (d["b1_wv"], 0, sq), "o": (d["b1_wo"], 0, sq), "bo": (d["b1_bo"].broadcast_to([P, P]), 0, sq)}


STAGES = ("a0", "f0", "b0", "f0", "a1", "f1", "b1", "f1")


def build(nc, d, out, stages=STAGES):
    scratch = {
        "q": nc.dram_tensor("scratch_q", [UNITS + 2, 32, 3, S], BF16, kind="Internal").ap(),
        "k": nc.dram_tensor("scratch_k", [UNITS + 2, 32, 3, S], BF16, kind="Internal").ap(),
        "qr": nc.dram_tensor("scratch_qr", [UNITS + 2, 16, 3, S], BF16, kind="Internal").ap(),
        "kr": nc.dram_tensor("scratch_kr", [UNITS + 2, 4, 3, S], BF16, kind="Internal").ap(),
    }
    scratch["low"] = nc.dram_tensor("scratch_low", [2, HG, KT, P], F32, kind="Internal").ap()
    with ExitStack() as ctx:
        sb = lambda name, shape, dt=F32: ctx.enter_context(nc.sbuf_tensor(name, shape, dt))
        X = sb("X", [P, NT, P])
        C = {"ident": sb("ident", [P, P]), "ident16": sb("ident16", [P, P], BF16),
             "mask": sb("mask", [P, P]), "mask16": sb("mask16", [P, P], BF16), "eps": sb("eps", [P, 1])}
        x_loaded, c_loaded, c_ready, x_stored = [nc.alloc_semaphore(n) for n in ("x_loaded", "c_loaded", "c_ready", "x_stored")]
        with nc.Block() as block:
            @block.sync
            def _(sp):
                sp.dma_start(X[:, :, :], d["x"].rearrange("(t p) e -> p t e", p=P)).then_inc(x_loaded, 16)
                sp.dma_start(C["ident"][:, :], d["ident"]).then_inc(c_loaded, 16)
                sp.dma_start(C["mask"][:, :], d["mask"]).then_inc(c_loaded, 16)
                sp.wait_ge(x_loaded, 16)

            @block.vector
            def _(dve):
                nc.vector.memset(C["eps"][:, :], LN_EPS).then_inc(c_ready, 1)
                dve.wait_ge(c_loaded, 32)
                nc.vector.tensor_copy(C["ident16"][:, :], C["ident"][:, :]).then_inc(c_ready, 1)
                nc.vector.tensor_copy(C["mask16"][:, :], C["mask"][:, :]).then_inc(c_ready, 1)

        for n, kind in enumerate(stages):
            if kind in LAYERS:
                attention(nc, LAYERS[kind], C, X, weights_of(kind, d), scratch, d)
            else:
                feed_forward(nc, kind, f"{kind}{n}_", C, X, d)
        with nc.Block() as block:
            @block.sync
            def _(sp):
                sp.dma_start(out.rearrange("(t p) e -> p t e", p=P), X[:, :, :]).then_inc(x_stored, 16)
                sp.wait_ge(x_stored, 16)


def laid_out(inputs):
    f = np.float32
    a = {k: np.asarray(v) for k, v in inputs.items()}
    d = {"x": a["L0_attn_a_x"].reshape(B * S, E)}
    d["ident"] = np.eye(P, dtype=f)
    d["mask"] = np.where(np.arange(P)[None, :] > np.arange(P)[:, None], f(NEG), f(0))
    w1 = a["L0_attn_a_W1"].reshape(E, H, 3, D)
    b1 = a["L0_attn_a_b1"].reshape(H, 3, D)
    for i, n in enumerate("qkv"):
        d["a0_w" + n] = w1[:, :, i].reshape(E, P)
    d["a0_bq"], d["a0_bk"], d["a0_bv"] = b1[:, 0].reshape(P, 1), b1[:, 1].reshape(P, 1), b1[:, 2].reshape(1, P)
    d["a0_wo"], d["a0_bo"] = a["L0_attn_a_Wp"], a["L0_attn_a_bp"].reshape(1, P)
    d["b0_down"] = np.concatenate([a["L0_attn_b_W_DQ"], a["L0_attn_b_W_DKV"]], 1)
    d["b0_wq"], d["b0_wk"], d["b0_wv"] = a["L0_attn_b_W_UQ"], a["L0_attn_b_W_UK"], a["L0_attn_b_W_UV"]
    d["b0_wo"] = a["L0_attn_b_W_O"]
    pairs = lambda w: w.reshape(w.shape[0], -1, 2)[:, :, ::-1].reshape(w.shape)
    d["b0_qr"], d["b0_kr"] = a["L0_attn_b_W_QR"], a["L0_attn_b_W_KR"]
    d["b0_qrr"], d["b0_krr"] = pairs(d["b0_qr"]), pairs(d["b0_kr"])
    wt = a["L1_attn_a_w_qkv"].T
    for i, n in enumerate("qkv"):
        d["a1_w" + n] = wt[:, i * P:(i + 1) * P]
    d["a1_wo"] = a["L1_attn_a_w_proj"].T
    halves = lambda w: w.reshape(E, H, 2, D // 2)[:, :, ::-1].reshape(E, P)
    for i, n in enumerate("qkv"):
        d["b1_w" + n] = a["L1_attn_b_w_qkv"][:, i * P:(i + 1) * P]
    d["b1_wqr"], d["b1_wkr"] = halves(d["b1_wq"]), halves(d["b1_wk"])
    d["b1_wo"], d["b1_bo"] = a["L1_attn_b_w_out"], a["L1_attn_b_b_out"].reshape(1, P)
    d["heads"] = (np.arange(P)[:, None] // D == np.arange(H)[None, :]).astype(f)
    d["masked"] = (S - 1 - np.arange(KT)[None, :] * P - np.arange(P)[:, None]).astype(f)
    ew = lambda x, y: np.concatenate([x, y[None]], 0)
    for kind, ws in (("f0", ("L0_ffn_eW1", "L0_ffn_sW1", "L0_ffn_eb1", "L0_ffn_sb1", "L0_ffn_eW2", "L0_ffn_sW2", "L0_ffn_eb2", "L0_ffn_sb2")),
                     ("f1", ("L1_ffn_W1", "L1_ffn_Ws1", "L1_ffn_b1", "L1_ffn_bs1", "L1_ffn_W2", "L1_ffn_Ws2", "L1_ffn_b2", "L1_ffn_bs2"))):
        W1, b1, W2, b2 = (ew(a[ws[2 * i]], a[ws[2 * i + 1]]) for i in range(4))
        ex, ch = W1.shape[0], W1.shape[2] // P
        d[kind + "_W1"] = W1.transpose(1, 0, 2)
        d[kind + "_W2"] = W2.reshape(ex, ch, P, P).transpose(2, 0, 1, 3)
        d[kind + "_b1"] = b1.reshape(ex * ch, P).T
        d[kind + "_b2"] = b2
    d["f0_router"], d["f0_br"] = a["L0_ffn_router_W"], a["L0_ffn_router_b"].reshape(1, -1)
    d["f1_router"] = a["L1_ffn_gate_weight"].T
    r = np.arange(P)[:, None]
    d["pick"] = ((r % GW == np.arange(GW)[None, :]) & (r < 3 * GW)).astype(f)
    pos = np.arange(S, dtype=f)
    inv = f(10000.0) ** (-np.arange(0, 4, 2, dtype=f) / f(4))
    ang = pos[None, :] * inv[:, None]
    r = np.arange(64)
    d["pairs"] = np.stack([np.cos(ang)[(r % 4) // 2], np.sin(ang)[(r % 4) // 2] * np.where(r % 2 == 0, f(-1), f(1))[:, None]], 1)
    theta = f(1.0) / f(10000.0) ** (np.arange(0, D, 2, dtype=f) / f(D))
    ang = pos[None, :] * theta[:, None]
    r = np.arange(P)
    d["half"] = np.stack([np.cos(ang)[r % 4], np.sin(ang)[r % 4] * np.where(r % D < D // 2, f(-1), f(1))[:, None]], 1)
    return {k: np.ascontiguousarray(v) for k, v in d.items()}


def kernel(**inputs):
    import concourse.bacc as bacc
    from concourse.bass_utils import run_bass_kernel_spmd

    nc = bacc.Bacc("TRN2", target_bir_lowering=False, num_devices=1)
    arrays = laid_out(inputs)
    d = {n: nc.dram_tensor("in_" + n, v.shape, mybir.dt.from_np(v.dtype), kind="ExternalInput").ap() for n, v in arrays.items()}
    out = nc.dram_tensor("out", (B * S, E), F32, kind="ExternalOutput").ap()
    build(nc, d, out)
    r = run_bass_kernel_spmd(nc, [{"in_" + n: v for n, v in arrays.items()}], core_ids=[0])
    return np.asarray(r.results[0]["out"]).reshape(B, S, E)
```

```python
from contextlib import ExitStack

import numpy as np

import concourse.bass as bass
from concourse import mybir

F32 = mybir.dt.float32
BF16 = mybir.dt.bfloat16
I32 = mybir.dt.int32
F32R = mybir.dt.float32r
ALU = mybir.AluOpType
ACT = mybir.ActivationFunctionType
AX_X = mybir.AxisListType.X
ds = bass.ds

P = 128
B, S, E = 4, 1024, 128
NT = B * S // P
NB = 8
TB = 4
BW = TB * P
H, D = 16, 8
G, HG = 4, 4
UNITS = B * G
KT = S // P
VW = 32
LN_EPS = 1e-5
NEG = -1e30

Q_TERMS = (0, 0, 0, 1, 1, 2)
K_TERMS = (0, 1, 2, 0, 1, 0)
NTERM = len(Q_TERMS)
R_ROW = 64
M_ROW = 96
LAG = 2
SPLIT_AHEAD, MAXIMA_AHEAD = 6000, 3600
RING_P = 4
RING_Q = 4


class Chain:

    def __init__(self, eng, sem, base=0):
        self.eng, self.sem, self.base, self.n = eng, sem, base, 0

    def step(self, ins):
        ins.then_inc(self.sem, 1)
        self.n += 1

    def wait(self):
        self.eng.wait_ge(self.sem, self.base + self.n)

    def link(self, ins):
        self.step(ins)
        self.wait()


def matmul_split(pe, out, weights, moving, start, stop):
    (wh, wl), (mh, ml) = weights, moving
    pe.matmul(out, wh, mh, start=start, stop=False)
    pe.matmul(out, wh, ml, start=False, stop=False)
    return pe.matmul(out, wl, mh, start=False, stop=stop)


def semaphores(nc, ctx, prefix):
    held = []

    def sem(name):
        held.append(nc.alloc_semaphore(prefix + name))
        return held[-1]

    def give_back():
        nc.clear_and_free_semaphores(held)
        nc.all_engine_barrier()
    ctx.callback(give_back)
    return sem


def steps_of(causal):
    out = []
    for qb in range(S // BW):
        for kt in range(TB * (qb + 1) if causal else KT):
            diagonal = causal and kt >= TB * qb
            out.append((qb, kt, P * (kt - TB * qb) if diagonal else 0, diagonal))
    return out


def row_blocks_of(causal):
    out = []
    for j in range(HG):
        for qt in range(KT):
            keys = P * (qt + 1) if causal else S
            for half in range((keys + BW - 1) // BW):
                width = min(BW, keys - BW * half)
                out.append((j, qt, half, width, causal and BW * half + width == keys))
    return out


def beside_of(steps, rows):
    parts = [(s, part, (BW - q0) * (1, 1, 2)[part]) for s, (_, _, q0, _) in enumerate(steps) for part in range(3)]
    beside = [[[], [], []] for _ in steps]
    if not rows:
        return beside, []
    left = [sum(w for _, _, w in parts[k + 1:]) for k in range(len(parts))]
    split_at = max(k for k in range(len(parts)) if left[k] >= SPLIT_AHEAD)
    maxima_at = max(k for k in range(len(parts)) if left[k] >= MAXIMA_AHEAD)
    order = list(range(split_at, len(parts))) + list(range(split_at))
    total, cost = sum(w for _, _, w in parts), sum(b[3] + 64 for b in rows)
    todo, spent, passed, early = list(rows), 0, 0, []
    s, part, _ = parts[split_at]
    beside[s][part].append(("split", None))
    for k in order:
        s, part, w = parts[k]
        passed += w
        if k == maxima_at:
            beside[s][part].append(("maxima", None))
        while todo and (spent + (todo[0][3] + 64) / 2) * total <= passed * cost:
            b = todo.pop(0)
            spent += b[3] + 64
            beside[s][part].append(("rows", (2 if k >= split_at else 1, b)))
            if k >= split_at:
                early.append(b)
    assert not todo
    return beside, early


def attention_prepare(nc, L, C, X, A, w, scratch):
    rope, has_bias, latent, suffix = L["rope"], L["bias"], L["latent"], L["suffix"]
    nm = L["name"]
    with ExitStack() as ctx:
        sb = lambda name, shape, dt=F32: ctx.enter_context(nc.sbuf_tensor(nm + name, shape, dt))
        sem = semaphores(nc, ctx, nm + "prepare_")
        psum = lambda name, dt=F32: ctx.enter_context(nc.psum_tensor(nm + name, [P, BW], dt))

        stats = sb("stats", [P, 2, TB, 6])
        mv = sb("mv", [P, 2, TB, 2])
        sd = sb("sd", [P, 2, TB])
        rstd = sb("rstd", [P, 2, TB])
        xn = sb("xn", [P, 2, TB, P])
        xnT = sb("xnT", [P, 2, BW])
        psT = [psum("psT0"), psum("psT1")]
        psV = psum("psV")
        parts = [("q", P), ("k", P)] + ([("qr", 64), ("kr", 4)] if latent else [])
        roped = {"q", "k"} if rope == "half" else {"qr", "kr"} if rope == "pairs" else set()
        ps = {}
        if latent:
            ps_c = psum("psC")
            banks = [psum(f"psP{i}") for i in range(4)]
            ps = {"q": banks[0], "k": banks[1], "qr": banks[2], "kr": banks[3],
                  "qr_rot": banks[0], "kr_rot": banks[1]}
            cT = sb("cT", [64, 2, BW])
        else:
            for name, _ in parts:
                ps[name] = psum("ps" + name)
                if name in roped:
                    ps[name + "_rot"] = psum("ps" + name + "r")
        full = {n: sb("full" + n, [r, BW]) for n, r in parts}
        rest = {n: sb("rest" + n, [r, BW]) for n, r in parts}
        turned = {n: sb("turned" + n, [r, BW]) for n, r in parts if n in roped}
        pieces = {n: sb("pieces" + n, [r, 2, 3, BW], BF16) for n, r in parts}
        if suffix:
            square = {n: sb("square" + n, [P, BW]) for n in "qk"}
            norms = {n: psum("norms" + n) for n in "qk"}
            squared, norms_full, norms_read = sem("squared"), sem("norms_full"), sem("norms_read")

        mv_ready, sd_ready, xn_ready = sem("mv_ready"), sem("sd_ready"), sem("xn_ready")
        xT_in_psum, xT_ready, c_in_psum, c_ready = sem("xT_in_psum"), sem("xT_ready"), sem("c_in_psum"), sem("c_ready")
        proj_ready = {n: sem("proj_" + n) for n, _ in parts}
        rot_ready = {n: sem("rot_" + n) for n in roped}
        v_in_psum, v_ready = sem("v_in_psum"), sem("v_ready")
        full_ready = {n: sem("full_" + n) for n, _ in parts}
        first_ready = {n: sem("first_" + n) for n, _ in parts}
        rest_ready = {n: sem("rest_" + n) for n, _ in parts}
        second_ready = {n: sem("second_" + n) for n, _ in parts}
        third_ready = {n: sem("third_" + n) for n, _ in parts}
        stored = [sem("stored0"), sem("stored1")]
        dve_chain, pads_ready = sem("dve_chain"), sem("pads_ready")
        turned_ready = {n: sem("turned_" + n) for n in roped}
        w_ready = sem("w_ready")
        stores = G * len(parts)
        store_done = 16 * stores

        block = ctx.enter_context(nc.Block())

        @block.sync
        def _(sp):
            for dst, src in w["loads"]:
                sp.dma_start(dst, src).then_inc(w_ready, 16)
            for p in range(2):
                sp.sem_inc(stored[p], store_done)
            with sp.Fori(0, NB // 2) as i:
                for p in range(2):
                    for name, rows in parts:
                        sp.wait_ge(third_ready[name], 2 * i + p + 1)
                        per = rows // G if name != "kr" else rows
                        for g in range(G):
                            first = per * g if name != "kr" else 0
                            sp.dma_start(
                                scratch[name][ds(i * G + g, 1), :, :, p * BW:(p + 1) * BW].rearrange("u r c n -> (u r) c n"),
                                pieces[name][first:first + per, p]).then_inc(stored[p], 16)
            for p in range(2):
                sp.wait_ge(stored[p], store_done * (NB // 2 + 1))

        @block.tensor
        def _(pe):
            pe.wait_ge(w_ready, 16 * len(w["loads"]))
            with pe.Fori(0, NB // 2) as i:
                for p in range(2):
                    n = 2 * i + p
                    pe.wait_ge(xn_ready, n + 1)
                    for t in range(TB):
                        mm = pe.transpose(psT[p][:, t * P:(t + 1) * P], xn[:, p, t, :], C["ident"][:, :])
                    mm.then_inc(xT_in_psum, 1)
                    pe.wait_ge(xT_ready, n + 1)
                    x_block = xnT[:, p, :]
                    if latent:
                        pe.wait_ge(c_ready, n + 1)
                        pe.matmul(ps_c[0:64, :], w["down"][:, :], x_block, start=True, stop=True).then_inc(c_in_psum, 1)
                        pe.wait_ge(full_ready["kr"], n + 1)
                        pe.matmul(ps["kr"][0:4, :], w["kr"][:, :], x_block, start=True, stop=True).then_inc(proj_ready["kr"], 1)
                        pe.wait_ge(c_ready, n + 2)
                        pe.wait_ge(full_ready["qr"], n + 1)
                        pe.matmul(ps["qr"][0:64, :], w["qr"][0:32, :], cT[0:32, p, :], start=True, stop=True).then_inc(proj_ready["qr"], 1)
                        pe.matmul(ps["q"][:, :], w["q"][0:32, :], cT[0:32, p, :], start=True, stop=True).then_inc(proj_ready["q"], 1)
                        pe.matmul(ps["k"][:, :], w["k"][32:64, :], cT[32:64, p, :], start=True, stop=True).then_inc(proj_ready["k"], 1)
                        pe.wait_ge(first_ready["q"], n + 1)
                        pe.wait_ge(full_ready["q"], n + 2)
                        pe.matmul(ps["qr_rot"][0:64, :], w["qr_rot"][0:32, :], cT[0:32, p, :], start=True, stop=True).then_inc(rot_ready["qr"], 1)
                        pe.wait_ge(first_ready["k"], n + 1)
                        pe.wait_ge(full_ready["k"], n + 2)
                        pe.matmul(ps["kr_rot"][0:4, :], w["kr_rot"][:, :], x_block, start=True, stop=True).then_inc(rot_ready["kr"], 1)
                    else:
                        for name, _ in parts:
                            pe.wait_ge(full_ready[name], n + 1)
                            if name not in roped:
                                pe.wait_ge(first_ready[name], n + 1)
                            pe.matmul(ps[name][:, :], w[name][:, :], x_block, start=True, stop=True).then_inc(proj_ready[name], 1)
                            if name in roped:
                                pe.matmul(ps[name + "_rot"][:, :], w[name + "_rot"][:, :], x_block,
                                          start=True, stop=True).then_inc(rot_ready[name], 1)
                    pe.wait_ge(v_ready, n + 1)
                    for t in range(TB):
                        if latent:
                            mm = pe.matmul(psV[:, t * P:(t + 1) * P], cT[32:64, p, t * P:(t + 1) * P], w["v"][32:64, :],
                                           start=True, stop=True)
                        else:
                            mm = pe.matmul(psV[:, t * P:(t + 1) * P], xnT[:, p, t * P:(t + 1) * P], w["v"][:, :],
                                           start=True, stop=True)
                    mm.then_inc(v_in_psum, 1)
                    if suffix:
                        for k, name in enumerate("qk"):
                            pe.wait_ge(squared, 2 * n + k + 3)
                            pe.wait_ge(norms_read, 2 * n + k + 1)
                            pe.matmul(norms[name][0:H, :], w["heads"][:, :], square[name][:, :], start=True, stop=True).then_inc(norms_full, 1)

        @block.scalar
        def _(act):
            act.wait_ge(w_ready, 16 * len(w["loads"]))
            if latent:
                act.sem_inc(c_ready, 1)
            for name, _ in parts:
                if name not in roped:
                    act.sem_inc(full_ready[name], 1)
                    if not latent:
                        act.sem_inc(first_ready[name], 1)
            if not has_bias:
                act.sem_inc(v_ready, 1)
            with act.Fori(0, NB // 2) as i:
                for p in range(2):
                    n = 2 * i + p
                    act.wait_ge(mv_ready, n + 1)
                    nc.scalar.activation(sd[:, p, :], mv[:, p, :, 1], ACT.Sqrt, bias=C["eps"][:, 0:1]).then_inc(sd_ready, 1)
                    act.wait_ge(xT_in_psum, n + 1)
                    nc.scalar.activation(xnT[:, p, :], psT[p][:, :], ACT.Copy).then_inc(xT_ready, 1)
                    if latent:
                        act.wait_ge(c_in_psum, n + 1)
                        nc.scalar.activation(cT[:, p, :], ps_c[0:64, :], ACT.Copy).then_inc(c_ready, 1)
                    order = [x[0] for x in parts if x[0] not in roped] + [x[0] for x in parts if x[0] in roped]
                    for name in order:
                        if name in roped:
                            act.wait_ge(full_ready[name], n + 2)
                            src = full[name][:, :]
                        else:
                            act.wait_ge(proj_ready[name], n + 1)
                            rows = dict(parts)[name]
                            src = ps[name][0:rows, :]
                            act.wait_ge(rest_ready[name], n + 1)
                            if suffix:
                                act.wait_ge(squared, 2 * n + 1 + (name == "k"))
                            if has_bias:
                                nc.scalar.activation(full[name][:, :], src, ACT.Identity, bias=w["b" + name][:, 0:1]).then_inc(full_ready[name], 1)
                            else:
                                nc.scalar.activation(full[name][:, :], src, ACT.Copy).then_inc(full_ready[name], 1)
                        if name == order[0]:
                            act.wait_ge(stored[p], store_done * (i + 1))
                        if has_bias:
                            nc.scalar.activation(pieces[name][:, p, 0, :], src, ACT.Identity, bias=w["b" + name][:, 0:1]).then_inc(first_ready[name], 1)
                        else:
                            nc.scalar.activation(pieces[name][:, p, 0, :], src, ACT.Copy).then_inc(first_ready[name], 1)
                    if not has_bias:
                        act.wait_ge(v_in_psum, n + 1)
                        nc.scalar.activation(A["VR"][:, ds(i * G, G), p * TB:(p + 1) * TB, :],
                                             psV[:, :].rearrange("p (t g r) -> p g t r", g=G, r=32), ACT.Copy).then_inc(v_ready, 1)
                    for name in order:
                        act.wait_ge(rest_ready[name], n + 2)
                        nc.scalar.activation(pieces[name][:, p, 1, :], rest[name][:, :], ACT.Copy).then_inc(second_ready[name], 1)

        @block.vector
        def _(dve):
            dve.wait_ge(w_ready, 16 * len(w["loads"]))
            for name in roped:
                dve.sem_inc(turned_ready[name], 1)
            for name, _ in parts:
                dve.sem_inc(rest_ready[name], 1)
            if has_bias:
                dve.sem_inc(v_ready, 1)
            if suffix:
                dve.sem_inc(norms_read, 2)
            per = TB + 1
            with dve.Fori(0, NB // 2) as i:
                for p in range(2):
                    n = 2 * i + p
                    chain = Chain(dve, dve_chain, per * n)
                    for t in range(TB):
                        chain.step(nc.vector.bn_stats(stats[:, p, t, :], X[:, ds(n * TB + t, 1), :].rearrange("p a e -> p (a e)")))
                    chain.wait()
                    dve.nop(nofuse=True)
                    for t in range(TB):
                        ins = nc.vector.bn_aggr(mv[:, p, t, :], stats[:, p, t, :])
                    ins.then_inc(mv_ready, 1)
                    dve.wait_ge(sd_ready, n + 1)
                    chain.link(nc.vector.reciprocal(rstd[:, p, :], sd[:, p, :]))
                    for t in range(TB):
                        ins = nc.vector.tensor_scalar(xn[:, p, t, :], X[:, ds(n * TB + t, 1), :].rearrange("p a e -> p (a e)"),
                                                      mv[:, p, t, 0:1], rstd[:, p, t:t + 1], ALU.subtract, ALU.mult)
                    ins.then_inc(xn_ready, 1)
                    for name, rows in parts:
                        if name in roped:
                            table = C[L["tables"]]
                            dve.wait_ge(proj_ready[name], n + 1)
                            dve.wait_ge(turned_ready[name], n + 1)
                            nc.vector.tensor_tensor(rest[name][:, :], ps[name][0:rows, :], table[0:rows, 0, p * BW:(p + 1) * BW], ALU.mult)
                            dve.wait_ge(rot_ready[name], n + 1)
                            nc.vector.tensor_tensor(turned[name][:, :], ps[name + "_rot"][0:rows, :],
                                                    table[0:rows, 1, p * BW:(p + 1) * BW], ALU.mult).then_inc(turned_ready[name], 1)
                    for name, _ in parts:
                        dve.wait_ge(first_ready[name], n + 1 + (0 if latent or name in roped else 1))
                        dve.wait_ge(full_ready[name], n + 2)
                        nc.vector.tensor_tensor(rest[name][:, :], full[name][:, :], pieces[name][:, p, 0, :], ALU.subtract).then_inc(rest_ready[name], 1)
                    for name, _ in parts:
                        dve.wait_ge(second_ready[name], n + 1)
                        nc.vector.tensor_tensor(pieces[name][:, p, 2, :], rest[name][:, :], pieces[name][:, p, 1, :], ALU.subtract).then_inc(third_ready[name], 1)
                    if suffix:
                        for k, name in enumerate("qk"):
                            dve.wait_ge(norms_full, 2 * n + k + 1)
                            nc.vector.tensor_reduce(A["peak"][:, k, ds(n, 1)], norms[name][0:H, :], AX_X, ALU.max).then_inc(norms_read, 1)
                    if has_bias:
                        dve.wait_ge(v_in_psum, n + 1)
                        for t in range(TB):
                            ins = nc.vector.tensor_tensor(
                                A["VR"][:, ds(i * G, G), p * TB + t, :],
                                psV[:, t * P:(t + 1) * P].rearrange("p (g r) -> p g r", r=32),
                                w["bv"][:, :].rearrange("p (g r) -> p g r", r=32), ALU.add)
                        ins.then_inc(v_ready, 1)

        @block.gpsimd
        def _(pool):
            for name in roped:
                pool.sem_inc(full_ready[name], 1)
            nc.gpsimd.memset(A["VR"][:, UNITS, :, :], 0.0)
            for b in range(RING_Q):
                nc.gpsimd.memset(A["Q"][b][:, :, :].bitcast(I32), 0)
                nc.gpsimd.memset(A["K"][b][:, :, :].bitcast(I32), 0)
            for b in range(2):
                last = nc.gpsimd.memset(A["V"][b][:, :, :, :], 0.0)
            last.then_inc(pads_ready, 1)
            pool.wait_ge(pads_ready, 1)
            for b in range(RING_Q):
                last = nc.gpsimd.memset(A["K"][b][M_ROW:M_ROW + 3, :, :], 1.0)
            last.then_inc(pads_ready, 1)
            pool.wait_ge(pads_ready, 2)
            for b in range(2):
                last = nc.gpsimd.memset(A["V"][b][:, :, :, D:D + 1], 1.0)
            last.then_inc(pads_ready, 1)
            pool.wait_ge(pads_ready, 3)
            if suffix:
                pool.sem_inc(squared, 2)
                with pool.Fori(0, NB) as n:
                    for k, name in enumerate("qk"):
                        pool.wait_ge(full_ready[name], n + 2)
                        pool.wait_ge(norms_read, 2 * n + k + 1)
                        nc.gpsimd.tensor_tensor(square[name][:, :], full[name][:, :], full[name][:, :], ALU.mult).then_inc(squared, 1)
            if roped:
                with pool.Fori(0, NB // 2) as i:
                    for p in range(2):
                        n = 2 * i + p
                        for name, _ in parts:
                            if name in roped:
                                pool.wait_ge(turned_ready[name], n + 2)
                                nc.gpsimd.tensor_tensor(full[name][:, :], rest[name][:, :], turned[name][:, :], ALU.add).then_inc(full_ready[name], 1)


def masked_sums(nc, L, C, A, d):
    nm = L["name"]
    with ExitStack() as ctx:
        sb = lambda name, shape, dt=F32: ctx.enter_context(nc.sbuf_tensor(nm + name, shape, dt))
        sem = semaphores(nc, ctx, nm + "sums_")
        bank = lambda name: ctx.enter_context(nc.psum_tensor(nm + name, [P, BW], F32))
        later, ones = sb("later", [P, P]), sb("onesq", [P, P])
        after = sb("after", [P, 2, UNITS, 32])
        peaks, bound, most = sb("peaks", [H, 2]), sb("bound", [H, 1]), sb("most", [1, 1])
        psS, psB = [bank("psF0"), bank("psF1")], bank("psB")
        ready, later_ready, added, done, copied, bounded, turned = [sem("ms_" + x) for x in ("ready", "later", "added", "done", "copied", "bounded", "turned")]
        chain_sem = sem("ms_chain")
        block = ctx.enter_context(nc.Block())
        V = A["VR"]

        @block.sync
        def _(sp):
            sp.dma_start(A["masked"][:, :], d["masked"]).then_inc(ready, 16)
            sp.wait_ge(ready, 16)

        @block.gpsimd
        def _(pool):
            nc.gpsimd.memset(A["SUF"][:, 0, :, :], 0.0)
            nc.gpsimd.memset(A["SUM"][:, 0, :], 0.0)
            nc.gpsimd.memset(after[:, (KT - 1) % 2], 0.0).then_inc(added, 1)
            for t in reversed(range(-1, KT - 1)):
                pool.wait_ge(added, KT - 1 - t)
                if t < KT - 2:
                    pool.wait_ge(done, KT - 2 - t)
                nc.gpsimd.tensor_tensor(after[:, t % 2], after[:, (t + 1) % 2], V[:, 0:UNITS, t + 1, :], ALU.add).then_inc(added, 1)

        @block.tensor
        def _(pe):
            pe.wait_ge(later_ready, 2)
            for n, t in enumerate(reversed(range(-1, KT))):
                pe.wait_ge(added, n + 1)
                if n >= 2:
                    pe.wait_ge(copied, n - 1)
                out = psS[n % 2][:, :].rearrange("p (u r) -> p u r", r=32)
                if t >= 0:
                    pe.matmul(out, later[:, :], V[:, 0:UNITS, t, :], start=True, stop=False)
                pe.matmul(out, ones[:, :], after[:, t % 2], start=t < 0, stop=True).then_inc(done, 1)
            pe.wait_ge(bounded, 1)
            pe.matmul(psB[0:1, 0:H], bound[:, :], C["ident"][0:H, 0:H], start=True, stop=True).then_inc(turned, 1)

        @block.scalar
        def _(act):
            for n, t in enumerate(reversed(range(-1, KT))):
                act.wait_ge(done, n + 1)
                src = psS[n % 2][:, :].rearrange("p (u r) -> p u r", r=32)
                dst = A["SUF"][:, 1:UNITS + 1, t, :] if t >= 0 else A["SUM"][:, 1:UNITS + 1, :]
                nc.scalar.activation(dst, src, ACT.Copy).then_inc(copied, 1)

        @block.vector
        def _(dve):
            chain = Chain(dve, chain_sem)
            nc.vector.memset(ones[:, :], 1.0).then_inc(later_ready, 1)
            nc.vector.memset(A["clip_bias"][:, :], -L["clip"])
            chain.link(nc.vector.tensor_scalar(later[:, :], C["mask"][:, :], -1.0, None, ALU.is_ge))
            nc.vector.tensor_tensor(later[:, :], later[:, :], C["ident"][:, :], ALU.subtract).then_inc(later_ready, 1)
            chain.link(nc.vector.tensor_reduce(peaks[:, :], A["peak"][:, :, :], AX_X, ALU.max))
            nc.vector.tensor_tensor(bound[:, :], peaks[:, 0:1], peaks[:, 1:2], ALU.mult).then_inc(bounded, 1)
            dve.wait_ge(turned, 1)
            chain.link(nc.vector.tensor_reduce(most[:, :], psB[0:1, 0:H], AX_X, ALU.max))
            chain.link(nc.vector.tensor_scalar(A["may_clip"][0:1, :], most[:, :], 0.99 * (L["clip"] / L["scale"]) ** 2, None, ALU.is_ge))


def attention_core(nc, L, C, A, scratch):
    nm = L["name"]
    causal, needs_max, scale, latent = L["causal"], L["max"], L["scale"], L["latent"]
    floor = L["floor"]
    steps = steps_of(causal)
    NS = len(steps)
    rows = row_blocks_of(causal) if needs_max else []
    NR = len(rows)
    first_half = max(s for s in range(NS) if steps[s][0] == 0)
    NDIAG = sum(s[3] for s in steps)

    beside, early = beside_of(steps, rows)
    beside[LAG + 1][0].append(("output", -1))
    beside[first_half + LAG + 2][0].append(("output", 0))
    before = [("rows", (0, b)) for b in rows] + [("split", None), ("maxima", None)] + [("rows", (1, b)) for b in early] if needs_max else []
    PRO = sum(kind != "split" for kind, _ in before)
    USES = sum(kind != "split" for step in beside for part in step for kind, _ in part)
    if needs_max:
        MAX_PRO = NR
        MAX_USE = [kind for step in beside for part in step for kind, _ in part if kind != "split"].index("maxima")
    EXP0, TRI0, CLIP0 = 2 * (LAG + 1), LAG, LAG + 1

    with ExitStack() as ctx:
        sb = lambda name, shape, dt=F32: ctx.enter_context(nc.sbuf_tensor(nm + name, shape, dt))
        sem = semaphores(nc, ctx, nm + "core_")
        st = [ctx.enter_context(nc.psum_tensor(nm + f"st{i}", [P, 2, BW], F32)) for i in range(2)]
        row = [ctx.enter_context(nc.psum_tensor(nm + f"row{i}", [P, BW], F32)) for i in range(2)]
        acc = [ctx.enter_context(nc.psum_tensor(nm + f"acc{i}", [P, BW], F32)) for i in range(2)]
        prob = sb("prob", [P, RING_P, HG, BW])
        halfmax = sb("halfmax", [P, 2, HG, KT, 2])
        rowmax = sb("rowmax", [P, 2, HG, KT])
        left = sb("left", [P, 2, HG, KT])
        mpieces = sb("mpieces", [P, 3, HG, KT], BF16)
        mT = sb("mT", [3 * HG * KT, 2, P], BF16)
        accS = sb("accS", [P, 2, BW])
        rsum = sb("rsum", [P, TB, HG])
        if floor:
            lowest = sb("lowest", [P, 2, HG, KT])
            num = sb("num", [P, TB, HG, D])
            tail = sb("tail", [P, TB, HG, D])
            mass = sb("mass", [P, TB, HG])
            share = sb("share", [P, TB, HG])
            whole = sb("whole", [P, TB, HG])
            floors = sb("floors", [P, HG, S])
            low_ready, low_stored, floors_loaded = sem("low_ready"), sem("low_stored"), sem("floors_loaded")

        loaded = [sem(f"loaded{b}") for b in range(RING_Q)]
        v_loaded = sem("v_loaded")
        m_loaded = [sem("m_loaded0"), sem("m_loaded1")]
        st_full, exp_done = sem("st_full"), sem("exp_done")
        tri_done, clip_done = sem("tri_done"), sem("clip_done")
        pv_done = sem("pv_done")
        row_full, row_read = sem("row_full"), sem("row_read")
        m_split = sem("m_split")
        acc_copied, acc_turned = sem("acc_copied"), sem("acc_turned")
        dve_chain = sem("dve_chain")
        stand_in, stand_in_prob = sem("stand_in"), sem("stand_in_prob")
        NLOAD = 2 * NTERM * (2 if latent else 1)

        def over_units(eng, body):
            def rounds(general):
                with eng.Fori(0, UNITS // RING_Q) as i:
                    for q in range(RING_Q):
                        body(RING_Q * i + q, q, i, general)

            if not floor:
                rounds(L["clip"] is not None)
                return
            may_clip = eng.value_load(A["may_clip"][0:1, 0:1], min_val=0, max_val=1)
            with eng.If(may_clip):
                rounds(True)
            with eng.Else():
                rounds(False)

        block = ctx.enter_context(nc.Block())

        @block.sync
        def _(sp):
            stands = ["q", "k"] + (["qr", "kr"] if latent else [])
            for name in stands:
                for e in range(2):
                    sp.dma_start(scratch[name][UNITS + e], scratch[name][0]).then_inc(stand_in, 16)
            for par in range(2):
                sp.sem_inc(m_loaded[par], 48)

            def load(u, q):
                at = ds(u, 1)
                for t in range(NTERM):
                    for name, dst, piece in (("q", A["Q"], Q_TERMS[t]), ("k", A["K"], K_TERMS[t])):
                        sp.dma_start(dst[q][D * t:D * (t + 1), :, :],
                                     scratch[name][at, :, piece, :].rearrange("u (j d) n -> (u d) j n", d=D)).then_inc(loaded[q], 16)
                    if latent:
                        r0 = R_ROW + 4 * t
                        sp.dma_start(A["Q"][q][r0:r0 + 4, :, :],
                                     scratch["qr"][at, :, Q_TERMS[t], :].rearrange("u (j d) n -> (u d) j n", d=4)).then_inc(loaded[q], 16)
                        one = scratch["kr"][at, :, K_TERMS[t], :].rearrange("u d n -> (u d) n")
                        sp.dma_start(A["K"][q][r0:r0 + 4, :, :], one.unsqueeze(1).broadcast_to([4, HG, S])).then_inc(loaded[q], 16)

            def move_maxima(q, index):
                sp.wait_ge(row_read, index + 3)
                for c in range(3):
                    sp.dma_start(A["Q"][q][M_ROW + c:M_ROW + c + 1, :, :],
                                 mT[HG * KT * c:HG * KT * (c + 1), q % 2, :]).then_inc(m_loaded[q % 2], 16)

            load(0, 0)
            load(1, 1)
            sp.wait_ge(stand_in, 32 * len(stands))
            if needs_max:
                move_maxima(0, MAX_PRO)

            def body(u, q, i, general):
                if q == 0:
                    sp.wait_ge(pv_done, NS * u + 1)
                else:
                    sp.wait_ge(pv_done, RING_P + NS * (RING_Q * i + q - 1))
                load(u + 2, (q + 2) % RING_Q)
                if floor and general:
                    sp.wait_ge(low_ready, u + 2)
                    sp.dma_start(scratch["low"][q % 2].rearrange("j t p -> p j t"), lowest[:, q % 2],
                                 allow_slow_non_contiguous=True).then_inc(low_stored, 16)
                    sp.wait_ge(low_stored, 16 * u + 16)
                    sp.nop(nofuse=True)
                    sp.wait_ge(clip_done, CLIP0 + NS * u)
                    sp.dma_start(floors[:, :, :].rearrange("p j n -> p (j n)"),
                                 scratch["low"][q % 2].rearrange("j t p -> (j t p)").partition_broadcast(P)).then_inc(floors_loaded, 16)
                if needs_max:
                    move_maxima((q + 1) % RING_Q, PRO + USES * u + MAX_USE)
            over_units(sp, body)
            for q in range(RING_Q):
                sp.wait_ge(loaded[q], 16 * NLOAD * (UNITS // RING_Q + (q < 2)))
            if needs_max:
                for par in range(2):
                    sp.wait_ge(m_loaded[par], 48 * (1 + UNITS // 2 + (par == 0)))

        @block.gpsimd
        def _(pool):
            def load_v(u, par):
                nc.gpsimd.tensor_copy(A["V"][par][:, :, :, 0:D],
                                      A["VR"][:, ds(u, 1), :, :].rearrange("p u t (j d) -> p (u t) j d", d=D)).then_inc(v_loaded, 1)

            def body(u, q, i, general):
                nd = 0
                for s, (qb, kt, q0, diagonal) in enumerate(steps):
                    if s == LAG + 1:
                        pool.wait_ge(pv_done, RING_P + NS * u + 1)
                        load_v(u + 1, (q + 1) % 2)
                    if diagonal:
                        if general:
                            pool.wait_ge(clip_done, CLIP0 + NS * u + s + 1)
                        else:
                            pool.wait_ge(exp_done, EXP0 + 2 * (NS * u + s) + 2)
                        pool.nop(nofuse=True)
                        on = prob[:, s % RING_P, :, q0:q0 + P]
                        nc.gpsimd.affine_select(out=on, in_=on, compare_op=ALU.is_ge, fill=0.0, base=0,
                                                pattern=[[0, HG], [1, P]], channel_multiplier=-1).then_inc(tri_done, 1)
            if causal:
                pool.sem_inc(tri_done, TRI0)
            for t in range(LAG):
                nc.gpsimd.memset(prob[:, RING_P - 1 - t], 1.0).then_inc(stand_in_prob, 1)
            load_v(0, 0)
            over_units(pool, body)

        @block.tensor
        def _(pe):
            pe.sem_inc(pv_done, RING_P - LAG)

            def rows_of(slot, ring, b):
                j, qt, half, width, diagonal = b
                mm = pe.matmul(slot[:, 0:width], A["Q"][ring][0:M_ROW, j, qt * P:(qt + 1) * P],
                               A["K"][ring][0:M_ROW, j, half * BW:half * BW + width], start=True, stop=not diagonal)
                if diagonal:
                    mm = pe.matmul(slot[:, width - P:width], C["ident16"][:, :], C["mask16"][:, :], start=False, stop=True)
                return mm

            def maxima_of(slot, v):
                pe.wait_ge(m_split, v + 1)
                return pe.transpose(slot[0:3 * HG * KT, 0:P // 2].bitcast(BF16),
                                    mpieces[:, :, :, :].rearrange("p c j t -> p (c j t)"), C["ident16"][:, :])

            def output_of(slot, u, qb):
                pe.wait_ge(acc_copied, 2 * u + qb + 3)
                for t in range(TB):
                    mm = pe.transpose(slot[:, t * P:(t + 1) * P], accS[:, qb % 2, t * P:(t + 1) * P], C["ident"][:, :])
                return mm

            def through_v(u, q, t, general):
                ring, s = (q - (t < 0)) % 2, t % NS
                qb, kt, q0, diagonal = steps[s]
                if t == 0:
                    pe.wait_ge(v_loaded, u + 1)
                if kt == 0:
                    pe.wait_ge(acc_copied, 2 * u + qb + 1)
                if diagonal:
                    before_it = sum(x[3] for x in steps[:s]) - (NDIAG if t < 0 else 0)
                    pe.wait_ge(tri_done, NDIAG * u + before_it + TRI0 + 1)
                elif general:
                    pe.wait_ge(clip_done, NS * u + t + CLIP0 + 1)
                else:
                    pe.wait_ge(exp_done, 2 * (NS * u + t) + EXP0 + 2)
                last = s + 1 == NS or steps[s + 1][0] != qb
                for j in range(HG):
                    mm = pe.matmul(acc[qb][VW * j:VW * (j + 1), q0:BW], A["V"][ring][:, kt, j, :],
                                   prob[:, s % RING_P, j, q0:BW], start=kt == 0, stop=last)
                mm.then_inc(pv_done, 1)

            pe.wait_ge(stand_in_prob, LAG)
            for j in range(HG):
                pe.matmul(acc[1][VW * j:VW * (j + 1), :], A["V"][1][:, 0, j, :], prob[:, RING_P - 1, j, :], start=True, stop=False)

            if needs_max:
                pe.wait_ge(loaded[0], 16 * NLOAD)
                pe.wait_ge(loaded[1], 16 * NLOAD)
                for k, (kind, b) in enumerate(x for x in before if x[0] != "split"):
                    pe.wait_ge(row_read, k + 1)
                    mm = rows_of(row[k % 2], b[0], b[1]) if kind == "rows" else maxima_of(row[k % 2], 0)
                    mm.then_inc(row_full, 1)

            def body(u, q, i, general):
                if needs_max:
                    pe.wait_ge(m_loaded[q % 2], 48 * (2 * i + q // 2 + 2))
                else:
                    pe.wait_ge(loaded[q], 16 * NLOAD * (i + 1))
                k = 0
                for s, (qb, kt, q0, diagonal) in enumerate(steps):
                    for part in range(3):
                        if part < 2:
                            pe.wait_ge(exp_done, 2 * (NS * u + s - 1) + EXP0 + part + 1)
                            for j in (2 * part, 2 * part + 1):
                                mm = pe.matmul(st[part][:, j % 2, q0:BW], A["K"][q][:, j, kt * P:(kt + 1) * P],
                                               A["Q"][q][:, j, qb * BW + q0:(qb + 1) * BW], start=True, stop=True)
                            mm.then_inc(st_full, 1)
                        else:
                            through_v(u, q, s - LAG, general)
                        for kind, b in beside[s][part]:
                            if kind == "split":
                                continue
                            pe.wait_ge(row_read, PRO + USES * u + k + 1)
                            slot = row[(PRO + USES * q + k) % 2]
                            if kind == "rows":
                                if b[0] == 2 and b[1] == rows[0]:
                                    pe.wait_ge(loaded[(q + 2) % RING_Q], 16 * NLOAD * (i + 1 + (q + 2) // RING_Q))
                                rows_of(slot, (q + b[0]) % RING_Q, b[1]).then_inc(row_full, 1)
                            elif kind == "maxima":
                                maxima_of(slot, u + 1).then_inc(row_full, 1)
                            else:
                                output_of(slot, u, b).then_inc(row_full, 1)
                            k += 1

            over_units(pe, body)
            for t in range(-LAG, 0):
                through_v(UNITS, 0, t, False)
            pe.wait_ge(row_read, PRO + USES * UNITS + 1)
            output_of(row[PRO % 2], UNITS, -1).then_inc(row_full, 1)

        @block.scalar
        def _(act):
            act.sem_inc(exp_done, EXP0)
            act.sem_inc(acc_copied, 1)

            def copy_output(u, block_done, v_count):
                act.wait_ge(pv_done, v_count)
                act.wait_ge(acc_turned, 2 * u + (1 if block_done == 1 else 2))
                nc.scalar.activation(accS[:, block_done, :], acc[block_done][:, :], ACT.Copy).then_inc(acc_copied, 1)

            def body(u, q, i, general):
                if floor:
                    act.wait_ge(m_split, u + 1)
                    nc.scalar.activation(lowest[:, q % 2], rowmax[:, q % 2], ACT.Exp, bias=A["clip_bias"][:, 0:1], scale=-scale).then_inc(low_ready, 1)
                for s, (qb, kt, q0, diagonal) in enumerate(steps):
                    act.wait_ge(pv_done, NS * u + s + 1)
                    for pair in range(2):
                        act.wait_ge(st_full, 2 * (NS * u + s) + pair + 1)
                        nc.scalar.activation(prob[:, s % RING_P, 2 * pair:2 * pair + 2, q0:BW], st[pair][:, :, q0:BW],
                                             ACT.Exp, scale=scale).then_inc(exp_done, 1)
                    if s == LAG:
                        copy_output(u, 1, RING_P + NS * u)
                    if s == first_half + LAG + 1:
                        copy_output(u, 0, RING_P + NS * u + first_half + 1)
            with act.Fori(0, UNITS // RING_Q) as i:
                for q in range(RING_Q):
                    body(RING_Q * i + q, q, i, False)
            copy_output(UNITS, 1, RING_P + NS * UNITS)

        @block.vector
        def _(dve):
            dve.sem_inc(row_read, 2)
            dve.sem_inc(clip_done, CLIP0)
            dve.sem_inc(acc_turned, 2)
            if floor:
                nc.vector.memset(lowest[:, :, :, :], 0.0).then_inc(low_ready, 1)

            def read_rows(slot, ring, b):
                j, qt, half, width, diagonal = b
                return nc.vector.tensor_reduce(halfmax[:, ring % 2, j, qt, half:half + 1], slot[:, 0:width], AX_X, ALU.max)

            def split_maxima(index, ring, chain):
                m, halves = rowmax[:, ring % 2], halfmax[:, ring % 2]
                dve.wait_ge(row_read, index + 2)
                if causal:
                    nc.vector.tensor_copy(m[:, :, 0:TB], halves[:, :, 0:TB, 0])
                    chain.link(nc.vector.tensor_tensor(m[:, :, TB:KT], halves[:, :, TB:KT, 0], halves[:, :, TB:KT, 1], ALU.max))
                else:
                    chain.link(nc.vector.tensor_tensor(m[:, :, :], halves[:, :, :, 0], halves[:, :, :, 1], ALU.max))
                if floor:
                    limit = L["clip"] / scale
                    chain.link(nc.vector.tensor_scalar(m[:, :, :], m[:, :, :], limit, -limit, ALU.min, ALU.max))
                chain.link(nc.vector.tensor_scalar(left[:, 0], m[:, :, :], -1.0, None, ALU.mult))
                chain.link(nc.vector.tensor_copy(mpieces[:, 0], left[:, 0]))
                chain.link(nc.vector.tensor_tensor(left[:, 1], left[:, 0], mpieces[:, 0], ALU.subtract))
                chain.link(nc.vector.tensor_copy(mpieces[:, 1], left[:, 1]))
                nc.vector.tensor_tensor(mpieces[:, 2], left[:, 1], mpieces[:, 1], ALU.subtract).then_inc(m_split, 1)

            def take_maxima(slot, ring, v):
                dve.wait_ge(m_loaded[ring % 2], v)
                return nc.vector.tensor_copy(mT[:, ring % 2, :], slot[0:3 * HG * KT, 0:P // 2].bitcast(BF16))

            def take_output(slot, u, q, qb, chain):
                view = slot[:, :].rearrange("p (t j r) -> p t j r", t=TB, r=VW)
                at = ds(u + 1 + (-1 if qb < 0 else 0), 1)
                tiles = slice((qb % 2) * TB, (qb % 2 + 1) * TB)
                out = A["AO"][:, at, tiles, :].rearrange("p u t (j d) -> p (u t) j d", d=D)
                if floor:
                    wide = lambda x: x.unsqueeze(3).broadcast_to([P, TB, HG, D])
                    dve.wait_ge(low_ready, u + (1 if qb < 0 else 2))
                    low = lowest[:, (q + (qb < 0)) % 2, :, tiles].rearrange("p j t -> p t j")
                    masked = A["masked"][:, tiles].unsqueeze(2).broadcast_to([P, TB, HG])
                    suffix = A["SUF"][:, at, tiles, :].rearrange("p u t (j d) -> p (u t) j d", d=D)
                    every = A["SUM"][:, at, :].rearrange("p u (j d) -> p u j d", d=D).broadcast_to([P, TB, HG, D])
                    chain.link(nc.vector.tensor_tensor(mass[:, :, :], low, masked, ALU.mult))
                    chain.link(nc.vector.tensor_tensor(mass[:, :, :], mass[:, :, :], view[:, :, :, D], ALU.add))
                    chain.link(nc.vector.tensor_scalar(share[:, :, :], mass[:, :, :], 1e-6, 1e-8, ALU.add, ALU.mult))
                    chain.link(nc.vector.scalar_tensor_tensor(whole[:, :, :], share[:, :, :], float(S), mass[:, :, :], ALU.mult, ALU.add))
                    chain.step(nc.vector.reciprocal(rsum[:, :, :], whole[:, :, :]))
                    chain.link(nc.vector.tensor_tensor(tail[:, :, :, :], wide(low), suffix, ALU.mult))
                    chain.link(nc.vector.tensor_tensor(num[:, :, :, :], tail[:, :, :, :], view[:, :, :, 0:D], ALU.add))
                    chain.link(nc.vector.tensor_tensor(tail[:, :, :, :], wide(share[:, :, :]), every, ALU.mult))
                    chain.link(nc.vector.tensor_tensor(num[:, :, :, :], num[:, :, :, :], tail[:, :, :, :], ALU.add))
                    return nc.vector.tensor_tensor(out, num[:, :, :, :], wide(rsum[:, :, :]), ALU.mult)
                chain.link(nc.vector.reciprocal(rsum[:, :, :], view[:, :, :, D]))
                return nc.vector.tensor_tensor(out, view[:, :, :, 0:D], rsum[:, :, :].unsqueeze(3).broadcast_to([P, TB, HG, D]), ALU.mult)

            pre = Chain(dve, dve_chain, 0)
            k = 0
            for kind, b in before:
                if kind == "split":
                    split_maxima(k, 0, pre)
                    continue
                dve.wait_ge(row_full, k + 1)
                ins = read_rows(row[k % 2], b[0], b[1]) if kind == "rows" else take_maxima(row[k % 2], 0, 48)
                ins.then_inc(row_read, 1)
                k += 1
            LINKS = 2 * (9 if floor else 1) + ((6 if floor else 5) if needs_max else 0)

            def body(u, q, i, general):
                chain = Chain(dve, dve_chain, pre.n + LINKS * u)
                k = 0
                for s, (qb, kt, q0, diagonal) in enumerate(steps):
                    for kind, b in beside[s][0] + beside[s][1] + beside[s][2]:
                        slot = row[(PRO + USES * q + k) % 2]
                        index = PRO + USES * u + k
                        if kind == "split":
                            split_maxima(index, q + 1, chain)
                            continue
                        dve.wait_ge(row_full, index + 1)
                        if kind == "rows":
                            read_rows(slot, q + b[0], b[1]).then_inc(row_read, 1)
                        elif kind == "maxima":
                            take_maxima(slot, q + 1, 48 * (2 * i + (q + 1) // 2 + 1)).then_inc(row_read, 1)
                        else:
                            dve.sem_inc(acc_turned, 1)
                            take_output(slot, u, q, b, chain).then_inc(row_read, 1)
                        k += 1
                    if general:
                        dve.wait_ge(exp_done, 2 * (NS * u + s) + EXP0 + 2)
                        on = prob[:, s % RING_P, :, q0:BW]
                        if floor:
                            dve.wait_ge(floors_loaded, 16 * u + 16)
                            ins = nc.vector.scalar_tensor_tensor(on, on, 1.0, floors[:, :, qb * BW + q0:(qb + 1) * BW], ALU.min, ALU.max)
                        else:
                            ins = nc.vector.tensor_scalar(on, on, L["most"], L["least"], ALU.min, ALU.max)
                        ins.then_inc(clip_done, 1)
                assert chain.n == LINKS, (chain.n, LINKS)
            over_units(dve, body)
            dve.wait_ge(row_full, PRO + USES * UNITS + 1)
            take_output(row[PRO % 2], UNITS, 0, -1, Chain(dve, dve_chain, pre.n + LINKS * UNITS)).then_inc(row_read, 1)


def attention_finish(nc, L, C, X, A, w):
    nm = L["name"]
    with ExitStack() as ctx:
        sb = lambda name, shape, dt=F32: ctx.enter_context(nc.sbuf_tensor(nm + name, shape, dt))
        sem = semaphores(nc, ctx, nm + "finish_")
        psT = [ctx.enter_context(nc.psum_tensor(nm + f"psA{i}", [P, BW], F32)) for i in range(2)]
        psY = [ctx.enter_context(nc.psum_tensor(nm + f"psY{i}", [P, BW], F32)) for i in range(2)]
        ao = sb("ao", [P, 2, TB, P])
        aoT = sb("aoT", [P, 2, BW])
        y = sb("y", [P, 2, BW])
        gathered, turned, aoT_ready = sem("gathered"), sem("turned"), sem("aoT_ready")
        y_in_psum, y_read, y_biased = sem("y_in_psum"), sem("y_read"), sem("y_biased")
        block = ctx.enter_context(nc.Block())

        @block.gpsimd
        def _(pool):
            pool_first = 2
            with pool.Fori(0, NB // 2) as i:
                for p in range(2):
                    n = 2 * i + p
                    pool.wait_ge(turned, n + 1)
                    nc.gpsimd.tensor_copy(ao[:, p].rearrange("p t (g r) -> p g t r", r=32),
                                          A["AO"][:, ds(i * G + 1, G), p * TB:(p + 1) * TB, :]).then_inc(gathered, 1)

        @block.tensor
        def _(pe):
            pe.sem_inc(turned, 2)
            with pe.Fori(0, NB // 2) as i:
                for p in range(2):
                    n = 2 * i + p
                    pe.wait_ge(gathered, n + 1)
                    pe.wait_ge(aoT_ready, n + 1)
                    for t in range(TB):
                        mm = pe.transpose(psT[p][:, t * P:(t + 1) * P], ao[:, p, t, :], C["ident"][:, :])
                    mm.then_inc(turned, 1)
                    pe.wait_ge(aoT_ready, n + 3)
                    pe.wait_ge(y_read, n + 1)
                    for t in range(TB):
                        mm = pe.matmul(psY[p][:, t * P:(t + 1) * P], aoT[:, p, t * P:(t + 1) * P], w["o"][:, :], start=True, stop=True)
                    mm.then_inc(y_in_psum, 1)

        @block.scalar
        def _(act):
            act.sem_inc(aoT_ready, 2)
            with act.Fori(0, NB // 2) as i:
                for p in range(2):
                    n = 2 * i + p
                    act.wait_ge(turned, n + 3)
                    act.wait_ge(y_read, n + 1)
                    nc.scalar.activation(aoT[:, p, :], psT[p][:, :], ACT.Copy).then_inc(aoT_ready, 1)

        @block.vector
        def _(dve):
            dve.sem_inc(y_read, 2)
            with dve.Fori(0, NB // 2) as i:
                for p in range(2):
                    n = 2 * i + p
                    dve.wait_ge(y_in_psum, n + 1)
                    x = X[:, ds(n * TB, TB), :]
                    ps = psY[p][:, :].rearrange("p (t e) -> p t e", t=TB)
                    if w["bo"] is None:
                        nc.vector.tensor_tensor(x, ps, x, ALU.add).then_inc(y_read, 1)
                    else:
                        nc.vector.tensor_tensor(y[:, p].rearrange("p (t e) -> p t e", t=TB), ps,
                                                w["bo"][:, :].unsqueeze(1).broadcast_to([P, TB, P]), ALU.add).then_inc(y_read, 1)
                        dve.wait_ge(y_read, n + 3)
                        nc.vector.tensor_tensor(x, y[:, p].rearrange("p (t e) -> p t e", t=TB), x, ALU.add).then_inc(y_biased, 1)


def attention(nc, L, C, X, weights, scratch, d):
    nm = L["name"]
    with ExitStack() as ctx:
        sb = lambda name, shape, dt=F32: ctx.enter_context(nc.sbuf_tensor(nm + name, shape, dt))
        A = {
            "Q": [sb(f"Q{b}", [P, HG, S], BF16) for b in range(RING_Q)],
            "K": [sb(f"K{b}", [P, HG, S], BF16) for b in range(RING_Q)],
            "V": [sb(f"V{b}", [P, KT, HG, VW]) for b in range(2)],
            "VR": sb("VR", [P, UNITS + 1, KT, HG * D]),
            "AO": sb("AO", [P, UNITS + 1, KT, HG * D]),
        }
        w = {"loads": [], "bo": None}
        for name, (src, first, shape) in weights.items():
            t = sb("w" + name, [first + shape[0], shape[1]])
            w[name] = t
            w["loads"].append((t[first:first + shape[0], :], src))
        if L["tables"]:
            rows = d[L["tables"]].shape[0]
            C = dict(C)
            C[L["tables"]] = sb("table", [rows, 2, S])
            w["loads"].append((C[L["tables"]][:, :, :], d[L["tables"]]))
        if L["floor"]:
            A.update({"SUF": sb("SUF", [P, UNITS + 1, KT, 32]), "SUM": sb("SUM", [P, UNITS + 1, 32]), "masked": sb("masked", [P, KT]),
                      "peak": sb("peak", [H, 2, NB]), "clip_bias": sb("clip_bias", [P, 1]), "may_clip": sb("may_clip", [1, 1], I32)})
        attention_prepare(nc, L, C, X, A, w, scratch)
        if L["floor"]:
            masked_sums(nc, L, C, A, d)
        attention_core(nc, L, C, A, scratch)
        attention_finish(nc, L, C, X, A, w)



FFN = {
    "f0": dict(gated=15, experts=16, chunks=1, act=ACT.Relu, top=3, ring=8, lag=4),
    "f1": dict(gated=8, experts=9, chunks=4, act=ACT.Gelu_apprx_tanh, chosen=2 * B * S, ring=6, lag=4),
}
GW = 16


def layernorm_all(nc, X, C, dve, act_sem, sd_sem, chain, T):
    stats, mean, sd, rstd, t1, t2 = T
    for t in range(NT):
        ins = nc.vector.bn_stats(stats[:, t, :], X[:, t, :])
    chain.link(ins)
    chain.link(nc.vector.tensor_tensor(t1[:, :], stats[:, :, 1], stats[:, :, 4], ALU.add))
    chain.step(nc.vector.tensor_scalar(mean[:, :], t1[:, :], 0.5, None, ALU.mult))
    chain.link(nc.vector.tensor_tensor(t2[:, :], stats[:, :, 1], stats[:, :, 4], ALU.subtract))
    chain.link(nc.vector.tensor_tensor(t2[:, :], t2[:, :], t2[:, :], ALU.mult))
    chain.link(nc.vector.tensor_tensor(t1[:, :], stats[:, :, 2], stats[:, :, 5], ALU.add))
    chain.link(nc.vector.tensor_scalar(t1[:, :], t1[:, :], 1.0 / E, None, ALU.mult))
    nc.vector.scalar_tensor_tensor(t1[:, :], t2[:, :], 0.25, t1[:, :], ALU.mult, ALU.add).then_inc(act_sem, 1)
    dve.wait_ge(sd_sem, 1)
    chain.link(nc.vector.reciprocal(rstd[:, :], sd[:, :]))


def route(nc, nm, F, C, X, R, w):
    ne, top = F["gated"], F.get("top")
    LW = 24 if top else ne
    NCOL = ne * NT
    with ExitStack() as ctx:
        sb = lambda name, shape, dt=F32: ctx.enter_context(nc.sbuf_tensor(nm + name, shape, dt))
        sem = semaphores(nc, ctx, nm + "route_")
        bank = lambda name: ctx.enter_context(nc.psum_tensor(nm + name, [P, BW], F32))
        T = [sb("stats", [P, NT, 6])] + [sb(n, [P, NT]) for n in ("mean", "sd", "rstd", "t1", "t2")]
        stats, mean, sd, rstd, t1, t2 = T
        xn, xs = sb("xn", [P, 2, TB, P]), sb("xs", [P, 2, BW])
        logits, ex = sb("logits", [P, NT, LW]), sb("ex", [P, NT, ne])
        gate, pieces = sb("gate", [P, NT, GW]), sb("pieces", [P, NT, P], BF16)
        most, total, inv = sb("most", [P, NT]), sb("total", [P, NT]), sb("inv", [P, NT])
        if top:
            best, wanted, marked = sb("best", [P, NT, 8]), sb("wanted", [P, NT, 8]), sb("marked", [P, NT, LW])
        else:
            score = sb("score", [P, ne, NT])
            over, same, pick = sb("over", [P, NCOL]), sb("same", [P, NCOL]), sb("picked", [P, NCOL])
            run = [sb("run0", [P, NCOL]), sb("run1", [P, NCOL])]
            ones, above = sb("ones", [P, P]), sb("above", [P, P])
            limit, trial, grow, stepi = [sb(n, [P, 1], I32) for n in ("limit", "trial", "grow", "stepi")]
            stepf, count, room = [sb(n, [P, 1]) for n in ("stepf", "count", "room")]
        psT, psR, psG = [bank("psT0"), bank("psT1")], [bank("psR0"), bank("psR1")], [bank("psG0"), bank("psG1")]
        psN = bank("psN")
        rest = sb("rest", [P, 2, NT, GW])
        w_ready, var_ready, sd_ready = sem("w_ready"), sem("var_ready"), sem("sd_ready")
        xn_ready, xT_in_psum, xs_ready, XT_ready = sem("xn_ready"), sem("xT_in_psum"), sem("xs_ready"), sem("XT_ready")
        XT_high, w_high, w_low, staged = sem("XT_high"), sem("w_high"), sem("w_low"), sem("staged")
        stage = sb("stage", [P, F["experts"] * F["chunks"] * P])
        lg_in_psum, lg_ready = sem("lg_in_psum"), sem("lg_ready")
        b2_ready = sem("b2_ready")
        dif_ready, ex_ready, preset = sem("dif_ready"), sem("ex_ready"), sem("preset")
        counted, summed = sem("counted"), sem("summed")
        pieces_ready, gt_in_psum, gt_ready = sem("pieces_ready"), sem("gt_in_psum"), sem("gt_ready")
        same_ready, ranked = sem("same_ready"), sem("ranked")
        chain_sem, loop_sem = sem("chain"), sem("loop")
        BITS = 30
        block = ctx.enter_context(nc.Block())

        @block.sync
        def _(sp):
            for dst, src in w["loads"]:
                sp.dma_start(dst, src).then_inc(w_ready, 16)
            sp.dma_start(stage[:, :], w["W1"]).then_inc(staged, 16)
            sp.wait_ge(w_low, 1)
            sp.dma_start(stage[:, :], w["W2"]).then_inc(staged, 16)
            sp.wait_ge(staged, 32)

        @block.gpsimd
        def _(pool):
            nc.gpsimd.memset(pieces[:, :, :].bitcast(I32), 0)
            nc.gpsimd.memset(w["b2r"][:, :], 0.0)
            nc.gpsimd.memset(gate[:, :, :], 0.0).then_inc(preset, 1)
            pool.wait_ge(preset, 1)
            ins = nc.gpsimd.memset(gate[:, :, ne:ne + 1], 1.0)
            if top:
                for c in range(ne, LW):
                    nc.gpsimd.memset(logits[:, :, c:c + 1], NEG * c)
                for c in range(top, 8):
                    ins = nc.gpsimd.memset(wanted[:, :, c:c + 1], NEG * (ne + c - top))
            ins.then_inc(preset, 1)
            pool.wait_ge(preset, 2)
            for c in range(3):
                pool.dma_start(w["b2r"][GW * c:GW * c + F["experts"], :], w["b2"]).then_inc(b2_ready, 16)
            def rest_of_weights(k, name):
                pool.wait_ge(w_high, k + 1)
                nc.gpsimd.tensor_tensor(w[name + "l"], stage[:, :], w[name + "h"].bitcast(F32), ALU.subtract).then_inc(w_low, 1)

            rest_of_weights(0, "W1")
            pool.sem_inc(XT_ready, 2)
            with pool.Fori(0, NB // 2) as i:
                for p in range(2):
                    n = 2 * i + p
                    pool.wait_ge(XT_high, n + 1)
                    nc.gpsimd.tensor_tensor(R["XTl"][:, ds(n * BW, BW)], xs[:, p, :], R["XTh"][:, ds(n * BW, BW)].bitcast(F32), ALU.subtract).then_inc(XT_ready, 1)
            rest_of_weights(1, "W2")

        @block.tensor
        def _(pe):
            pe.wait_ge(w_ready, 16 * len(w["loads"]))
            with pe.Fori(0, NB // 2) as i:
                for p in range(2):
                    n = 2 * i + p
                    pe.wait_ge(xn_ready, n + 1)
                    pe.wait_ge(xs_ready, n + 1)
                    for t in range(TB):
                        mm = pe.transpose(psT[p][:, t * P:(t + 1) * P], xn[:, p, t, :], C["ident"][:, :])
                    mm.then_inc(xT_in_psum, 1)
                    pe.wait_ge(xs_ready, n + 3)
                    pe.wait_ge(lg_ready, n + 1)
                    for t in range(TB):
                        mm = pe.matmul(psR[p][:, t * GW:t * GW + ne], xs[:, p, t * P:(t + 1) * P], w["router"][:, :], start=True, stop=True)
                    mm.then_inc(lg_in_psum, 1)
            if not top:
                with pe.Fori(0, BITS) as i:
                    pe.wait_ge(counted, i + 1)
                    pe.matmul(psN[:, 0:1], ones[:, :], count[:, :], start=True, stop=True).then_inc(summed, 1)
                pe.wait_ge(counted, BITS + 1)
                pe.matmul(psN[:, 0:1], ones[:, :], count[:, :], start=True, stop=True).then_inc(summed, 1)
                pe.wait_ge(same_ready, 1)
                pe.matmul(psR[0][:, 0:NCOL], above[:, :], same[:, :], start=True, stop=True).then_inc(ranked, 1)
                pe.matmul(psR[1][:, 0:NCOL], ones[:, :], same[:, :], start=True, stop=True).then_inc(ranked, 1)
            pe.wait_ge(pieces_ready, 1)
            for n in range(NB):
                if n >= 2:
                    pe.wait_ge(gt_ready, n - 1)
                for t in range(TB):
                    mm = pe.transpose(psG[n % 2][:, t * P // 2:(t + 1) * P // 2].bitcast(BF16), pieces[:, n * TB + t, :], C["ident16"][:, :])
                mm.then_inc(gt_in_psum, 1)

        @block.scalar
        def _(act):
            act.wait_ge(var_ready, 1)
            nc.scalar.activation(sd[:, :], t1[:, :], ACT.Sqrt, bias=C["eps"][:, 0:1]).then_inc(sd_ready, 1)
            act.wait_ge(dif_ready, 1)
            nc.scalar.activation(ex[:, :, :], ex[:, :, :], ACT.Exp).then_inc(ex_ready, 1)
            for n in range(NB):
                act.wait_ge(gt_in_psum, n + 1)
                nc.scalar.activation(R["GT"][:, n * BW:(n + 1) * BW], psG[n % 2][:, 0:BW // 2].bitcast(BF16), ACT.Copy).then_inc(gt_ready, 1)

        @block.vector
        def _(dve):
            chain = Chain(dve, chain_sem)
            dve.sem_inc(xs_ready, 2)
            dve.sem_inc(lg_ready, 2)
            layernorm_all(nc, X, C, dve, var_ready, sd_ready, chain, T)
            dve.wait_ge(w_ready, 16 * len(w["loads"]))
            dve.wait_ge(staged, 16)
            nc.vector.tensor_copy(w["W1h"], stage[:, :]).then_inc(w_high, 1)
            dve.wait_ge(preset, 2)
            dve.wait_ge(b2_ready, 48)
            with dve.Fori(0, NB // 2) as i:
                for p in range(2):
                    n = 2 * i + p
                    dve.wait_ge(xs_ready, n + 1)
                    for t in range(TB):
                        ins = nc.vector.tensor_scalar(xn[:, p, t, :], X[:, ds(n * TB + t, 1), :].rearrange("p a e -> p (a e)"),
                                                      mean[:, ds(n * TB + t, 1)], rstd[:, ds(n * TB + t, 1)], ALU.subtract, ALU.mult)
                    ins.then_inc(xn_ready, 1)
                    dve.wait_ge(xT_in_psum, n + 1)
                    dve.wait_ge(XT_ready, n + 1)
                    nc.vector.tensor_copy(xs[:, p, :], psT[p][:, :]).then_inc(xs_ready, 1)
                    dve.wait_ge(lg_in_psum, n + 1)
                    dve.wait_ge(xs_ready, n + 3)
                    nc.vector.tensor_copy(R["XTh"][:, ds(n * BW, BW)], xs[:, p, :]).then_inc(XT_high, 1)
                    lg = psR[p][:, 0:TB * GW].rearrange("p (t e) -> p t e", t=TB)[:, :, 0:ne]
                    dst = logits[:, ds(n * TB, TB), 0:ne]
                    if top:
                        nc.vector.tensor_tensor(dst, lg, w["br"][:, :].unsqueeze(1).broadcast_to([P, TB, ne]), ALU.add).then_inc(lg_ready, 1)
                    else:
                        nc.vector.tensor_scalar(dst, lg, 1.0, None, ALU.mult).then_inc(lg_ready, 1)
            dve.wait_ge(staged, 32)
            nc.vector.tensor_copy(w["W2h"], stage[:, :]).then_inc(w_high, 1)
            dve.wait_ge(lg_ready, NB + 2)
            wide = lambda x, k: x.unsqueeze(2).broadcast_to([P, NT, k])
            chain.link(nc.vector.tensor_reduce(most[:, :], logits[:, :, 0:ne], AX_X, ALU.max))
            nc.vector.tensor_tensor(ex[:, :, :], logits[:, :, 0:ne], wide(most[:, :], ne), ALU.subtract).then_inc(dif_ready, 1)
            if top:
                for t in range(NT):
                    ins = nc.vector.max(best[:, t, :], logits[:, t, :])
                chain.link(ins)
                chain.link(nc.vector.tensor_copy(wanted[:, :, 0:top], best[:, :, 0:top]))
                for t in range(NT):
                    ins = nc.vector.match_replace(marked[:, t, :], wanted[:, t, :], logits[:, t, :], -NEG)
                chain.link(ins)
            dve.wait_ge(ex_ready, 1)
            chain.link(nc.vector.tensor_reduce(total[:, :], ex[:, :, :], AX_X, ALU.add))
            chain.link(nc.vector.reciprocal(inv[:, :], total[:, :]))
            if top:
                chain.link(nc.vector.tensor_tensor(ex[:, :, :], ex[:, :, :], wide(inv[:, :], ne), ALU.mult))
                chain.link(nc.vector.scalar_tensor_tensor(gate[:, :, 0:ne], marked[:, :, 0:ne], -NEG, ex[:, :, :], ALU.is_ge, ALU.mult))
            else:
                chain.link(nc.vector.tensor_tensor(score[:, :, :].rearrange("p e t -> p t e"), ex[:, :, :], wide(inv[:, :], ne), ALU.mult))
                flat = score[:, :, :].rearrange("p e t -> p (e t)")
                chain.step(nc.vector.memset(ones[:, :], 1.0))
                chain.step(nc.vector.tensor_scalar(above[:, :], C["mask"][:, :], -1.0, None, ALU.is_lt))
                chain.step(nc.vector.memset(stepf[:, :], float(2 ** (BITS - 1))))
                chain.link(nc.vector.memset(limit[:, :], 0))
                LINKS = 5
                with dve.Fori(0, BITS) as i:
                    inner = Chain(dve, loop_sem, LINKS * i)
                    inner.link(nc.vector.tensor_copy(stepi[:, :], stepf[:, :]))
                    inner.link(nc.vector.tensor_tensor(trial[:, :], limit[:, :], stepi[:, :], ALU.bitwise_or))
                    nc.vector.tensor_scalar(over[:, :], flat, trial[:, :].bitcast(F32), 0.0, ALU.is_ge, ALU.add,
                                            accum_out=count[:, :]).then_inc(counted, 1)
                    dve.wait_ge(summed, i + 1)
                    inner.link(nc.vector.tensor_scalar(grow[:, :], psN[:, 0:1], float(F["chosen"]), stepf[:, :], ALU.is_ge, ALU.mult))
                    inner.link(nc.vector.tensor_tensor(limit[:, :], limit[:, :], grow[:, :], ALU.bitwise_or))
                    inner.link(nc.vector.tensor_scalar(stepf[:, :], stepf[:, :], 0.5, None, ALU.mult))
                    assert inner.n == LINKS
                at = limit[:, :].bitcast(F32)
                nc.vector.tensor_scalar(over[:, :], flat, at, 0.0, ALU.is_gt, ALU.add, accum_out=count[:, :]).then_inc(counted, 1)
                nc.vector.tensor_scalar(same[:, :], flat, at, None, ALU.is_equal).then_inc(same_ready, 1)
                dve.wait_ge(summed, BITS + 1)
                chain.link(nc.vector.tensor_scalar(room[:, :], psN[:, 0:1], -1.0, float(F["chosen"]), ALU.mult, ALU.add))
                dve.wait_ge(ranked, 2)
                chain.link(nc.vector.tensor_copy(run[0][:, :], psR[1][:, 0:NCOL]))
                width, a = 1, 0
                while width < NCOL:
                    chain.step(nc.vector.tensor_copy(run[1 - a][:, 0:width], run[a][:, 0:width]))
                    chain.link(nc.vector.tensor_tensor(run[1 - a][:, width:], run[a][:, width:], run[a][:, 0:NCOL - width], ALU.add))
                    width, a = 2 * width, 1 - a
                chain.link(nc.vector.tensor_tensor(pick[:, :], run[a][:, :], psR[1][:, 0:NCOL], ALU.subtract))
                chain.link(nc.vector.tensor_tensor(pick[:, :], pick[:, :], psR[0][:, 0:NCOL], ALU.add))
                chain.link(nc.vector.scalar_tensor_tensor(pick[:, :], pick[:, :], room[:, 0:1], same[:, :], ALU.is_lt, ALU.mult))
                chain.link(nc.vector.tensor_tensor(pick[:, :], pick[:, :], over[:, :], ALU.add))
                chain.link(nc.vector.tensor_tensor(gate[:, :, 0:ne], pick[:, :].rearrange("p (e t) -> p t e", e=ne),
                                                   score[:, :, :].rearrange("p e t -> p t e"), ALU.mult))
            cut = lambda c: pieces[:, :, GW * c:GW * (c + 1)]
            chain.link(nc.vector.tensor_copy(cut(0), gate[:, :, :]))
            chain.link(nc.vector.tensor_tensor(rest[:, 0], gate[:, :, :], cut(0), ALU.subtract))
            chain.link(nc.vector.tensor_copy(cut(1), rest[:, 0]))
            nc.vector.tensor_tensor(cut(2), rest[:, 0], cut(1), ALU.subtract).then_inc(pieces_ready, 1)
            b2p, b2f = R["b2p"], w["b2r"]
            chain.link(nc.vector.tensor_copy(b2p[:, 0, :], b2f[:, :]))
            chain.link(nc.vector.tensor_tensor(b2f[:, :], b2f[:, :], b2p[:, 0, :], ALU.subtract))
            chain.link(nc.vector.tensor_copy(b2p[:, 1, :], b2f[:, :]))
            chain.step(nc.vector.tensor_tensor(b2p[:, 2, :], b2f[:, :], b2p[:, 1, :], ALU.subtract))
            chain.step(nc.vector.tensor_copy(R["spread"][:, :, :], w["pick"][:, :].unsqueeze(2).broadcast_to([P, GW, P])))


def experts(nc, nm, F, C, X, R, w):
    chunks, fn, RH = F["chunks"], F["act"], F["ring"]
    pairs = [(e, c) for e in range(F["experts"]) for c in range(chunks)]
    NP, NE, LAG = len(pairs), F["experts"], F["lag"]
    RA = 4
    TURN = LAG + 3
    with ExitStack() as ctx:
        sb = lambda name, shape, dt=F32: ctx.enter_context(nc.sbuf_tensor(nm + name, shape, dt))
        sem = semaphores(nc, ctx, nm + "experts_")
        bank = lambda name: ctx.enter_context(nc.psum_tensor(nm + name, [P, BW], F32))
        psH, psG, psY, psT = [bank("psH0"), bank("psH1")], [bank("psS0"), bank("psS1")], [bank("psY0"), bank("psY1")], bank("psX")
        h, hs, yS = sb("h", [P, RA, BW]), sb("hs", [P, RA, BW]), sb("yS", [P, 2, BW])
        high, low = sb("high", [P, RH, BW], F32R), sb("low", [P, RH, BW], F32R)
        h_full, h_ready, g_full, g_used, hs_ready = [sem(x) for x in ("h_full", "h_ready", "g_full", "g_used", "hs_ready")]
        high_ready, low_ready, y_done = [sem(x) for x in ("high_ready", "low_ready", "y_done")]
        y_copied, y_turned, x_added = [sem(x) for x in ("y_copied", "y_turned", "x_added")]
        block = ctx.enter_context(nc.Block())

        def over_pairs(eng, pair):
            for k in range(TURN):
                pair(0, 0, k)

            def rest_of(n, p):
                for k in range(TURN, NP):
                    pair(n, p, k)
                return n + 1, 1 - p

            with eng.Fori(0, NB // 2 - 1) as i:
                for p in range(2):
                    n, q = rest_of(2 * i + p, p)
                    for k in range(TURN):
                        pair(n, q, k)
            n, q = rest_of(NB - 2, 0)
            for k in range(TURN):
                pair(n, q, k)
            rest_of(n, q)

        def first(n):
            return isinstance(n, int) and n == 0

        @block.tensor
        def _(pe):
            pe.sem_inc(y_done, RH)

            def out(n, p, k):
                e, c = pairs[k]
                if k == 0:
                    pe.wait_ge(y_copied, n + 1)
                    for b in range(3):
                        pe.matmul(psY[p][:, :], R["b2p"][:, b, :], R["GT"][:, ds(n * BW, BW)], start=b == 0, stop=False)
                pe.wait_ge(low_ready, NP * n + k + 1 + RA)
                at = slice(k * P, (k + 1) * P)
                matmul_split(pe, psY[p][:, :], (w["W2h"][:, at], w["W2l"][:, at]), (high[:, k % RH, :], low[:, k % RH, :]),
                             start=False, stop=k == NP - 1).then_inc(y_done, 1)

            def turn(p, n):
                pe.wait_ge(y_copied, n + 2)
                pe.wait_ge(x_added, n + 1)
                for t in range(TB):
                    mm = pe.transpose(psT[:, t * P:(t + 1) * P], yS[:, 1 - p, t * P:(t + 1) * P], C["ident"][:, :])
                mm.then_inc(y_turned, 1)

            def pair(n, p, k):
                e, c = pairs[k]
                here = ds(n * BW, BW)
                pe.wait_ge(h_ready, NP * n + k + 1)
                at = slice(k * P, (k + 1) * P)
                matmul_split(pe, psH[k % 2][:, :], (w["W1h"][:, at], w["W1l"][:, at]), (R["XTh"][:, here], R["XTl"][:, here]),
                             start=True, stop=True).then_inc(h_full, 1)
                if c == 0:
                    pe.wait_ge(g_used, NE * n + e + 1)
                    pe.matmul(psG[(NE * p + e) % 2][:, :], R["spread"][:, e, :], R["GT"][:, here], start=True, stop=True).then_inc(g_full, 1)
                if k >= LAG:
                    out(n, p, k - LAG)
                elif not first(n):
                    out(n - 1, 1 - p, NP + k - LAG)
                if k == LAG + 1 and not first(n):
                    turn(p, n)

            over_pairs(pe, pair)
            for k in range(NP - LAG, NP):
                out(NB - 1, 1, k)
            turn(0, NB)

        @block.scalar
        def _(act):
            act.sem_inc(h_ready, 2)
            act.sem_inc(y_copied, 2)

            def copy(n, p):
                act.wait_ge(y_done, NP * n + RH)
                act.wait_ge(x_added, n)
                nc.scalar.activation(yS[:, 1 - p, :], psY[1 - p][:, :], ACT.Copy).then_inc(y_copied, 1)

            def pair(n, p, k):
                act.wait_ge(h_full, NP * n + k + 1)
                act.wait_ge(hs_ready, NP * n + k + 1)
                nc.scalar.activation(h[:, k % RA, :], psH[k % 2][:, :], fn, bias=w["b1"][:, k:k + 1]).then_inc(h_ready, 1)
                if k == LAG and not first(n):
                    copy(n, p)

            over_pairs(act, pair)
            copy(NB, 0)

        @block.vector
        def _(dve):
            dve.sem_inc(hs_ready, RA)
            dve.sem_inc(g_used, 2)
            dve.sem_inc(x_added, 2)

            def take_high(n, k):
                dve.wait_ge(hs_ready, NP * n + k + 1 + RA)
                if pairs[k][1] == chunks - 1:
                    dve.sem_inc(g_used, 1)
                dve.wait_ge(y_done, NP * n + k + 1)
                nc.vector.tensor_copy(high[:, k % RH, :], hs[:, k % RA, :]).then_inc(high_ready, 1)

            def add(n):
                dve.wait_ge(y_turned, n)
                xt = X[:, ds((n - 1) * TB, TB), :]
                nc.vector.tensor_tensor(xt, psT[:, :].rearrange("p (t e) -> p t e", t=TB), xt, ALU.add).then_inc(x_added, 1)

            def pair(n, p, k):
                e, c = pairs[k]
                dve.wait_ge(h_ready, NP * n + k + 3)
                dve.wait_ge(low_ready, NP * n + k + 1)
                dve.wait_ge(g_full, NE * n + e + 1)
                nc.vector.tensor_tensor(hs[:, k % RA, :], h[:, k % RA, :], psG[(NE * p + e) % 2][:, :], ALU.mult).then_inc(hs_ready, 1)
                if k > 0:
                    take_high(n, k - 1)
                elif not first(n):
                    take_high(n - 1, NP - 1)
                if k == LAG + 2 and not first(n):
                    add(n)

            over_pairs(dve, pair)
            take_high(NB - 1, NP - 1)
            add(NB)

        @block.gpsimd
        def _(pool):
            pool.sem_inc(low_ready, RA)
            with pool.Fori(0, NB) as n:
                for k in range(NP):
                    pool.wait_ge(high_ready, NP * n + k + 1)
                    nc.gpsimd.tensor_tensor(low[:, k % RH, :], hs[:, k % RA, :], high[:, k % RH, :].bitcast(F32), ALU.subtract).then_inc(low_ready, 1)


def feed_forward(nc, kind, nm, C, X, d):
    F = FFN[kind]
    with ExitStack() as ctx:
        sb = lambda name, shape, dt=F32: ctx.enter_context(nc.sbuf_tensor(nm + name, shape, dt))
        ne, ch = F["gated"], F["chunks"]
        R = {"XTh": sb("XTh", [P, B * S], F32R), "XTl": sb("XTl", [P, B * S], F32R), "GT": sb("GT", [P, B * S], BF16),
             "b2p": sb("b2p", [P, 3, P], BF16), "spread": sb("spread", [P, GW, P], BF16)}
        hidden = F["experts"] * ch * P
        w = {n: sb(n, [P, hidden], F32R)[:, :] for n in ("W1h", "W1l", "W2h", "W2l")}
        w.update({"b1": sb("b1", [P, F["experts"] * ch]), "b2r": sb("b2r", [P, P]), "pick": sb("pick", [P, GW]),
                  "router": sb("router", [P, ne]), "b2": d[kind + "_b2"],
                  "W1": d[kind + "_W1"].rearrange("p e f -> p (e f)"), "W2": d[kind + "_W2"].rearrange("p e c f -> p (e c f)")})
        w["loads"] = [(w["router"][:, :], d[kind + "_router"]), (w["pick"][:, :], d["pick"]), (w["b1"][:, :], d[kind + "_b1"])]
        if "top" in F:
            w["br"] = sb("br", [P, ne])
            w["loads"].append((w["br"][:, :], d[kind + "_br"].broadcast_to([P, ne])))
        route(nc, nm, F, C, X, R, w)
        experts(nc, nm, F, C, X, R, w)


LAYERS = {
    "a0": dict(name="a0_", causal=True, max=True, scale=float(D) ** -0.5, clip=None, floor=False,
               rope=None, bias=True, latent=False, suffix=False, tables=None),
    "b0": dict(name="b0_", causal=True, max=False, scale=float(D + D // 2) ** -0.5, clip=80.0, floor=False,
               rope="pairs", bias=False, latent=True, suffix=False, tables="pairs",
               most=float(np.exp(80.0 / np.sqrt(12.0))), least=float(np.exp(-80.0 / np.sqrt(12.0)))),
    "a1": dict(name="a1_", causal=True, max=True, scale=float(D) ** -0.5, clip=100.0, floor=True,
               rope=None, bias=False, latent=False, suffix=True, tables=None),
    "b1": dict(name="b1_", causal=False, max=True, scale=float(D) ** -0.5, clip=None, floor=False,
               rope="half", bias=False, latent=False, suffix=False, tables="half"),
}


def weights_of(kind, d):
    sq = (P, P)
    if kind == "a0":
        return {"q": (d["a0_wq"], 0, sq), "k": (d["a0_wk"], 0, sq), "v": (d["a0_wv"], 0, sq), "o": (d["a0_wo"], 0, sq),
                "bq": (d["a0_bq"], 0, (P, 1)), "bk": (d["a0_bk"], 0, (P, 1)),
                "bv": (d["a0_bv"].broadcast_to([P, P]), 0, sq), "bo": (d["a0_bo"].broadcast_to([P, P]), 0, sq)}
    if kind == "b0":
        return {"down": (d["b0_down"], 0, (P, 64)), "kr": (d["b0_kr"], 0, (P, 4)), "kr_rot": (d["b0_krr"], 0, (P, 4)),
                "q": (d["b0_wq"], 0, (32, P)), "k": (d["b0_wk"], 32, (32, P)), "v": (d["b0_wv"], 32, (32, P)),
                "qr": (d["b0_qr"], 0, (32, 64)), "qr_rot": (d["b0_qrr"], 0, (32, 64)), "o": (d["b0_wo"], 0, sq)}
    if kind == "a1":
        return {**{n: (d["a1_w" + n], 0, sq) for n in "qkvo"}, "heads": (d["heads"], 0, (P, H))}
    return {"q": (d["b1_wq"], 0, sq), "q_rot": (d["b1_wqr"], 0, sq), "k": (d["b1_wk"], 0, sq), "k_rot": (d["b1_wkr"], 0, sq),
            "v": (d["b1_wv"], 0, sq), "o": (d["b1_wo"], 0, sq), "bo": (d["b1_bo"].broadcast_to([P, P]), 0, sq)}


STAGES = ("a0", "f0", "b0", "f0", "a1", "f1", "b1", "f1")


def build(nc, d, out, stages=STAGES):
    scratch = {
        "q": nc.dram_tensor("scratch_q", [UNITS + 2, 32, 3, S], BF16, kind="Internal").ap(),
        "k": nc.dram_tensor("scratch_k", [UNITS + 2, 32, 3, S], BF16, kind="Internal").ap(),
        "qr": nc.dram_tensor("scratch_qr", [UNITS + 2, 16, 3, S], BF16, kind="Internal").ap(),
        "kr": nc.dram_tensor("scratch_kr", [UNITS + 2, 4, 3, S], BF16, kind="Internal").ap(),
    }
    scratch["low"] = nc.dram_tensor("scratch_low", [2, HG, KT, P], F32, kind="Internal").ap()
    with ExitStack() as ctx:
        sb = lambda name, shape, dt=F32: ctx.enter_context(nc.sbuf_tensor(name, shape, dt))
        X = sb("X", [P, NT, P])
        C = {"ident": sb("ident", [P, P]), "ident16": sb("ident16", [P, P], BF16),
             "mask": sb("mask", [P, P]), "mask16": sb("mask16", [P, P], BF16), "eps": sb("eps", [P, 1])}
        x_loaded, c_loaded, c_ready, x_stored = [nc.alloc_semaphore(n) for n in ("x_loaded", "c_loaded", "c_ready", "x_stored")]
        with nc.Block() as block:
            @block.sync
            def _(sp):
                sp.dma_start(X[:, :, :], d["x"].rearrange("(t p) e -> p t e", p=P)).then_inc(x_loaded, 16)
                sp.dma_start(C["ident"][:, :], d["ident"]).then_inc(c_loaded, 16)
                sp.dma_start(C["mask"][:, :], d["mask"]).then_inc(c_loaded, 16)
                sp.wait_ge(x_loaded, 16)

            @block.vector
            def _(dve):
                nc.vector.memset(C["eps"][:, :], LN_EPS).then_inc(c_ready, 1)
                dve.wait_ge(c_loaded, 32)
                nc.vector.tensor_copy(C["ident16"][:, :], C["ident"][:, :]).then_inc(c_ready, 1)
                nc.vector.tensor_copy(C["mask16"][:, :], C["mask"][:, :]).then_inc(c_ready, 1)

        for n, kind in enumerate(stages):
            if kind in LAYERS:
                attention(nc, LAYERS[kind], C, X, weights_of(kind, d), scratch, d)
            else:
                feed_forward(nc, kind, f"{kind}{n}_", C, X, d)
        with nc.Block() as block:
            @block.sync
            def _(sp):
                sp.dma_start(out.rearrange("(t p) e -> p t e", p=P), X[:, :, :]).then_inc(x_stored, 16)
                sp.wait_ge(x_stored, 16)


def laid_out(inputs):
    f = np.float32
    a = {k: np.asarray(v) for k, v in inputs.items()}
    d = {"x": a["L0_attn_a_x"].reshape(B * S, E)}
    d["ident"] = np.eye(P, dtype=f)
    d["mask"] = np.where(np.arange(P)[None, :] > np.arange(P)[:, None], f(NEG), f(0))
    w1 = a["L0_attn_a_W1"].reshape(E, H, 3, D)
    b1 = a["L0_attn_a_b1"].reshape(H, 3, D)
    for i, n in enumerate("qkv"):
        d["a0_w" + n] = w1[:, :, i].reshape(E, P)
    d["a0_bq"], d["a0_bk"], d["a0_bv"] = b1[:, 0].reshape(P, 1), b1[:, 1].reshape(P, 1), b1[:, 2].reshape(1, P)
    d["a0_wo"], d["a0_bo"] = a["L0_attn_a_Wp"], a["L0_attn_a_bp"].reshape(1, P)
    d["b0_down"] = np.concatenate([a["L0_attn_b_W_DQ"], a["L0_attn_b_W_DKV"]], 1)
    d["b0_wq"], d["b0_wk"], d["b0_wv"] = a["L0_attn_b_W_UQ"], a["L0_attn_b_W_UK"], a["L0_attn_b_W_UV"]
    d["b0_wo"] = a["L0_attn_b_W_O"]
    pairs = lambda w: w.reshape(w.shape[0], -1, 2)[:, :, ::-1].reshape(w.shape)
    d["b0_qr"], d["b0_kr"] = a["L0_attn_b_W_QR"], a["L0_attn_b_W_KR"]
    d["b0_qrr"], d["b0_krr"] = pairs(d["b0_qr"]), pairs(d["b0_kr"])
    wt = a["L1_attn_a_w_qkv"].T
    for i, n in enumerate("qkv"):
        d["a1_w" + n] = wt[:, i * P:(i + 1) * P]
    d["a1_wo"] = a["L1_attn_a_w_proj"].T
    halves = lambda w: w.reshape(E, H, 2, D // 2)[:, :, ::-1].reshape(E, P)
    for i, n in enumerate("qkv"):
        d["b1_w" + n] = a["L1_attn_b_w_qkv"][:, i * P:(i + 1) * P]
    d["b1_wqr"], d["b1_wkr"] = halves(d["b1_wq"]), halves(d["b1_wk"])
    d["b1_wo"], d["b1_bo"] = a["L1_attn_b_w_out"], a["L1_attn_b_b_out"].reshape(1, P)
    d["heads"] = (np.arange(P)[:, None] // D == np.arange(H)[None, :]).astype(f)
    d["masked"] = (S - 1 - np.arange(KT)[None, :] * P - np.arange(P)[:, None]).astype(f)
    ew = lambda x, y: np.concatenate([x, y[None]], 0)
    for kind, ws in (("f0", ("L0_ffn_eW1", "L0_ffn_sW1", "L0_ffn_eb1", "L0_ffn_sb1", "L0_ffn_eW2", "L0_ffn_sW2", "L0_ffn_eb2", "L0_ffn_sb2")),
                     ("f1", ("L1_ffn_W1", "L1_ffn_Ws1", "L1_ffn_b1", "L1_ffn_bs1", "L1_ffn_W2", "L1_ffn_Ws2", "L1_ffn_b2", "L1_ffn_bs2"))):
        W1, b1, W2, b2 = (ew(a[ws[2 * i]], a[ws[2 * i + 1]]) for i in range(4))
        ex, ch = W1.shape[0], W1.shape[2] // P
        d[kind + "_W1"] = W1.transpose(1, 0, 2)
        d[kind + "_W2"] = W2.reshape(ex, ch, P, P).transpose(2, 0, 1, 3)
        d[kind + "_b1"] = b1.reshape(ex * ch, P).T
        d[kind + "_b2"] = b2
    d["f0_router"], d["f0_br"] = a["L0_ffn_router_W"], a["L0_ffn_router_b"].reshape(1, -1)
    d["f1_router"] = a["L1_ffn_gate_weight"].T
    r = np.arange(P)[:, None]
    d["pick"] = ((r % GW == np.arange(GW)[None, :]) & (r < 3 * GW)).astype(f)
    pos = np.arange(S, dtype=f)
    inv = f(10000.0) ** (-np.arange(0, 4, 2, dtype=f) / f(4))
    ang = pos[None, :] * inv[:, None]
    r = np.arange(64)
    d["pairs"] = np.stack([np.cos(ang)[(r % 4) // 2], np.sin(ang)[(r % 4) // 2] * np.where(r % 2 == 0, f(-1), f(1))[:, None]], 1)
    theta = f(1.0) / f(10000.0) ** (np.arange(0, D, 2, dtype=f) / f(D))
    ang = pos[None, :] * theta[:, None]
    r = np.arange(P)
    d["half"] = np.stack([np.cos(ang)[r % 4], np.sin(ang)[r % 4] * np.where(r % D < D // 2, f(-1), f(1))[:, None]], 1)
    return {k: np.ascontiguousarray(v) for k, v in d.items()}


def kernel(**inputs):
    import concourse.bacc as bacc
    from concourse.bass_utils import run_bass_kernel_spmd

    nc = bacc.Bacc("TRN2", target_bir_lowering=False, num_devices=1)
    arrays = laid_out(inputs)
    d = {n: nc.dram_tensor("in_" + n, v.shape, mybir.dt.from_np(v.dtype), kind="ExternalInput").ap() for n, v in arrays.items()}
    out = nc.dram_tensor("out", (B * S, E), F32, kind="ExternalOutput").ap()
    build(nc, d, out)
    r = run_bass_kernel_spmd(nc, [{"in_" + n: v for n, v in arrays.items()}], core_ids=[0])
    return np.asarray(r.results[0]["out"]).reshape(B, S, E)
```

```python
from contextlib import ExitStack

import numpy as np

import concourse.bass as bass
from concourse import mybir

F32 = mybir.dt.float32
BF16 = mybir.dt.bfloat16
I32 = mybir.dt.int32
F32R = mybir.dt.float32r
ALU = mybir.AluOpType
ACT = mybir.ActivationFunctionType
AX_X = mybir.AxisListType.X
ds = bass.ds

P = 128
B, S, E = 4, 1024, 128
NT = B * S // P
NB = 8
TB = 4
BW = TB * P
H, D = 16, 8
G, HG = 4, 4
UNITS = B * G
KT = S // P
VW = 32
LN_EPS = 1e-5
NEG = -1e30

Q_TERMS = (0, 0, 0, 1, 1, 2)
K_TERMS = (0, 1, 2, 0, 1, 0)
NTERM = len(Q_TERMS)
LATENT = 32
R_ROWS = H * D // 2 + D // 2
R_ROW = 64
M_ROW = 96
SPLIT_AHEAD, MAXIMA_AHEAD = 16000, 8500
RING_P = 4
RING_Q = 4


class Chain:

    def __init__(self, eng, sem, base=0):
        self.eng, self.sem, self.base, self.n = eng, sem, base, 0

    def step(self, ins):
        ins.then_inc(self.sem, 1)
        self.n += 1

    def wait(self):
        self.eng.wait_ge(self.sem, self.base + self.n)

    def link(self, ins):
        self.step(ins)
        self.wait()


def matmul_split(pe, out, weights, moving, start, stop):
    (wh, wl), (mh, ml) = weights, moving
    pe.matmul(out, wh, mh, start=start, stop=False)
    pe.matmul(out, wh, ml, start=False, stop=False)
    return pe.matmul(out, wl, mh, start=False, stop=stop)


def semaphores(nc, ctx, prefix):
    held = []

    def sem(name):
        held.append(nc.alloc_semaphore(prefix + name))
        return held[-1]

    def give_back():
        nc.clear_and_free_semaphores(held)
        nc.all_engine_barrier()
    ctx.callback(give_back)
    return sem


def steps_of(causal):
    out = []
    for qb in range(S // BW):
        for kt in range(TB * (qb + 1) if causal else KT):
            diagonal = causal and kt >= TB * qb
            out.append((qb, kt, P * (kt - TB * qb) if diagonal else 0, diagonal))
    return out


def row_blocks_of(causal):
    out = []
    for j in range(HG):
        for qt in range(KT):
            keys = P * (qt + 1) if causal else S
            for half in range((keys + BW - 1) // BW):
                width = min(BW, keys - BW * half)
                out.append((j, qt, half, width, causal and BW * half + width == keys))
    return out


def before_in_ring(x, uses, slots):
    return x - slots if x >= slots else -1 - (uses - 1 - x) % slots


def beside_of(steps, rows, at_once, splits):
    costs = [at_once] * (HG // at_once) + [HG]
    parts = [(s, part, (BW - q0) * cost) for s, (_, _, q0, _) in enumerate(steps) for part, cost in enumerate(costs)]
    beside = [[[] for _ in costs] for _ in steps]
    if not rows:
        return beside, []
    left = [sum(w for _, _, w in parts[k + 1:]) for k in range(len(parts))]
    split_at = max(k for k in range(len(parts)) if left[k] >= SPLIT_AHEAD)
    maxima_at = max(k for k in range(len(parts)) if left[k] >= MAXIMA_AHEAD)
    order = list(range(split_at, len(parts))) + list(range(split_at))
    total, cost = sum(w for _, _, w in parts), sum(b[3] + 64 for b in rows)
    todo, spent, passed, early = list(rows), 0, 0, []
    split_steps = list(range(splits))
    for k in order:
        s, part, w = parts[k]
        passed += w
        if k == split_at:
            beside[s][part].append(("split", split_steps.pop(0)))
        if k == maxima_at:
            beside[s][part] += [("split", step) for step in split_steps] + [("maxima", None)]
            split_steps = []
        while todo and (spent + (todo[0][3] + 64) / 2) * total <= passed * cost:
            b = todo.pop(0)
            spent += b[3] + 64
            beside[s][part].append(("rows", (2 if k >= split_at else 1, b)))
            if k >= split_at:
                early.append(b)
            if split_steps:
                beside[s][part].append(("split", split_steps.pop(0)))
    assert not todo
    return beside, early


def over_blocks(eng, first, ahead, rest_of):
    def block_of(n, p, i):
        first(n, p, i)
        ahead(n + 1, 1 - p, i + p)
        rest_of(n, p, i)

    ahead(0, 0, 0)
    with eng.Fori(0, NB // 2 - 1) as i:
        for p in range(2):
            block_of(2 * i + p, p, i)
    block_of(NB - 2, 0, NB // 2 - 1)
    first(NB - 1, 1, NB // 2 - 1)
    rest_of(NB - 1, 1, NB // 2 - 1)


def nothing(n, p, i):
    pass


def layernorm_all(nc, X, C, dve, act_sem, sd_sem, chain, T):
    stats, mean, sd, rstd, t1, t2 = T
    for t in range(NT):
        ins = nc.vector.bn_stats(stats[:, t, :], X[:, t, :])
    chain.link(ins)
    chain.link(nc.vector.tensor_tensor(t1[:, :], stats[:, :, 1], stats[:, :, 4], ALU.add))
    chain.step(nc.vector.tensor_scalar(mean[:, :], t1[:, :], 0.5, None, ALU.mult))
    chain.link(nc.vector.tensor_tensor(t2[:, :], stats[:, :, 1], stats[:, :, 4], ALU.subtract))
    chain.link(nc.vector.tensor_tensor(t2[:, :], t2[:, :], t2[:, :], ALU.mult))
    chain.link(nc.vector.tensor_tensor(t1[:, :], stats[:, :, 2], stats[:, :, 5], ALU.add))
    chain.link(nc.vector.tensor_scalar(t1[:, :], t1[:, :], 1.0 / E, None, ALU.mult))
    nc.vector.scalar_tensor_tensor(t1[:, :], t2[:, :], 0.25, t1[:, :], ALU.mult, ALU.add).then_inc(act_sem, 1)
    dve.wait_ge(sd_sem, 1)
    chain.link(nc.vector.reciprocal(rstd[:, :], sd[:, :]))


def attention_prepare(nc, L, C, X, A, w, scratch):
    rope, has_bias, latent, suffix = L["rope"], L["bias"], L["latent"], L["suffix"]
    nm = L["name"]
    with ExitStack() as ctx:
        sb = lambda name, shape, dt=F32: ctx.enter_context(nc.sbuf_tensor(nm + name, shape, dt))
        sem = semaphores(nc, ctx, nm + "prepare_")
        psum = lambda name, dt=F32: ctx.enter_context(nc.psum_tensor(nm + name, [P, BW], dt))

        T = [sb("stats", [P, NT, 6])] + [sb(n, [P, NT]) for n in ("mean", "sd", "rstd", "t1", "t2")]
        _, mean, sd, rstd, t1, _ = T
        xn = sb("xn", [P, 2, TB, P])
        xnT = sb("xnT", [P, 2, BW])
        psT = [psum("psT0"), psum("psT1")]
        psV = psum("psV")
        parts = [("q", P), ("k", P)] + ([("r", R_ROWS)] if latent else [])
        roped = {"q", "k"} if rope == "half" else {"r"} if rope == "pairs" else set()
        ps = {}
        for name, _ in parts:
            ps[name] = psum("ps" + name)
            if name in roped:
                ps[name + "_rot"] = psum("ps" + name + "r")
        if latent:
            fused_in_psum, fused_ready = sem("fused_in_psum"), sem("fused_ready")
        full = {n: sb("full" + n, [r, BW]) for n, r in parts}
        rest = {n: sb("rest" + n, [r, BW]) for n, r in parts}
        turned = {n: sb("turned" + n, [r, BW]) for n, r in parts if n in roped}
        pieces = {n: sb("pieces" + n, [r, 2, 3, BW], BF16) for n, r in parts}
        if suffix:
            square = {n: sb("square" + n, [P, BW]) for n in "qk"}
            norms = {n: psum("norms" + n) for n in "qk"}
            squared, norms_full, norms_read = sem("squared"), sem("norms_full"), sem("norms_read")

        var_ready, sd_ready, xn_ready = sem("var_ready"), sem("sd_ready"), sem("xn_ready")
        xT_in_psum, xT_ready = sem("xT_in_psum"), sem("xT_ready")
        proj_ready = {n: sem("proj_" + n) for n, _ in parts}
        rot_ready = {n: sem("rot_" + n) for n in roped}
        v_in_psum, v_ready = sem("v_in_psum"), sem("v_ready")
        full_ready = {n: sem("full_" + n) for n, _ in parts}
        first_ready = {n: sem("first_" + n) for n, _ in parts}
        rest_ready = {n: sem("rest_" + n) for n, _ in parts}
        second_ready = {n: sem("second_" + n) for n, _ in parts}
        third_ready = {n: sem("third_" + n) for n, _ in parts}
        stored = [sem("stored0"), sem("stored1")]
        dve_chain, pads_ready, zeros_ready = sem("dve_chain"), sem("pads_ready"), sem("zeros_ready")
        turned_ready = {n: sem("turned_" + n) for n in roped}
        w_ready = sem("w_ready")
        stores = [("q", "q", 0, P, G), ("k", "k", 0, P, G)]
        if latent:
            stores += [("qr", "r", 0, H * D // 2, G), ("kr", "r", H * D // 2, D // 2, 1)]
        store_done = 16 * len(stores)

        block = ctx.enter_context(nc.Block())

        @block.sync
        def _(sp):
            for dst, src in w["loads"]:
                sp.dma_start(dst, src).then_inc(w_ready, 16)
            for p in range(2):
                sp.sem_inc(stored[p], store_done)
            with sp.Fori(0, NB // 2) as i:
                for p in range(2):
                    for dst, name, first, rows, entries in stores:
                        sp.wait_ge(third_ready[name], 2 * i + p + 2)
                        sp.dma_start(
                            scratch[dst][ds(i * entries, entries), :, :, p * BW:(p + 1) * BW].rearrange("u r c n -> (u r) c n"),
                            pieces[name][first:first + rows, p]).then_inc(stored[p], 16)
            for p in range(2):
                sp.wait_ge(stored[p], store_done * (NB // 2 + 1))

        @block.tensor
        def _(pe):
            pe.wait_ge(w_ready, 16 * len(w["loads"]))
            if latent:
                at = 0
                for name, down, cols in (("uq", "down_q", P), ("uk", "down_kv", P), ("uv", "down_kv", P),
                                         ("uqr", "down_q", P // 2), ("uqr_rot", "down_q", P // 2)):
                    mm = pe.matmul(psV[:, at:at + cols], w[down][:, :], w[name][:, :], start=True, stop=True)
                    at += cols
                mm.then_inc(fused_in_psum, 1)
                pe.wait_ge(fused_ready, 2)

            def turn(n, p, i):
                pe.wait_ge(xn_ready, n + 1)
                for t in range(TB):
                    mm = pe.transpose(psT[p][:, t * P:(t + 1) * P], xn[:, p, t, :], C["ident"][:, :])
                mm.then_inc(xT_in_psum, 1)

            def project(n, p, i):
                pe.wait_ge(xT_ready, n + 1)
                x_block = xnT[:, p, :]
                for name, rows in parts:
                    pe.wait_ge(full_ready[name], n + 1)
                    if name not in roped:
                        pe.wait_ge(first_ready[name], n + 1)
                    pe.matmul(ps[name][0:rows, :], w[name][:, :], x_block, start=True, stop=True).then_inc(proj_ready[name], 1)
                    if name in roped:
                        pe.matmul(ps[name + "_rot"][0:rows, :], w[name + "_rot"][:, :], x_block,
                                  start=True, stop=True).then_inc(rot_ready[name], 1)
                pe.wait_ge(v_ready, n + 1)
                for t in range(TB):
                    mm = pe.matmul(psV[:, t * P:(t + 1) * P], xnT[:, p, t * P:(t + 1) * P], w["v"][:, :],
                                   start=True, stop=True)
                mm.then_inc(v_in_psum, 1)
                if suffix:
                    for k, name in enumerate("qk"):
                        pe.wait_ge(squared, 2 * n + k + 3)
                        pe.wait_ge(norms_read, 2 * n + k + 1)
                        pe.matmul(norms[name][0:H, :], w["heads"][:, :], square[name][:, :], start=True, stop=True).then_inc(norms_full, 1)

            over_blocks(pe, project, turn, nothing)

        @block.scalar
        def _(act):
            for b in range(RING_Q):
                zeros = A["K"][b][:, :, :].rearrange("p j n -> p (j n)").bitcast(F32).rearrange("p (k n) -> p k n", n=P)
                ins = nc.scalar.activation(zeros, C["ident"][:, :].unsqueeze(1).broadcast_to([P, HG * S // 2 // P, P]), ACT.Copy, scale=0.0)
            ins.then_inc(zeros_ready, 1)
            act.wait_ge(w_ready, 16 * len(w["loads"]))
            for name, _ in parts:
                if name not in roped:
                    act.sem_inc(full_ready[name], 1)
                    act.sem_inc(first_ready[name], 1)
            if not has_bias:
                act.sem_inc(v_ready, 1)
            if latent:
                act.wait_ge(fused_in_psum, 1)
                nc.scalar.activation(w["fused"][:, :, :], psV[:, 0:3 * P].rearrange("p (k n) -> p k n", k=3), ACT.Copy).then_inc(fused_ready, 1)
                nc.scalar.activation(w["both_r"][:, :, 0:P // 2], psV[:, 3 * P:4 * P].rearrange("p (k n) -> p k n", k=2), ACT.Copy).then_inc(fused_ready, 1)
            act.wait_ge(var_ready, 1)
            nc.scalar.activation(sd[:, :], t1[:, :], ACT.Sqrt, bias=C["eps"][:, 0:1]).then_inc(sd_ready, 1)

            def keep(n, p, i):
                act.wait_ge(xT_in_psum, n + 1)
                nc.scalar.activation(xnT[:, p, :], psT[p][:, :], ACT.Copy).then_inc(xT_ready, 1)

            def split(n, p, i):
                order = [x[0] for x in parts if x[0] not in roped] + [x[0] for x in parts if x[0] in roped]
                for name in order:
                    if name in roped:
                        act.wait_ge(full_ready[name], n + 2)
                        src = full[name][:, :]
                    else:
                        act.wait_ge(proj_ready[name], n + 1)
                        rows = dict(parts)[name]
                        src = ps[name][0:rows, :]
                        act.wait_ge(rest_ready[name], n + 1)
                        if suffix:
                            act.wait_ge(squared, 2 * n + 1 + (name == "k"))
                        if has_bias:
                            nc.scalar.activation(full[name][:, :], src, ACT.Identity, bias=w["b" + name][:, 0:1]).then_inc(full_ready[name], 1)
                        else:
                            nc.scalar.activation(full[name][:, :], src, ACT.Copy).then_inc(full_ready[name], 1)
                    if name == order[0]:
                        act.wait_ge(stored[p], store_done * (i + 1))
                    if has_bias:
                        nc.scalar.activation(pieces[name][:, p, 0, :], src, ACT.Identity, bias=w["b" + name][:, 0:1]).then_inc(first_ready[name], 1)
                    else:
                        nc.scalar.activation(pieces[name][:, p, 0, :], src, ACT.Copy).then_inc(first_ready[name], 1)
                if not has_bias:
                    act.wait_ge(v_in_psum, n + 1)
                    nc.scalar.activation(A["VR"][:, ds(i * G, G), p * TB:(p + 1) * TB, :],
                                         psV[:, :].rearrange("p (t g r) -> p g t r", g=G, r=32), ACT.Copy).then_inc(v_ready, 1)

            def split_again(n, p, i):
                for name in [x[0] for x in parts if x[0] not in roped] + [x[0] for x in parts if x[0] in roped]:
                    act.wait_ge(rest_ready[name], n + 2)
                    nc.scalar.activation(pieces[name][:, p, 1, :], rest[name][:, :], ACT.Copy).then_inc(second_ready[name], 1)

            over_blocks(act, split, keep, split_again)

        @block.vector
        def _(dve):
            dve.wait_ge(w_ready, 16 * len(w["loads"]))
            for name in roped:
                dve.sem_inc(turned_ready[name], 1)
            for name, _ in parts:
                dve.sem_inc(rest_ready[name], 1)
                dve.sem_inc(third_ready[name], 1)
            if has_bias:
                dve.sem_inc(v_ready, 1)
            if suffix:
                dve.sem_inc(norms_read, 2)
            layernorm_all(nc, X, C, dve, var_ready, sd_ready, Chain(dve, dve_chain), T)

            def normalise(n, p, i):
                for t in range(TB):
                    at = ds(n * TB + t, 1)
                    ins = nc.vector.tensor_scalar(xn[:, p, t, :], X[:, at, :].rearrange("p a e -> p (a e)"),
                                                  mean[:, at], rstd[:, at], ALU.subtract, ALU.mult)
                ins.then_inc(xn_ready, 1)

            def split(n, p, i):
                for name, rows in parts:
                    if name in roped:
                        table = C[L["tables"]]
                        dve.wait_ge(proj_ready[name], n + 1)
                        dve.wait_ge(turned_ready[name], n + 1)
                        dve.wait_ge(third_ready[name], n + 1)
                        nc.vector.tensor_tensor(rest[name][:, :], ps[name][0:rows, :], table[0:rows, 0, p * BW:(p + 1) * BW], ALU.mult)
                        dve.wait_ge(rot_ready[name], n + 1)
                        nc.vector.tensor_tensor(turned[name][:, :], ps[name + "_rot"][0:rows, :],
                                                table[0:rows, 1, p * BW:(p + 1) * BW], ALU.mult).then_inc(turned_ready[name], 1)
                for name, _ in parts:
                    dve.wait_ge(first_ready[name], n + 1 + (0 if name in roped else 1))
                    dve.wait_ge(full_ready[name], n + 2)
                    dve.wait_ge(third_ready[name], n + 1)
                    nc.vector.tensor_tensor(rest[name][:, :], full[name][:, :], pieces[name][:, p, 0, :], ALU.subtract).then_inc(rest_ready[name], 1)
                if has_bias:
                    dve.wait_ge(v_in_psum, n + 1)
                    for t in range(TB):
                        ins = nc.vector.tensor_tensor(
                            A["VR"][:, ds(i * G, G), p * TB + t, :],
                            psV[:, t * P:(t + 1) * P].rearrange("p (g r) -> p g r", r=32),
                            w["bv"][:, :].rearrange("p (g r) -> p g r", r=32), ALU.add)
                    ins.then_inc(v_ready, 1)
                for name, _ in parts:
                    dve.wait_ge(second_ready[name], n + 1)
                    nc.vector.tensor_tensor(pieces[name][:, p, 2, :], rest[name][:, :], pieces[name][:, p, 1, :], ALU.subtract).then_inc(third_ready[name], 1)
                if suffix:
                    for k, name in enumerate("qk"):
                        dve.wait_ge(norms_full, 2 * n + k + 1)
                        nc.vector.tensor_reduce(A["peak"][:, k, ds(n, 1)], norms[name][0:H, :], AX_X, ALU.max).then_inc(norms_read, 1)

            over_blocks(dve, nothing, normalise, split)

        @block.gpsimd
        def _(pool):
            for name in roped:
                pool.sem_inc(full_ready[name], 1)
            nc.gpsimd.memset(A["VR"][:, UNITS, :, :], 0.0)
            for b in range(RING_Q):
                nc.gpsimd.memset(A["Q"][b][:, :, :].bitcast(I32), 0)
            for b in range(2):
                last = nc.gpsimd.memset(A["V"][b][:, :, :, :], 0.0)
            last.then_inc(pads_ready, 1)
            pool.wait_ge(pads_ready, 1)
            pool.wait_ge(zeros_ready, 1)
            for b in range(RING_Q):
                last = nc.gpsimd.memset(A["K"][b][M_ROW:M_ROW + 3, :, :], 1.0)
            last.then_inc(pads_ready, 1)
            pool.wait_ge(pads_ready, 2)
            for b in range(2):
                last = nc.gpsimd.memset(A["V"][b][:, :, :, D:D + 1], 1.0)
            last.then_inc(pads_ready, 1)
            pool.wait_ge(pads_ready, 3)
            if suffix:
                pool.sem_inc(squared, 2)
                with pool.Fori(0, NB) as n:
                    for k, name in enumerate("qk"):
                        pool.wait_ge(full_ready[name], n + 2)
                        pool.wait_ge(norms_read, 2 * n + k + 1)
                        nc.gpsimd.tensor_tensor(square[name][:, :], full[name][:, :], full[name][:, :], ALU.mult).then_inc(squared, 1)
            if roped:
                with pool.Fori(0, NB // 2) as i:
                    for p in range(2):
                        n = 2 * i + p
                        for name, _ in parts:
                            if name in roped:
                                pool.wait_ge(turned_ready[name], n + 2)
                                nc.gpsimd.tensor_tensor(full[name][:, :], rest[name][:, :], turned[name][:, :], ALU.add).then_inc(full_ready[name], 1)


def masked_sums(nc, L, C, A, d):
    nm = L["name"]
    with ExitStack() as ctx:
        sb = lambda name, shape, dt=F32: ctx.enter_context(nc.sbuf_tensor(nm + name, shape, dt))
        sem = semaphores(nc, ctx, nm + "sums_")
        bank = lambda name: ctx.enter_context(nc.psum_tensor(nm + name, [P, BW], F32))
        later, ones = sb("later", [P, P]), sb("onesq", [P, P])
        after = sb("after", [P, 2, UNITS, 32])
        peaks, bound, most = sb("peaks", [H, 2]), sb("bound", [H, 1]), sb("most", [1, 1])
        psS, psB = [bank("psF0"), bank("psF1")], bank("psB")
        ready, later_ready, added, done, copied, bounded, turned = [sem("ms_" + x) for x in ("ready", "later", "added", "done", "copied", "bounded", "turned")]
        chain_sem = sem("ms_chain")
        block = ctx.enter_context(nc.Block())
        V = A["VR"]

        @block.sync
        def _(sp):
            sp.dma_start(A["masked"][:, :], d["masked"]).then_inc(ready, 16)
            sp.wait_ge(ready, 16)

        @block.gpsimd
        def _(pool):
            nc.gpsimd.memset(A["SUF"][:, 0, :, :], 0.0)
            nc.gpsimd.memset(A["SUM"][:, 0, :], 0.0)
            nc.gpsimd.memset(after[:, (KT - 1) % 2], 0.0).then_inc(added, 1)
            for t in reversed(range(-1, KT - 1)):
                pool.wait_ge(added, KT - 1 - t)
                if t < KT - 2:
                    pool.wait_ge(done, KT - 2 - t)
                nc.gpsimd.tensor_tensor(after[:, t % 2], after[:, (t + 1) % 2], V[:, 0:UNITS, t + 1, :], ALU.add).then_inc(added, 1)

        @block.tensor
        def _(pe):
            pe.wait_ge(later_ready, 2)
            for n, t in enumerate(reversed(range(-1, KT))):
                pe.wait_ge(added, n + 1)
                if n >= 2:
                    pe.wait_ge(copied, n - 1)
                out = psS[n % 2][:, :].rearrange("p (u r) -> p u r", r=32)
                if t >= 0:
                    pe.matmul(out, later[:, :], V[:, 0:UNITS, t, :], start=True, stop=False)
                pe.matmul(out, ones[:, :], after[:, t % 2], start=t < 0, stop=True).then_inc(done, 1)
            pe.wait_ge(bounded, 1)
            pe.matmul(psB[0:1, 0:H], bound[:, :], C["ident"][0:H, 0:H], start=True, stop=True).then_inc(turned, 1)

        @block.scalar
        def _(act):
            for n, t in enumerate(reversed(range(-1, KT))):
                act.wait_ge(done, n + 1)
                src = psS[n % 2][:, :].rearrange("p (u r) -> p u r", r=32)
                dst = A["SUF"][:, 1:UNITS + 1, t, :] if t >= 0 else A["SUM"][:, 1:UNITS + 1, :]
                nc.scalar.activation(dst, src, ACT.Copy).then_inc(copied, 1)

        @block.vector
        def _(dve):
            chain = Chain(dve, chain_sem)
            nc.vector.memset(ones[:, :], 1.0).then_inc(later_ready, 1)
            nc.vector.memset(A["clip_bias"][:, :], -L["clip"])
            chain.link(nc.vector.tensor_scalar(later[:, :], C["mask"][:, :], -1.0, None, ALU.is_ge))
            nc.vector.tensor_tensor(later[:, :], later[:, :], C["ident"][:, :], ALU.subtract).then_inc(later_ready, 1)
            chain.link(nc.vector.tensor_reduce(peaks[:, :], A["peak"][:, :, :], AX_X, ALU.max))
            nc.vector.tensor_tensor(bound[:, :], peaks[:, 0:1], peaks[:, 1:2], ALU.mult).then_inc(bounded, 1)
            dve.wait_ge(turned, 1)
            chain.link(nc.vector.tensor_reduce(most[:, :], psB[0:1, 0:H], AX_X, ALU.max))
            chain.link(nc.vector.tensor_scalar(A["may_clip"][0:1, :], most[:, :], 0.99 * (L["clip"] / L["scale"]) ** 2, None, ALU.is_ge))


def attention_core(nc, L, C, A, scratch):
    nm = L["name"]
    causal, needs_max, scale, latent = L["causal"], L["max"], L["scale"], L["latent"]
    floor = L["floor"]
    LAG = 2 if needs_max else 3
    steps = steps_of(causal)
    NS = len(steps)
    rows = row_blocks_of(causal) if needs_max else []
    first_half = max(s for s in range(NS) if steps[s][0] == 0)
    NDIAG = sum(s[3] for s in steps)

    AT_ONCE, ST, RS = (1, 3, 3) if needs_max else (2, 2, 2)
    GROUPS = HG // AT_ONCE
    SPLITS = 6 if floor else 5
    beside, early = beside_of(steps, rows, AT_ONCE, SPLITS)
    beside[LAG + 1][0].append(("output", -1))
    beside[first_half + LAG + 2][0].append(("output", 0))
    before = []
    if needs_max:
        before = [("rows", (0, b)) for b in rows]
        for k in range(SPLITS):
            before += [("split", k)] + [("rows", (1, b)) for b in early[k:k + 1]]
        before += [("maxima", None)] + [("rows", (1, b)) for b in early[SPLITS:]]
    PRO = sum(kind != "split" for kind, _ in before)
    USES = sum(kind != "split" for step in beside for part in step for kind, _ in part)
    if needs_max:
        MAX_PRO = [kind for kind, _ in before if kind != "split"].index("maxima")
        MAX_USE = [kind for step in beside for part in step for kind, _ in part if kind != "split"].index("maxima")
    EXP0, TRI0, CLIP0 = GROUPS * (LAG + 1), LAG, LAG + 1

    with ExitStack() as ctx:
        sb = lambda name, shape, dt=F32: ctx.enter_context(nc.sbuf_tensor(nm + name, shape, dt))
        sem = semaphores(nc, ctx, nm + "core_")
        st = [ctx.enter_context(nc.psum_tensor(nm + f"st{i}", [P, AT_ONCE, BW], F32)) for i in range(ST)]
        row = [ctx.enter_context(nc.psum_tensor(nm + f"row{i}", [P, BW], F32)) for i in range(RS)]
        acc = [ctx.enter_context(nc.psum_tensor(nm + f"acc{i}", [P, BW], F32)) for i in range(2)]
        prob = sb("prob", [P, RING_P, HG, BW])
        halfmax = sb("halfmax", [P, 2, HG, KT, 2])
        rowmax = sb("rowmax", [P, 2, HG, KT])
        left = sb("left", [P, HG, KT])
        mpieces = sb("mpieces", [P, 3, HG, KT], BF16)
        mT = sb("mT", [3 * HG * KT, 2, P], BF16)
        accS = sb("accS", [P, 2, BW])
        if floor:
            floors = sb("floors", [P, HG, S])
            low_ready, low_stored, floors_loaded = sem("low_ready"), sem("low_stored"), sem("floors_loaded")

        loaded = [sem(f"loaded{b}") for b in range(RING_Q)]
        v_loaded = sem("v_loaded")
        m_loaded = [sem("m_loaded0"), sem("m_loaded1")]
        st_full, exp_done = sem("st_full"), sem("exp_done")
        tri_done, clip_done = sem("tri_done"), sem("clip_done")
        pv_done = sem("pv_done")
        row_full, row_read = sem("row_full"), sem("row_read")
        m_split = sem("m_split")
        acc_copied, acc_turned = sem("acc_copied"), sem("acc_turned")
        dve_chain = sem("dve_chain")
        stand_in, stand_in_prob = sem("stand_in"), sem("stand_in_prob")
        NLOAD = 2 * NTERM * (2 if latent else 1)

        def over_units(eng, body):
            def rounds(general):
                with eng.Fori(0, UNITS // RING_Q) as i:
                    for q in range(RING_Q):
                        body(RING_Q * i + q, q, i, general)

            if not floor:
                rounds(L["clip"] is not None)
                return
            may_clip = eng.value_load(A["may_clip"][0:1, 0:1], min_val=0, max_val=1)
            with eng.If(may_clip):
                rounds(True)
            with eng.Else():
                rounds(False)

        block = ctx.enter_context(nc.Block())

        @block.sync
        def _(sp):
            for par in range(2):
                sp.sem_inc(m_loaded[par], 48)

            def load(u, q, batch):
                at = ds(u, 1)
                for t in range(NTERM):
                    for name, dst, piece in (("q", A["Q"], Q_TERMS[t]), ("k", A["K"], K_TERMS[t])):
                        sp.dma_start(dst[q][D * t:D * (t + 1), :, :],
                                     scratch[name][at, :, piece, :].rearrange("u (j d) n -> (u d) j n", d=D)).then_inc(loaded[q], 16)
                    if latent:
                        r0 = R_ROW + 4 * t
                        sp.dma_start(A["Q"][q][r0:r0 + 4, :, :],
                                     scratch["qr"][at, :, Q_TERMS[t], :].rearrange("u (j d) n -> (u d) j n", d=4)).then_inc(loaded[q], 16)
                        one = scratch["kr"][ds(batch, 1), :, K_TERMS[t], :].rearrange("u d n -> (u d) n")
                        sp.dma_start(A["K"][q][r0:r0 + 4, :, :], one.unsqueeze(1).broadcast_to([4, HG, S])).then_inc(loaded[q], 16)

            def move_maxima(q, index):
                sp.wait_ge(row_read, index + 1 + RS)
                for c in range(3):
                    sp.dma_start(A["Q"][q][M_ROW + c:M_ROW + c + 1, :, :],
                                 mT[HG * KT * c:HG * KT * (c + 1), q % 2, :]).then_inc(m_loaded[q % 2], 16)

            load(0, 0, 0)
            load(1, 1, 0)
            stands = [("q", UNITS), ("q", UNITS + 1), ("k", UNITS), ("k", UNITS + 1)]
            if latent:
                stands += [("qr", UNITS), ("qr", UNITS + 1), ("kr", B)]
            for name, entry in stands:
                sp.dma_start(scratch[name][entry], scratch[name][0]).then_inc(stand_in, 16)
            sp.wait_ge(stand_in, 16 * len(stands))
            if needs_max:
                move_maxima(0, MAX_PRO)

            def body(u, q, i, general):
                if q == 0:
                    sp.wait_ge(pv_done, NS * u + 1)
                else:
                    sp.wait_ge(pv_done, RING_P + NS * (RING_Q * i + q - 1))
                load(u + 2, (q + 2) % RING_Q, i + (q + 2) // G)
                if floor and general:
                    sp.wait_ge(low_ready, u + 1)
                    sp.dma_start(scratch["low"][q % 2].rearrange("j t p -> p j t"), A["LOW"][:, ds(u, 1), :, :].rearrange("p u j t -> p (u j) t"),
                                 allow_slow_non_contiguous=True).then_inc(low_stored, 16)
                    sp.wait_ge(low_stored, 16 * u + 16)
                    sp.nop(nofuse=True)
                    sp.wait_ge(clip_done, CLIP0 + NS * u)
                    sp.dma_start(floors[:, :, :].rearrange("p j n -> p (j n)"),
                                 scratch["low"][q % 2].rearrange("j t p -> (j t p)").partition_broadcast(P)).then_inc(floors_loaded, 16)
                if needs_max:
                    move_maxima((q + 1) % RING_Q, PRO + USES * u + MAX_USE)
            over_units(sp, body)
            for q in range(RING_Q):
                sp.wait_ge(loaded[q], 16 * NLOAD * (UNITS // RING_Q + (q < 2)))
            if needs_max:
                for par in range(2):
                    sp.wait_ge(m_loaded[par], 48 * (1 + UNITS // 2 + (par == 0)))

        @block.gpsimd
        def _(pool):
            def load_v(u, par):
                nc.gpsimd.tensor_copy(A["V"][par][:, :, :, 0:D],
                                      A["VR"][:, ds(u, 1), :, :].rearrange("p u t (j d) -> p (u t) j d", d=D)).then_inc(v_loaded, 1)

            def body(u, q, i, general):
                for s, (qb, kt, q0, diagonal) in enumerate(steps):
                    if s == LAG + 1:
                        pool.wait_ge(pv_done, RING_P + NS * u + 1)
                        load_v(u + 1, (q + 1) % 2)
                    if diagonal:
                        if general:
                            pool.wait_ge(clip_done, CLIP0 + NS * u + s + 1)
                        else:
                            pool.wait_ge(exp_done, EXP0 + GROUPS * (NS * u + s + 1))
                        pool.nop(nofuse=True)
                        on = prob[:, s % RING_P, :, q0:q0 + P]
                        nc.gpsimd.affine_select(out=on, in_=on, compare_op=ALU.is_ge, fill=0.0, base=0,
                                                pattern=[[0, HG], [1, P]], channel_multiplier=-1).then_inc(tri_done, 1)
            if causal:
                pool.sem_inc(tri_done, TRI0)
            for t in range(LAG):
                nc.gpsimd.memset(prob[:, RING_P - 1 - t], 1.0).then_inc(stand_in_prob, 1)
            load_v(0, 0)
            over_units(pool, body)

        @block.tensor
        def _(pe):
            pe.sem_inc(pv_done, RING_P - LAG)

            def rows_of(slot, ring, b):
                j, qt, half, width, diagonal = b
                mm = pe.matmul(slot[:, 0:width], A["Q"][ring][0:M_ROW, j, qt * P:(qt + 1) * P],
                               A["K"][ring][0:M_ROW, j, half * BW:half * BW + width], start=True, stop=not diagonal)
                if diagonal:
                    mm = pe.matmul(slot[:, width - P:width], C["ident16"][:, :], C["mask16"][:, :], start=False, stop=True)
                return mm

            def maxima_of(slot, v):
                pe.wait_ge(m_split, v + 1)
                return pe.transpose(slot[0:3 * HG * KT, 0:P // 2].bitcast(BF16),
                                    mpieces[:, :, :, :].rearrange("p c j t -> p (c j t)"), C["ident16"][:, :])

            def output_of(slot, u, qb):
                pe.wait_ge(acc_copied, 2 * u + qb + 3)
                for t in range(TB):
                    mm = pe.transpose(slot[:, t * P:(t + 1) * P], accS[:, qb % 2, t * P:(t + 1) * P], C["ident"][:, :])
                return mm

            def through_v(u, q, t, general):
                ring, s = (q - (t < 0)) % 2, t % NS
                qb, kt, q0, diagonal = steps[s]
                if t == 0:
                    pe.wait_ge(v_loaded, u + 1)
                if kt == 0:
                    pe.wait_ge(acc_copied, 2 * u + qb + 1)
                if diagonal:
                    before_it = sum(x[3] for x in steps[:s]) - (NDIAG if t < 0 else 0)
                    pe.wait_ge(tri_done, NDIAG * u + before_it + TRI0 + 1)
                elif general:
                    pe.wait_ge(clip_done, NS * u + t + CLIP0 + 1)
                else:
                    pe.wait_ge(exp_done, GROUPS * (NS * u + t + 1) + EXP0)
                last = s + 1 == NS or steps[s + 1][0] != qb
                for j in range(HG):
                    mm = pe.matmul(acc[qb][VW * j:VW * (j + 1), q0:BW], A["V"][ring][:, kt, j, :],
                                   prob[:, s % RING_P, j, q0:BW], start=kt == 0, stop=last)
                mm.then_inc(pv_done, 1)

            pe.wait_ge(stand_in_prob, LAG)
            for j in range(HG):
                pe.matmul(acc[1][VW * j:VW * (j + 1), :], A["V"][1][:, 0, j, :], prob[:, RING_P - 1, j, :], start=True, stop=False)

            if needs_max:
                pe.wait_ge(loaded[0], 16 * NLOAD)
                pe.wait_ge(loaded[1], 16 * NLOAD)
                for k, (kind, b) in enumerate(x for x in before if x[0] != "split"):
                    pe.wait_ge(row_read, k + 1)
                    slot = row[(k - PRO + USES) % RS]
                    mm = rows_of(slot, b[0], b[1]) if kind == "rows" else maxima_of(slot, 0)
                    mm.then_inc(row_full, 1)

            def body(u, q, i, general):
                if needs_max:
                    pe.wait_ge(m_loaded[q % 2], 48 * (2 * i + q // 2 + 2))
                else:
                    pe.wait_ge(loaded[q], 16 * NLOAD * (i + 1))
                k = 0
                for s, (qb, kt, q0, diagonal) in enumerate(steps):
                    for part in range(GROUPS + 1):
                        if part < GROUPS:
                            x = GROUPS * s + part
                            pe.wait_ge(exp_done, GROUPS * NS * u + before_in_ring(x, GROUPS * NS, ST) + EXP0 + 1)
                            for j in range(AT_ONCE * part, AT_ONCE * (part + 1)):
                                mm = pe.matmul(st[x % ST][:, j % AT_ONCE, q0:BW], A["K"][q][:, j, kt * P:(kt + 1) * P],
                                               A["Q"][q][:, j, qb * BW + q0:(qb + 1) * BW], start=True, stop=True)
                            mm.then_inc(st_full, 1)
                        else:
                            through_v(u, q, s - LAG, general)
                        for kind, b in beside[s][part]:
                            if kind == "split":
                                continue
                            pe.wait_ge(row_read, PRO + USES * u + before_in_ring(k, USES, RS) + RS + 1)
                            slot = row[k % RS]
                            if kind == "rows":
                                if b[0] == 2 and b[1] == rows[0]:
                                    pe.wait_ge(loaded[(q + 2) % RING_Q], 16 * NLOAD * (i + 1 + (q + 2) // RING_Q))
                                rows_of(slot, (q + b[0]) % RING_Q, b[1]).then_inc(row_full, 1)
                            elif kind == "maxima":
                                maxima_of(slot, u + 1).then_inc(row_full, 1)
                            else:
                                output_of(slot, u, b).then_inc(row_full, 1)
                            k += 1

            over_units(pe, body)
            for t in range(-LAG, 0):
                through_v(UNITS, 0, t, False)
            pe.wait_ge(row_read, PRO + USES * UNITS + before_in_ring(0, USES, RS) + RS + 1)
            output_of(row[0], UNITS, -1).then_inc(row_full, 1)

        @block.scalar
        def _(act):
            act.sem_inc(exp_done, EXP0)
            act.sem_inc(acc_copied, 1)

            def copy_output(u, block_done, v_count):
                act.wait_ge(pv_done, v_count)
                act.wait_ge(acc_turned, 2 * u + (1 if block_done == 1 else 2))
                nc.scalar.activation(accS[:, block_done, :], acc[block_done][:, :], ACT.Copy).then_inc(acc_copied, 1)

            def body(u, q, i, general):
                if floor:
                    act.wait_ge(m_split, u + 1)
                    nc.scalar.activation(A["LOW"][:, ds(u, 1), :, :].rearrange("p u j t -> p (u j) t"), rowmax[:, q % 2], ACT.Exp, bias=A["clip_bias"][:, 0:1], scale=-scale).then_inc(low_ready, 1)
                for s, (qb, kt, q0, diagonal) in enumerate(steps):
                    act.wait_ge(pv_done, NS * u + s + 1)
                    for part in range(GROUPS):
                        x = GROUPS * s + part
                        act.wait_ge(st_full, GROUPS * NS * u + x + 1)
                        nc.scalar.activation(prob[:, s % RING_P, AT_ONCE * part:AT_ONCE * (part + 1), q0:BW], st[x % ST][:, :, q0:BW],
                                             ACT.Exp, scale=scale).then_inc(exp_done, 1)
                    if s == LAG:
                        copy_output(u, 1, RING_P + NS * u)
                    if s == first_half + LAG + 1:
                        copy_output(u, 0, RING_P + NS * u + first_half + 1)
            with act.Fori(0, UNITS // RING_Q) as i:
                for q in range(RING_Q):
                    body(RING_Q * i + q, q, i, False)
            copy_output(UNITS, 1, RING_P + NS * UNITS)

        @block.vector
        def _(dve):
            dve.sem_inc(row_read, RS)
            dve.sem_inc(clip_done, CLIP0)
            dve.sem_inc(acc_turned, 2)

            def read_rows(slot, ring, b):
                j, qt, half, width, diagonal = b
                return nc.vector.tensor_reduce(halfmax[:, ring % 2, j, qt, half:half + 1], slot[:, 0:width], AX_X, ALU.max)

            def split_maxima(index, ring, chain, step):
                m, halves = rowmax[:, ring % 2], halfmax[:, ring % 2]
                if step > 0:
                    chain.wait()
                if step == 0:
                    dve.wait_ge(row_read, index + RS)
                    if causal:
                        nc.vector.tensor_copy(m[:, :, 0:TB], halves[:, :, 0:TB, 0])
                        chain.step(nc.vector.tensor_tensor(m[:, :, TB:KT], halves[:, :, TB:KT, 0], halves[:, :, TB:KT, 1], ALU.max))
                    else:
                        chain.step(nc.vector.tensor_tensor(m[:, :, :], halves[:, :, :, 0], halves[:, :, :, 1], ALU.max))
                elif step == SPLITS - 5:
                    limit = L["clip"] / scale
                    chain.step(nc.vector.tensor_scalar(m[:, :, :], m[:, :, :], limit, -limit, ALU.min, ALU.max))
                elif step == SPLITS - 4:
                    chain.step(nc.vector.tensor_scalar(mpieces[:, 0], m[:, :, :], -1.0, None, ALU.mult))
                elif step == SPLITS - 3:
                    chain.step(nc.vector.scalar_tensor_tensor(left[:, :, :], m[:, :, :], -1.0, mpieces[:, 0], ALU.mult, ALU.subtract))
                elif step == SPLITS - 2:
                    chain.step(nc.vector.tensor_copy(mpieces[:, 1], left[:, :, :]))
                else:
                    nc.vector.tensor_tensor(mpieces[:, 2], left[:, :, :], mpieces[:, 1], ALU.subtract).then_inc(m_split, 1)

            def take_maxima(slot, ring, v):
                dve.wait_ge(m_loaded[ring % 2], v)
                return nc.vector.tensor_copy(mT[:, ring % 2, :], slot[0:3 * HG * KT, 0:P // 2].bitcast(BF16))

            def take_output(slot, u, qb):
                tiles = slice((qb % 2) * TB, (qb % 2 + 1) * TB)
                out = A["AO"][:, ds(u + 1 + (-1 if qb < 0 else 0), 1), tiles, :, :].rearrange("p u t j d -> p (u t) j d")
                return nc.vector.tensor_copy(out, slot[:, :].rearrange("p (t j r) -> p t j r", t=TB, r=VW)[:, :, :, 0:D + 1])

            pre = Chain(dve, dve_chain, 0)
            k = 0
            for kind, b in before:
                if kind == "split":
                    split_maxima(k, 0, pre, b)
                    continue
                dve.wait_ge(row_full, k + 1)
                slot = row[(k - PRO + USES) % RS]
                ins = read_rows(slot, b[0], b[1]) if kind == "rows" else take_maxima(slot, 0, 48)
                ins.then_inc(row_read, 1)
                k += 1
            LINKS = SPLITS - 1 if needs_max else 0

            def body(u, q, i, general):
                chain = Chain(dve, dve_chain, pre.n + LINKS * u)
                k = 0
                for s, (qb, kt, q0, diagonal) in enumerate(steps):
                    for kind, b in [x for part in beside[s] for x in part]:
                        slot = row[k % RS]
                        index = PRO + USES * u + k
                        if kind == "split":
                            split_maxima(index, q + 1, chain, b)
                            continue
                        dve.wait_ge(row_full, index + 1)
                        if kind == "rows":
                            read_rows(slot, q + b[0], b[1]).then_inc(row_read, 1)
                        elif kind == "maxima":
                            take_maxima(slot, q + 1, 48 * (2 * i + (q + 1) // 2 + 1)).then_inc(row_read, 1)
                        else:
                            dve.sem_inc(acc_turned, 1)
                            take_output(slot, u, b).then_inc(row_read, 1)
                        k += 1
                    if general:
                        dve.wait_ge(exp_done, EXP0 + GROUPS * (NS * u + s + 1))
                        on = prob[:, s % RING_P, :, q0:BW]
                        if floor:
                            dve.wait_ge(floors_loaded, 16 * u + 16)
                            ins = nc.vector.scalar_tensor_tensor(on, on, 1.0, floors[:, :, qb * BW + q0:(qb + 1) * BW], ALU.min, ALU.max)
                        else:
                            ins = nc.vector.tensor_scalar(on, on, L["most"], L["least"], ALU.min, ALU.max)
                        ins.then_inc(clip_done, 1)
                assert chain.n == LINKS, (chain.n, LINKS)
            over_units(dve, body)
            dve.wait_ge(row_full, PRO + USES * UNITS + 1)
            take_output(row[0], UNITS, -1).then_inc(row_read, 1)


def attention_finish(nc, L, C, X, A, w):
    nm, floor = L["name"], L["floor"]
    with ExitStack() as ctx:
        sb = lambda name, shape, dt=F32: ctx.enter_context(nc.sbuf_tensor(nm + name, shape, dt))
        sem = semaphores(nc, ctx, nm + "finish_")
        psT = [ctx.enter_context(nc.psum_tensor(nm + f"psA{i}", [P, BW], F32)) for i in range(2)]
        psY = [ctx.enter_context(nc.psum_tensor(nm + f"psY{i}", [P, BW], F32)) for i in range(2)]
        rsum = sb("rsum", [P, 2, G, TB, HG])
        ao = sb("ao", [P, NB, TB, P])
        aoT = sb("aoT", [P, 2, BW])
        y = sb("y", [P, 2, BW])
        if floor:
            mass, share, whole = [sb(x, [P, G, TB, HG]) for x in ("mass", "share", "whole")]
            tail, num = sb("tail", [P, G, TB, HG, D]), sb("num", [P, G, TB, HG, D])
        divided, turned, aoT_ready = sem("divided"), sem("turned"), sem("aoT_ready")
        y_in_psum, y_read, y_biased, chain_sem = sem("y_in_psum"), sem("y_read"), sem("y_biased"), sem("chain")
        block = ctx.enter_context(nc.Block())

        @block.tensor
        def _(pe):
            def turn(n, p):
                pe.wait_ge(divided, n + 2)
                pe.wait_ge(aoT_ready, n + 1)
                for t in range(TB):
                    mm = pe.transpose(psT[p][:, t * P:(t + 1) * P], ao[:, n, t, :], C["ident"][:, :])
                mm.then_inc(turned, 1)

            def project(n, p):
                pe.wait_ge(aoT_ready, n + 3)
                pe.wait_ge(y_read, n + 1)
                for t in range(TB):
                    mm = pe.matmul(psY[p][:, t * P:(t + 1) * P], aoT[:, p, t * P:(t + 1) * P], w["o"][:, :], start=True, stop=True)
                mm.then_inc(y_in_psum, 1)

            for n in range(NB + 1):
                if n < NB:
                    turn(n, n % 2)
                if n > 0:
                    project(n - 1, (n - 1) % 2)

        @block.scalar
        def _(act):
            act.sem_inc(aoT_ready, 2)
            with act.Fori(0, NB // 2) as i:
                for p in range(2):
                    n = 2 * i + p
                    act.wait_ge(turned, n + 1)
                    act.wait_ge(y_read, n + 1)
                    nc.scalar.activation(aoT[:, p, :], psT[p][:, :], ACT.Copy).then_inc(aoT_ready, 1)

        @block.vector
        def _(dve):
            dve.sem_inc(y_read, 2)
            dve.sem_inc(divided, 1)
            LINKS = 8 if floor else 1

            def divide(n, p, i):
                chain = Chain(dve, chain_sem, LINKS * n)
                tiles = slice(p * TB, (p + 1) * TB)
                den = A["AO"][:, ds(i * G + 1, G), tiles, :, D]
                wide = lambda x: x.unsqueeze(3).broadcast_to([P, TB, HG, D])
                sums = lambda g: A["AO"][:, ds(i * G + 1 + g, 1), tiles, :, 0:D].rearrange("p u t j d -> p (u t) j d")
                dve.wait_ge(divided, n + 1)
                if floor:
                    low = A["LOW"][:, ds(i * G, G), :, tiles].rearrange("p g j t -> p g t j")
                    masked = A["masked"][:, tiles].unsqueeze(1).unsqueeze(3).broadcast_to([P, G, TB, HG])
                    chain.link(nc.vector.tensor_tensor(mass[:, :, :, :], low, masked, ALU.mult))
                    chain.link(nc.vector.tensor_tensor(mass[:, :, :, :], mass[:, :, :, :], den, ALU.add))
                    chain.link(nc.vector.tensor_scalar(share[:, :, :, :], mass[:, :, :, :], 1e-6, 1e-8, ALU.add, ALU.mult))
                    chain.link(nc.vector.scalar_tensor_tensor(whole[:, :, :, :], share[:, :, :, :], float(S), mass[:, :, :, :], ALU.mult, ALU.add))
                    nc.vector.reciprocal(rsum[:, p], whole[:, :, :, :])
                    for g in range(G):
                        lowest = A["LOW"][:, ds(i * G + g, 1), :, tiles].rearrange("p u j t -> p t (u j)")
                        suffix = A["SUF"][:, ds(i * G + 1 + g, 1), tiles, :].rearrange("p u t (j d) -> p (u t) j d", d=D)
                        ins = nc.vector.tensor_tensor(tail[:, g], wide(lowest), suffix, ALU.mult)
                    chain.link(ins)
                    for g in range(G):
                        ins = nc.vector.tensor_tensor(num[:, g], tail[:, g], sums(g), ALU.add)
                    chain.link(ins)
                    for g in range(G):
                        every = A["SUM"][:, ds(i * G + 1 + g, 1), :].rearrange("p u (j d) -> p u j d", d=D).broadcast_to([P, TB, HG, D])
                        ins = nc.vector.tensor_tensor(tail[:, g], wide(share[:, g]), every, ALU.mult)
                    chain.link(ins)
                    for g in range(G):
                        ins = nc.vector.tensor_tensor(num[:, g], num[:, g], tail[:, g], ALU.add)
                    chain.link(ins)
                else:
                    chain.link(nc.vector.reciprocal(rsum[:, p], den))
                for g in range(G):
                    out = ao[:, ds(n, 1), :, HG * D * g:HG * D * (g + 1)].rearrange("p a t (j d) -> p (a t) j d", d=D)
                    ins = nc.vector.tensor_tensor(out, num[:, g] if floor else sums(g), wide(rsum[:, p, g]), ALU.mult)
                ins.then_inc(divided, 1)
                assert chain.n == LINKS

            def add(n, p, i):
                dve.wait_ge(y_in_psum, n + 1)
                x = X[:, ds(n * TB, TB), :]
                ps = psY[p][:, :].rearrange("p (t e) -> p t e", t=TB)
                if w["bo"] is None:
                    nc.vector.tensor_tensor(x, ps, x, ALU.add).then_inc(y_read, 1)
                else:
                    nc.vector.tensor_tensor(y[:, p].rearrange("p (t e) -> p t e", t=TB), ps,
                                            w["bo"][:, :].unsqueeze(1).broadcast_to([P, TB, P]), ALU.add).then_inc(y_read, 1)
                    dve.wait_ge(y_read, n + 3)
                    nc.vector.tensor_tensor(x, y[:, p].rearrange("p (t e) -> p t e", t=TB), x, ALU.add).then_inc(y_biased, 1)

            for stage in (divide, add):
                with dve.Fori(0, NB // 2) as i:
                    for p in range(2):
                        stage(2 * i + p, p, i)


def attention(nc, L, C, X, weights, scratch, d):
    nm = L["name"]
    with ExitStack() as ctx:
        sb = lambda name, shape, dt=F32: ctx.enter_context(nc.sbuf_tensor(nm + name, shape, dt))
        A = {
            "Q": [sb(f"Q{b}", [P, HG, S], BF16) for b in range(RING_Q)],
            "K": [sb(f"K{b}", [P, HG, S], BF16) for b in range(RING_Q)],
            "V": [sb(f"V{b}", [P, KT, HG, VW]) for b in range(2)],
            "VR": sb("VR", [P, UNITS + 1, KT, HG * D]),
            "AO": sb("AO", [P, UNITS + 1, KT, HG, D + 1]),
        }
        w = {"loads": [], "bo": None}
        for name, (src, shape) in weights.items():
            w[name] = sb("w" + name, list(shape))
            w["loads"].append((w[name][:, :], src))
        if L["latent"]:
            w["fused"], w["both_r"] = sb("fused", [P, 3, P]), sb("both_r", [P, 2, R_ROWS])
            w.update({name: w["fused"][:, k, :] for k, name in enumerate("qkv")})
            w["r"], w["r_rot"] = w["both_r"][:, 0, :], w["both_r"][:, 1, :]
            w["loads"] += [(w["r"][:, P // 2:R_ROWS], d["b0_kr"]), (w["r_rot"][:, P // 2:R_ROWS], d["b0_krr"])]
        if L["tables"]:
            rows = d[L["tables"]].shape[0]
            C = dict(C)
            C[L["tables"]] = sb("table", [rows, 2, S])
            w["loads"].append((C[L["tables"]][:, :, :], d[L["tables"]]))
        if L["floor"]:
            A.update({"SUF": sb("SUF", [P, UNITS + 1, KT, 32]), "SUM": sb("SUM", [P, UNITS + 1, 32]), "masked": sb("masked", [P, KT]),
                      "LOW": sb("LOW", [P, UNITS, HG, KT]),
                      "peak": sb("peak", [H, 2, NB]), "clip_bias": sb("clip_bias", [P, 1]), "may_clip": sb("may_clip", [1, 1], I32)})
        attention_prepare(nc, L, C, X, A, w, scratch)
        if L["floor"]:
            masked_sums(nc, L, C, A, d)
        attention_core(nc, L, C, A, scratch)
        attention_finish(nc, L, C, X, A, w)



FFN = {
    "f0": dict(gated=15, experts=16, chunks=1, act=ACT.Relu, top=3, ring=8, lag=4),
    "f1": dict(gated=8, experts=9, chunks=4, act=ACT.Gelu_apprx_tanh, chosen=2 * B * S, ring=6, lag=4),
}
DIGITS, UNROLL = 15, 3
GW = 16


def route(nc, nm, F, C, X, R, w):
    ne, top = F["gated"], F.get("top")
    LW = 24 if top else ne
    NCOL = ne * NT
    with ExitStack() as ctx:
        sb = lambda name, shape, dt=F32: ctx.enter_context(nc.sbuf_tensor(nm + name, shape, dt))
        sem = semaphores(nc, ctx, nm + "route_")
        bank = lambda name: ctx.enter_context(nc.psum_tensor(nm + name, [P, BW], F32))
        T = [sb("stats", [P, NT, 6])] + [sb(n, [P, NT]) for n in ("mean", "sd", "rstd", "t1", "t2")]
        _, mean, sd, rstd, t1, _ = T
        xn, xs = sb("xn", [P, 2, TB, P]), sb("xs", [P, 2, BW])
        logits, ex = sb("logits", [P, NT, LW]), sb("ex", [P, NT, ne])
        gate, pieces = sb("gate", [P, NT, GW]), sb("pieces", [P, NT, P], BF16)
        most, total, inv = sb("most", [P, NT]), sb("total", [P, NT]), sb("inv", [P, NT])
        if top:
            best, wanted, marked = sb("best", [P, NT, 8]), sb("wanted", [P, NT, 8]), sb("marked", [P, NT, LW])
        else:
            score = sb("score", [P, ne, NT])
            over, same, pick = sb("over", [P, NCOL]), sb("same", [P, NCOL]), sb("picked", [P, NCOL])
            run = [sb("run0", [P, NCOL]), sb("run1", [P, NCOL])]
            ones, above = sb("ones", [P, P]), sb("above", [P, P])
            limit, grow = [sb(n, [P, 1], I32) for n in ("limit", "grow")]
            trial, digits = sb("trial", [P, 3], I32), sb("digits", [P, DIGITS, 3], I32)
            count, reach, reached, room = sb("count", [P, 3]), sb("reach", [P, 3]), sb("reached", [P, 1]), sb("room", [P, 1])
        psT, psR, psG = [bank("psT0"), bank("psT1")], [bank("psR0"), bank("psR1")], [bank("psG0"), bank("psG1")]
        psN = bank("psN")
        rest = sb("rest", [P, 2, NT, GW])
        w_ready, var_ready, sd_ready = sem("w_ready"), sem("var_ready"), sem("sd_ready")
        xn_ready, xT_in_psum, xs_ready, XT_ready = sem("xn_ready"), sem("xT_in_psum"), sem("xs_ready"), sem("XT_ready")
        XT_high, w_high, w_low, staged = sem("XT_high"), sem("w_high"), sem("w_low"), sem("staged")
        stage = sb("stage", [P, F["experts"] * F["chunks"] * P])
        lg_in_psum, lg_ready = sem("lg_in_psum"), sem("lg_ready")
        b2_ready = sem("b2_ready")
        dif_ready, ex_ready, preset = sem("dif_ready"), sem("ex_ready"), sem("preset")
        counted, summed = sem("counted"), sem("summed")
        pieces_ready, gt_in_psum, gt_ready = sem("pieces_ready"), sem("gt_in_psum"), sem("gt_ready")
        same_ready, ranked = sem("same_ready"), sem("ranked")
        chain_sem, loop_sem = sem("chain"), sem("loop")
        block = ctx.enter_context(nc.Block())

        @block.sync
        def _(sp):
            for dst, src in w["loads"]:
                sp.dma_start(dst, src).then_inc(w_ready, 16)
            sp.dma_start(stage[:, :], w["W1"]).then_inc(staged, 16)
            sp.wait_ge(w_low, 1)
            sp.dma_start(stage[:, :], w["W2"]).then_inc(staged, 16)
            sp.wait_ge(staged, 32)

        @block.gpsimd
        def _(pool):
            nc.gpsimd.memset(pieces[:, :, :].bitcast(I32), 0)
            nc.gpsimd.memset(w["b2r"][:, :], 0.0)
            nc.gpsimd.memset(gate[:, :, :], 0.0).then_inc(preset, 1)
            pool.wait_ge(preset, 1)
            ins = nc.gpsimd.memset(gate[:, :, ne:ne + 1], 1.0)
            if top:
                for c in range(ne, LW):
                    nc.gpsimd.memset(logits[:, :, c:c + 1], NEG * c)
                for c in range(top, 8):
                    ins = nc.gpsimd.memset(wanted[:, :, c:c + 1], NEG * (ne + c - top))
            ins.then_inc(preset, 1)
            pool.wait_ge(preset, 2)
            for c in range(3):
                pool.dma_start(w["b2r"][GW * c:GW * c + F["experts"], :], w["b2"]).then_inc(b2_ready, 16)
            def rest_of_weights(k, name):
                pool.wait_ge(w_high, k + 1)
                nc.gpsimd.tensor_tensor(w[name + "l"], stage[:, :], w[name + "h"].bitcast(F32), ALU.subtract).then_inc(w_low, 1)

            rest_of_weights(0, "W1")
            pool.sem_inc(XT_ready, 2)
            with pool.Fori(0, NB // 2) as i:
                for p in range(2):
                    n = 2 * i + p
                    pool.wait_ge(XT_high, n + 1)
                    nc.gpsimd.tensor_tensor(R["XTl"][:, ds(n * BW, BW)], xs[:, p, :], R["XTh"][:, ds(n * BW, BW)].bitcast(F32), ALU.subtract).then_inc(XT_ready, 1)
            rest_of_weights(1, "W2")

        @block.tensor
        def _(pe):
            pe.wait_ge(w_ready, 16 * len(w["loads"]))

            def turn(n, p, i):
                pe.wait_ge(xn_ready, n + 1)
                pe.wait_ge(xs_ready, n + 1)
                for t in range(TB):
                    mm = pe.transpose(psT[p][:, t * P:(t + 1) * P], xn[:, p, t, :], C["ident"][:, :])
                mm.then_inc(xT_in_psum, 1)

            def find_logits(n, p, i):
                pe.wait_ge(xs_ready, n + 3)
                pe.wait_ge(lg_ready, n + 1)
                for t in range(TB):
                    mm = pe.matmul(psR[p][:, t * GW:t * GW + ne], xs[:, p, t * P:(t + 1) * P], w["router"][:, :], start=True, stop=True)
                mm.then_inc(lg_in_psum, 1)

            over_blocks(pe, find_logits, turn, nothing)
            if not top:
                with pe.Fori(0, DIGITS) as i:
                    pe.wait_ge(counted, i + 1)
                    pe.matmul(psN[:, 0:3], ones[:, :], count[:, :], start=True, stop=True).then_inc(summed, 1)
                pe.wait_ge(counted, DIGITS + 1)
                pe.matmul(psN[:, 0:1], ones[:, :], count[:, 0:1], start=True, stop=True).then_inc(summed, 1)
                pe.wait_ge(same_ready, 1)
                pe.matmul(psR[0][:, 0:NCOL], above[:, :], same[:, :], start=True, stop=True).then_inc(ranked, 1)
                pe.matmul(psR[1][:, 0:NCOL], ones[:, :], same[:, :], start=True, stop=True).then_inc(ranked, 1)
            pe.wait_ge(pieces_ready, 1)
            for n in range(NB):
                if n >= 2:
                    pe.wait_ge(gt_ready, n - 1)
                for t in range(TB):
                    mm = pe.transpose(psG[n % 2][:, t * P // 2:(t + 1) * P // 2].bitcast(BF16), pieces[:, n * TB + t, :], C["ident16"][:, :])
                mm.then_inc(gt_in_psum, 1)

        @block.scalar
        def _(act):
            act.wait_ge(var_ready, 1)
            nc.scalar.activation(sd[:, :], t1[:, :], ACT.Sqrt, bias=C["eps"][:, 0:1]).then_inc(sd_ready, 1)
            act.wait_ge(dif_ready, 1)
            nc.scalar.activation(ex[:, :, :], ex[:, :, :], ACT.Exp).then_inc(ex_ready, 1)
            for n in range(NB):
                act.wait_ge(gt_in_psum, n + 1)
                nc.scalar.activation(R["GT"][:, n * BW:(n + 1) * BW], psG[n % 2][:, 0:BW // 2].bitcast(BF16), ACT.Copy).then_inc(gt_ready, 1)

        @block.vector
        def _(dve):
            chain = Chain(dve, chain_sem)
            dve.sem_inc(xs_ready, 2)
            dve.sem_inc(lg_ready, 2)
            layernorm_all(nc, X, C, dve, var_ready, sd_ready, chain, T)
            dve.wait_ge(w_ready, 16 * len(w["loads"]))
            dve.wait_ge(staged, 16)
            nc.vector.tensor_copy(w["W1h"], stage[:, :]).then_inc(w_high, 1)
            dve.wait_ge(preset, 2)
            dve.wait_ge(b2_ready, 48)

            def normalise(n, p, i):
                dve.wait_ge(xs_ready, n + 1)
                for t in range(TB):
                    ins = nc.vector.tensor_scalar(xn[:, p, t, :], X[:, ds(n * TB + t, 1), :].rearrange("p a e -> p (a e)"),
                                                  mean[:, ds(n * TB + t, 1)], rstd[:, ds(n * TB + t, 1)], ALU.subtract, ALU.mult)
                ins.then_inc(xn_ready, 1)

            def keep(n, p, i):
                dve.wait_ge(xT_in_psum, n + 1)
                dve.wait_ge(XT_ready, n + 1)
                nc.vector.tensor_copy(xs[:, p, :], psT[p][:, :]).then_inc(xs_ready, 1)
                dve.wait_ge(xs_ready, n + 3)
                nc.vector.tensor_copy(R["XTh"][:, ds(n * BW, BW)], xs[:, p, :]).then_inc(XT_high, 1)

            def take_logits(n, p, i):
                dve.wait_ge(lg_in_psum, n + 1)
                lg = psR[p][:, 0:TB * GW].rearrange("p (t e) -> p t e", t=TB)[:, :, 0:ne]
                dst = logits[:, ds(n * TB, TB), 0:ne]
                if top:
                    nc.vector.tensor_tensor(dst, lg, w["br"][:, :].unsqueeze(1).broadcast_to([P, TB, ne]), ALU.add).then_inc(lg_ready, 1)
                else:
                    nc.vector.tensor_scalar(dst, lg, 1.0, None, ALU.mult).then_inc(lg_ready, 1)

            over_blocks(dve, keep, normalise, take_logits)
            dve.wait_ge(staged, 32)
            nc.vector.tensor_copy(w["W2h"], stage[:, :]).then_inc(w_high, 1)
            dve.wait_ge(lg_ready, NB + 2)
            wide = lambda x, k: x.unsqueeze(2).broadcast_to([P, NT, k])
            chain.link(nc.vector.tensor_reduce(most[:, :], logits[:, :, 0:ne], AX_X, ALU.max))
            nc.vector.tensor_tensor(ex[:, :, :], logits[:, :, 0:ne], wide(most[:, :], ne), ALU.subtract).then_inc(dif_ready, 1)
            if top:
                for t in range(NT):
                    ins = nc.vector.max(best[:, t, :], logits[:, t, :])
                chain.link(ins)
                chain.link(nc.vector.tensor_copy(wanted[:, :, 0:top], best[:, :, 0:top]))
                for t in range(NT):
                    ins = nc.vector.match_replace(marked[:, t, :], wanted[:, t, :], logits[:, t, :], -NEG)
                chain.link(ins)
            dve.wait_ge(ex_ready, 1)
            chain.link(nc.vector.tensor_reduce(total[:, :], ex[:, :, :], AX_X, ALU.add))
            chain.link(nc.vector.reciprocal(inv[:, :], total[:, :]))
            if top:
                chain.link(nc.vector.tensor_tensor(ex[:, :, :], ex[:, :, :], wide(inv[:, :], ne), ALU.mult))
                chain.link(nc.vector.scalar_tensor_tensor(gate[:, :, 0:ne], marked[:, :, 0:ne], -NEG, ex[:, :, :], ALU.is_ge, ALU.mult))
            else:
                chain.link(nc.vector.tensor_tensor(score[:, :, :].rearrange("p e t -> p t e"), ex[:, :, :], wide(inv[:, :], ne), ALU.mult))
                flat = score[:, :, :].rearrange("p e t -> p (e t)")
                chain.step(nc.vector.memset(ones[:, :], 1.0))
                chain.step(nc.vector.tensor_scalar(above[:, :], C["mask"][:, :], -1.0, None, ALU.is_lt))
                chain.step(nc.vector.tensor_copy(digits[:, :, :], w["digits"][:, :, :]))
                chain.link(nc.vector.memset(limit[:, :], 0))
                LINKS = 4
                with dve.Fori(0, DIGITS // UNROLL) as r:
                    for k in range(UNROLL):
                        i = UNROLL * r + k
                        inner = Chain(dve, loop_sem, LINKS * i)
                        inner.link(nc.vector.tensor_tensor(trial[:, :].unsqueeze(1), limit[:, :].unsqueeze(1).broadcast_to([P, 1, 3]),
                                                           digits[:, ds(i, 1), :], ALU.bitwise_or))
                        for c in range(3):
                            ins = nc.vector.tensor_scalar((over, same, pick)[c][:, :], flat, trial[:, c:c + 1].bitcast(F32), 0.0, ALU.is_ge, ALU.add,
                                                          accum_out=count[:, c:c + 1])
                        ins.then_inc(counted, 1)
                        dve.wait_ge(summed, i + 1)
                        inner.link(nc.vector.tensor_scalar(reach[:, :], psN[:, 0:3], float(F["chosen"]), 0.0, ALU.is_ge, ALU.add,
                                                           accum_out=reached[:, :]))
                        inner.link(nc.vector.tensor_tensor(grow[:, :].unsqueeze(1), reached[:, :].unsqueeze(1),
                                                           w["digits"][:, ds(i, 1), 0:1], ALU.mult))
                        inner.link(nc.vector.tensor_tensor(limit[:, :], limit[:, :], grow[:, :], ALU.bitwise_or))
                        assert inner.n == LINKS
                at = limit[:, :].bitcast(F32)
                nc.vector.tensor_scalar(over[:, :], flat, at, 0.0, ALU.is_gt, ALU.add, accum_out=count[:, 0:1]).then_inc(counted, 1)
                nc.vector.tensor_scalar(same[:, :], flat, at, None, ALU.is_equal).then_inc(same_ready, 1)
                dve.wait_ge(summed, DIGITS + 1)
                chain.link(nc.vector.tensor_scalar(room[:, :], psN[:, 0:1], -1.0, float(F["chosen"]), ALU.mult, ALU.add))
                dve.wait_ge(ranked, 2)
                chain.link(nc.vector.tensor_copy(run[0][:, :], psR[1][:, 0:NCOL]))
                width, a = 1, 0
                while width < NCOL:
                    chain.step(nc.vector.tensor_copy(run[1 - a][:, 0:width], run[a][:, 0:width]))
                    chain.link(nc.vector.tensor_tensor(run[1 - a][:, width:], run[a][:, width:], run[a][:, 0:NCOL - width], ALU.add))
                    width, a = 2 * width, 1 - a
                chain.link(nc.vector.tensor_tensor(pick[:, :], run[a][:, :], psR[1][:, 0:NCOL], ALU.subtract))
                chain.link(nc.vector.tensor_tensor(pick[:, :], pick[:, :], psR[0][:, 0:NCOL], ALU.add))
                chain.link(nc.vector.scalar_tensor_tensor(pick[:, :], pick[:, :], room[:, 0:1], same[:, :], ALU.is_lt, ALU.mult))
                chain.link(nc.vector.tensor_tensor(pick[:, :], pick[:, :], over[:, :], ALU.add))
                chain.link(nc.vector.tensor_tensor(gate[:, :, 0:ne], pick[:, :].rearrange("p (e t) -> p t e", e=ne),
                                                   score[:, :, :].rearrange("p e t -> p t e"), ALU.mult))
            cut = lambda c: pieces[:, :, GW * c:GW * (c + 1)]
            chain.link(nc.vector.tensor_copy(cut(0), gate[:, :, :]))
            chain.link(nc.vector.tensor_tensor(rest[:, 0], gate[:, :, :], cut(0), ALU.subtract))
            chain.link(nc.vector.tensor_copy(cut(1), rest[:, 0]))
            nc.vector.tensor_tensor(cut(2), rest[:, 0], cut(1), ALU.subtract).then_inc(pieces_ready, 1)
            b2p, b2f = R["b2p"], w["b2r"]
            chain.link(nc.vector.tensor_copy(b2p[:, 0, :], b2f[:, :]))
            chain.link(nc.vector.tensor_tensor(b2f[:, :], b2f[:, :], b2p[:, 0, :], ALU.subtract))
            chain.link(nc.vector.tensor_copy(b2p[:, 1, :], b2f[:, :]))
            chain.step(nc.vector.tensor_tensor(b2p[:, 2, :], b2f[:, :], b2p[:, 1, :], ALU.subtract))
            chain.step(nc.vector.tensor_copy(R["spread"][:, :, :], w["pick"][:, :].unsqueeze(2).broadcast_to([P, GW, P])))


def experts(nc, nm, F, C, X, R, w):
    chunks, fn, RH = F["chunks"], F["act"], F["ring"]
    pairs = [(e, c) for e in range(F["experts"]) for c in range(chunks)]
    NP, NE, LAG = len(pairs), F["experts"], F["lag"]
    RA = 4
    TURN = LAG + 3
    with ExitStack() as ctx:
        sb = lambda name, shape, dt=F32: ctx.enter_context(nc.sbuf_tensor(nm + name, shape, dt))
        sem = semaphores(nc, ctx, nm + "experts_")
        bank = lambda name: ctx.enter_context(nc.psum_tensor(nm + name, [P, BW], F32))
        psH, psG, psY, psT = [bank("psH0"), bank("psH1")], [bank("psS0"), bank("psS1")], [bank("psY0"), bank("psY1")], bank("psX")
        h, hs, yS = sb("h", [P, RA, BW]), sb("hs", [P, RA, BW]), sb("yS", [P, 2, BW])
        high, low = sb("high", [P, RH, BW], F32R), sb("low", [P, RH, BW], F32R)
        h_full, h_ready, g_full, g_used, hs_ready = [sem(x) for x in ("h_full", "h_ready", "g_full", "g_used", "hs_ready")]
        high_ready, low_ready, y_done = [sem(x) for x in ("high_ready", "low_ready", "y_done")]
        y_copied, y_turned, x_added = [sem(x) for x in ("y_copied", "y_turned", "x_added")]
        block = ctx.enter_context(nc.Block())

        def over_pairs(eng, pair):
            for k in range(TURN):
                pair(0, 0, k)

            def rest_of(n, p):
                for k in range(TURN, NP):
                    pair(n, p, k)
                return n + 1, 1 - p

            with eng.Fori(0, NB // 2 - 1) as i:
                for p in range(2):
                    n, q = rest_of(2 * i + p, p)
                    for k in range(TURN):
                        pair(n, q, k)
            n, q = rest_of(NB - 2, 0)
            for k in range(TURN):
                pair(n, q, k)
            rest_of(n, q)

        def first(n):
            return isinstance(n, int) and n == 0

        @block.tensor
        def _(pe):
            pe.sem_inc(y_done, RH)

            def out(n, p, k):
                if k == 0:
                    pe.wait_ge(y_copied, n + 1)
                    for b in range(3):
                        pe.matmul(psY[p][:, :], R["b2p"][:, b, :], R["GT"][:, ds(n * BW, BW)], start=b == 0, stop=False)
                pe.wait_ge(low_ready, NP * n + k + 1 + RA)
                at = slice(k * P, (k + 1) * P)
                matmul_split(pe, psY[p][:, :], (w["W2h"][:, at], w["W2l"][:, at]), (high[:, k % RH, :], low[:, k % RH, :]),
                             start=False, stop=k == NP - 1).then_inc(y_done, 1)

            def turn(p, n):
                pe.wait_ge(y_copied, n + 2)
                pe.wait_ge(x_added, n + 1)
                for t in range(TB):
                    mm = pe.transpose(psT[:, t * P:(t + 1) * P], yS[:, 1 - p, t * P:(t + 1) * P], C["ident"][:, :])
                mm.then_inc(y_turned, 1)

            def pair(n, p, k):
                e, c = pairs[k]
                here = ds(n * BW, BW)
                pe.wait_ge(h_ready, NP * n + k + 1)
                at = slice(k * P, (k + 1) * P)
                matmul_split(pe, psH[k % 2][:, :], (w["W1h"][:, at], w["W1l"][:, at]), (R["XTh"][:, here], R["XTl"][:, here]),
                             start=True, stop=True).then_inc(h_full, 1)
                if c == 0:
                    pe.wait_ge(g_used, NE * n + e + 1)
                    pe.matmul(psG[(NE * p + e) % 2][:, :], R["spread"][:, e, :], R["GT"][:, here], start=True, stop=True).then_inc(g_full, 1)
                if k >= LAG:
                    out(n, p, k - LAG)
                elif not first(n):
                    out(n - 1, 1 - p, NP + k - LAG)
                if k == LAG + 1 and not first(n):
                    turn(p, n)

            over_pairs(pe, pair)
            for k in range(NP - LAG, NP):
                out(NB - 1, 1, k)
            turn(0, NB)

        @block.scalar
        def _(act):
            act.sem_inc(h_ready, 2)
            act.sem_inc(y_copied, 2)

            def copy(n, p):
                act.wait_ge(y_done, NP * n + RH)
                act.wait_ge(x_added, n)
                nc.scalar.activation(yS[:, 1 - p, :], psY[1 - p][:, :], ACT.Copy).then_inc(y_copied, 1)

            def pair(n, p, k):
                act.wait_ge(h_full, NP * n + k + 1)
                act.wait_ge(hs_ready, NP * n + k + 1)
                nc.scalar.activation(h[:, k % RA, :], psH[k % 2][:, :], fn, bias=w["b1"][:, k:k + 1]).then_inc(h_ready, 1)
                if k == LAG and not first(n):
                    copy(n, p)

            over_pairs(act, pair)
            copy(NB, 0)

        @block.vector
        def _(dve):
            dve.sem_inc(hs_ready, RA)
            dve.sem_inc(g_used, 2)
            dve.sem_inc(x_added, 2)

            def take_high(n, k):
                dve.wait_ge(hs_ready, NP * n + k + 1 + RA)
                if pairs[k][1] == chunks - 1:
                    dve.sem_inc(g_used, 1)
                dve.wait_ge(y_done, NP * n + k + 1)
                nc.vector.tensor_copy(high[:, k % RH, :], hs[:, k % RA, :]).then_inc(high_ready, 1)

            def add(n):
                dve.wait_ge(y_turned, n)
                xt = X[:, ds((n - 1) * TB, TB), :]
                nc.vector.tensor_tensor(xt, psT[:, :].rearrange("p (t e) -> p t e", t=TB), xt, ALU.add).then_inc(x_added, 1)

            def pair(n, p, k):
                e, _ = pairs[k]
                dve.wait_ge(h_ready, NP * n + k + 3)
                dve.wait_ge(low_ready, NP * n + k + 1)
                dve.wait_ge(g_full, NE * n + e + 1)
                nc.vector.tensor_tensor(hs[:, k % RA, :], h[:, k % RA, :], psG[(NE * p + e) % 2][:, :], ALU.mult).then_inc(hs_ready, 1)
                if k > 0:
                    take_high(n, k - 1)
                elif not first(n):
                    take_high(n - 1, NP - 1)
                if k == LAG + 2 and not first(n):
                    add(n)

            over_pairs(dve, pair)
            take_high(NB - 1, NP - 1)
            add(NB)

        @block.gpsimd
        def _(pool):
            pool.sem_inc(low_ready, RA)
            with pool.Fori(0, NB) as n:
                for k in range(NP):
                    pool.wait_ge(high_ready, NP * n + k + 1)
                    nc.gpsimd.tensor_tensor(low[:, k % RH, :], hs[:, k % RA, :], high[:, k % RH, :].bitcast(F32), ALU.subtract).then_inc(low_ready, 1)


def feed_forward(nc, kind, nm, C, X, d):
    F = FFN[kind]
    with ExitStack() as ctx:
        sb = lambda name, shape, dt=F32: ctx.enter_context(nc.sbuf_tensor(nm + name, shape, dt))
        ne, ch = F["gated"], F["chunks"]
        R = {"XTh": sb("XTh", [P, B * S], F32R), "XTl": sb("XTl", [P, B * S], F32R), "GT": sb("GT", [P, B * S], BF16),
             "b2p": sb("b2p", [P, 3, P], BF16), "spread": sb("spread", [P, GW, P], BF16)}
        hidden = F["experts"] * ch * P
        w = {n: sb(n, [P, hidden], F32R)[:, :] for n in ("W1h", "W1l", "W2h", "W2l")}
        w.update({"b1": sb("b1", [P, F["experts"] * ch]), "b2r": sb("b2r", [P, P]), "pick": sb("pick", [P, GW]),
                  "router": sb("router", [P, ne]), "b2": d[kind + "_b2"],
                  "W1": d[kind + "_W1"].rearrange("p e f -> p (e f)"), "W2": d[kind + "_W2"].rearrange("p e c f -> p (e c f)")})
        w["loads"] = [(w["router"][:, :], d[kind + "_router"]), (w["pick"][:, :], d["pick"]), (w["b1"][:, :], d[kind + "_b1"])]
        if "top" in F:
            w["br"] = sb("br", [P, ne])
            w["loads"].append((w["br"][:, :], d[kind + "_br"].broadcast_to([P, ne])))
        else:
            w["digits"] = sb("digits_f", [P, DIGITS, 3])
            w["loads"].append((w["digits"][:, :, :], d["digits"].broadcast_to([P, DIGITS, 3])))
        route(nc, nm, F, C, X, R, w)
        experts(nc, nm, F, C, X, R, w)


LAYERS = {
    "a0": dict(name="a0_", causal=True, max=True, scale=float(D) ** -0.5, clip=None, floor=False,
               rope=None, bias=True, latent=False, suffix=False, tables=None),
    "b0": dict(name="b0_", causal=True, max=False, scale=float(D + D // 2) ** -0.5, clip=80.0, floor=False,
               rope="pairs", bias=False, latent=True, suffix=False, tables="pairs",
               most=float(np.exp(80.0 / np.sqrt(12.0))), least=float(np.exp(-80.0 / np.sqrt(12.0)))),
    "a1": dict(name="a1_", causal=True, max=True, scale=float(D) ** -0.5, clip=100.0, floor=True,
               rope=None, bias=False, latent=False, suffix=True, tables=None),
    "b1": dict(name="b1_", causal=False, max=True, scale=float(D) ** -0.5, clip=None, floor=False,
               rope="half", bias=False, latent=False, suffix=False, tables="half"),
}


def weights_of(kind, d):
    sq = (P, P)
    if kind == "a0":
        return {"q": (d["a0_wq"], sq), "k": (d["a0_wk"], sq), "v": (d["a0_wv"], sq), "o": (d["a0_wo"], sq),
                "bq": (d["a0_bq"], (P, 1)), "bk": (d["a0_bk"], (P, 1)),
                "bv": (d["a0_bv"].broadcast_to([P, P]), sq), "bo": (d["a0_bo"].broadcast_to([P, P]), sq)}
    if kind == "b0":
        up, rotary = (LATENT, P), (LATENT, P // 2)
        return {"down_q": (d["b0_dq"], up), "down_kv": (d["b0_dkv"], up), "uq": (d["b0_wq"], up), "uk": (d["b0_wk"], up),
                "uv": (d["b0_wv"], up), "uqr": (d["b0_qr"], rotary), "uqr_rot": (d["b0_qrr"], rotary), "o": (d["b0_wo"], sq)}
    if kind == "a1":
        return {**{n: (d["a1_w" + n], sq) for n in "qkvo"}, "heads": (d["heads"], (P, H))}
    return {"q": (d["b1_wq"], sq), "q_rot": (d["b1_wqr"], sq), "k": (d["b1_wk"], sq), "k_rot": (d["b1_wkr"], sq),
            "v": (d["b1_wv"], sq), "o": (d["b1_wo"], sq), "bo": (d["b1_bo"].broadcast_to([P, P]), sq)}


STAGES = ("a0", "f0", "b0", "f0", "a1", "f1", "b1", "f1")


def build(nc, d, out, stages=STAGES):
    scratch = {
        "q": nc.dram_tensor("scratch_q", [UNITS + 2, 32, 3, S], BF16, kind="Internal").ap(),
        "k": nc.dram_tensor("scratch_k", [UNITS + 2, 32, 3, S], BF16, kind="Internal").ap(),
        "qr": nc.dram_tensor("scratch_qr", [UNITS + 2, 16, 3, S], BF16, kind="Internal").ap(),
        "kr": nc.dram_tensor("scratch_kr", [B + 1, D // 2, 3, S], BF16, kind="Internal").ap(),
    }
    scratch["low"] = nc.dram_tensor("scratch_low", [2, HG, KT, P], F32, kind="Internal").ap()
    with ExitStack() as ctx:
        sb = lambda name, shape, dt=F32: ctx.enter_context(nc.sbuf_tensor(name, shape, dt))
        X = sb("X", [P, NT, P])
        C = {"ident": sb("ident", [P, P]), "ident16": sb("ident16", [P, P], BF16),
             "mask": sb("mask", [P, P]), "mask16": sb("mask16", [P, P], BF16), "eps": sb("eps", [P, 1])}
        x_loaded, c_loaded, c_ready, x_stored = [nc.alloc_semaphore(n) for n in ("x_loaded", "c_loaded", "c_ready", "x_stored")]
        with nc.Block() as block:
            @block.sync
            def _(sp):
                sp.dma_start(X[:, :, :], d["x"].rearrange("(t p) e -> p t e", p=P)).then_inc(x_loaded, 16)
                sp.dma_start(C["ident"][:, :], d["ident"]).then_inc(c_loaded, 16)
                sp.dma_start(C["mask"][:, :], d["mask"]).then_inc(c_loaded, 16)
                sp.wait_ge(x_loaded, 16)

            @block.vector
            def _(dve):
                nc.vector.memset(C["eps"][:, :], LN_EPS).then_inc(c_ready, 1)
                dve.wait_ge(c_loaded, 32)
                nc.vector.tensor_copy(C["ident16"][:, :], C["ident"][:, :]).then_inc(c_ready, 1)
                nc.vector.tensor_copy(C["mask16"][:, :], C["mask"][:, :]).then_inc(c_ready, 1)

        for n, kind in enumerate(stages):
            if kind in LAYERS:
                attention(nc, LAYERS[kind], C, X, weights_of(kind, d), scratch, d)
            else:
                feed_forward(nc, kind, f"{kind}{n}_", C, X, d)
        with nc.Block() as block:
            @block.sync
            def _(sp):
                sp.dma_start(out.rearrange("(t p) e -> p t e", p=P), X[:, :, :]).then_inc(x_stored, 16)
                sp.wait_ge(x_stored, 16)


def laid_out(inputs):
    f = np.float32
    a = {k: np.asarray(v) for k, v in inputs.items()}
    d = {"x": a["L0_attn_a_x"].reshape(B * S, E)}
    d["ident"] = np.eye(P, dtype=f)
    d["mask"] = np.where(np.arange(P)[None, :] > np.arange(P)[:, None], f(NEG), f(0))
    w1 = a["L0_attn_a_W1"].reshape(E, H, 3, D)
    b1 = a["L0_attn_a_b1"].reshape(H, 3, D)
    for i, n in enumerate("qkv"):
        d["a0_w" + n] = w1[:, :, i].reshape(E, P)
    d["a0_bq"], d["a0_bk"], d["a0_bv"] = b1[:, 0].reshape(P, 1), b1[:, 1].reshape(P, 1), b1[:, 2].reshape(1, P)
    d["a0_wo"], d["a0_bo"] = a["L0_attn_a_Wp"], a["L0_attn_a_bp"].reshape(1, P)
    d["b0_dq"], d["b0_dkv"] = a["L0_attn_b_W_DQ"].T, a["L0_attn_b_W_DKV"].T
    d["b0_wq"], d["b0_wk"], d["b0_wv"] = a["L0_attn_b_W_UQ"], a["L0_attn_b_W_UK"], a["L0_attn_b_W_UV"]
    d["b0_wo"] = a["L0_attn_b_W_O"]
    pairs = lambda w: w.reshape(w.shape[0], -1, 2)[:, :, ::-1].reshape(w.shape)
    d["b0_qr"], d["b0_kr"] = a["L0_attn_b_W_QR"], a["L0_attn_b_W_KR"]
    d["b0_qrr"], d["b0_krr"] = pairs(d["b0_qr"]), pairs(d["b0_kr"])
    wt = a["L1_attn_a_w_qkv"].T
    for i, n in enumerate("qkv"):
        d["a1_w" + n] = wt[:, i * P:(i + 1) * P]
    d["a1_wo"] = a["L1_attn_a_w_proj"].T
    halves = lambda w: w.reshape(E, H, 2, D // 2)[:, :, ::-1].reshape(E, P)
    for i, n in enumerate("qkv"):
        d["b1_w" + n] = a["L1_attn_b_w_qkv"][:, i * P:(i + 1) * P]
    d["b1_wqr"], d["b1_wkr"] = halves(d["b1_wq"]), halves(d["b1_wk"])
    d["b1_wo"], d["b1_bo"] = a["L1_attn_b_w_out"], a["L1_attn_b_b_out"].reshape(1, P)
    d["heads"] = (np.arange(P)[:, None] // D == np.arange(H)[None, :]).astype(f)
    d["masked"] = (S - 1 - np.arange(KT)[None, :] * P - np.arange(P)[:, None]).astype(f)
    ew = lambda x, y: np.concatenate([x, y[None]], 0)
    for kind, ws in (("f0", ("L0_ffn_eW1", "L0_ffn_sW1", "L0_ffn_eb1", "L0_ffn_sb1", "L0_ffn_eW2", "L0_ffn_sW2", "L0_ffn_eb2", "L0_ffn_sb2")),
                     ("f1", ("L1_ffn_W1", "L1_ffn_Ws1", "L1_ffn_b1", "L1_ffn_bs1", "L1_ffn_W2", "L1_ffn_Ws2", "L1_ffn_b2", "L1_ffn_bs2"))):
        W1, b1, W2, b2 = (ew(a[ws[2 * i]], a[ws[2 * i + 1]]) for i in range(4))
        ex, ch = W1.shape[0], W1.shape[2] // P
        d[kind + "_W1"] = W1.transpose(1, 0, 2)
        d[kind + "_W2"] = W2.reshape(ex, ch, P, P).transpose(2, 0, 1, 3)
        d[kind + "_b1"] = b1.reshape(ex * ch, P).T
        d[kind + "_b2"] = b2
    d["f0_router"], d["f0_br"] = a["L0_ffn_router_W"], a["L0_ffn_router_b"].reshape(1, -1)
    d["f1_router"] = a["L1_ffn_gate_weight"].T
    d["digits"] = (f(4) ** np.arange(DIGITS - 1, -1, -1, dtype=f)[:, None] * np.arange(1, 4, dtype=f)[None, :])[None]
    r = np.arange(P)[:, None]
    d["pick"] = ((r % GW == np.arange(GW)[None, :]) & (r < 3 * GW)).astype(f)
    pos = np.arange(S, dtype=f)
    inv = f(10000.0) ** (-np.arange(0, 4, 2, dtype=f) / f(4))
    ang = pos[None, :] * inv[:, None]
    r = np.arange(R_ROWS)
    d["pairs"] = np.stack([np.cos(ang)[(r % 4) // 2], np.sin(ang)[(r % 4) // 2] * np.where(r % 2 == 0, f(-1), f(1))[:, None]], 1)
    theta = f(1.0) / f(10000.0) ** (np.arange(0, D, 2, dtype=f) / f(D))
    ang = pos[None, :] * theta[:, None]
    r = np.arange(P)
    d["half"] = np.stack([np.cos(ang)[r % 4], np.sin(ang)[r % 4] * np.where(r % D < D // 2, f(-1), f(1))[:, None]], 1)
    return {k: np.ascontiguousarray(v) for k, v in d.items()}


def kernel(**inputs):
    import concourse.bacc as bacc
    from concourse.bass_utils import run_bass_kernel_spmd

    nc = bacc.Bacc("TRN2", target_bir_lowering=False, num_devices=1)
    arrays = laid_out(inputs)
    d = {n: nc.dram_tensor("in_" + n, v.shape, mybir.dt.from_np(v.dtype), kind="ExternalInput").ap() for n, v in arrays.items()}
    out = nc.dram_tensor("out", (B * S, E), F32, kind="ExternalOutput").ap()
    build(nc, d, out)
    r = run_bass_kernel_spmd(nc, [{"in_" + n: v for n, v in arrays.items()}], core_ids=[0])
    return np.asarray(r.results[0]["out"]).reshape(B, S, E)
```
